# Optimizing a Trainium2 kernel written in Bass

```python
import numpy as np
import jax
import jax.numpy as jnp

def _softmax(x, axis=-1):
    return jax.nn.softmax(x, axis=axis)

def _gelu(x):
    return jax.nn.gelu(x, approximate=True)

def _silu(x):
    return jax.nn.silu(x)

def _sigmoid(x):
    return jax.nn.sigmoid(x)

def _layernorm(x, axis=-1, eps=1e-05):
    m = jnp.mean(x, axis=axis, keepdims=True)
    v = jnp.var(x, axis=axis, keepdims=True)
    return (x - m) / jnp.sqrt(v + eps)

def _scatter_add(tgt, idx, src, axis=0):
    return tgt.at[idx].add(src)

def _segment_sum(src, seg, n):
    return jax.ops.segment_sum(src, seg, n)
kernel_name = 'mk_xattn_ffn_d4_seqx_r8_19421d'

def setup_inputs(seed: int=0):
    np.random.seed(seed)
    _w = jnp.asarray

    def _rec_inputs():
        import jax
        import jax.numpy as jnp
        _rk = jax.random.key(seed)
        x = 7.22e-05 + 1 * jax.random.normal(jax.random.fold_in(_rk, 1), (64, 128, 128), jnp.float32)
        _lenS = 128 - jax.random.randint(jax.random.fold_in(_rk, 7), (64,), 0, max(1, 128 // 4) + 1, jnp.int32)
        _lenS2 = 77 - jax.random.randint(jax.random.fold_in(_rk, 8), (64,), 0, max(1, 77 // 4) + 1, jnp.int32)
        _ctx_768P = jax.random.normal(jax.random.fold_in(_rk, 11), (64, 16, 96), jnp.float32)
        _ctx_768c = jax.random.dirichlet(jax.random.fold_in(_rk, 511), 0.3 * jnp.ones((16,), jnp.float32), (64, 77))
        _ctx_768t = jnp.einsum('bsk,bkd->bsd', _ctx_768c, _ctx_768P)
        _ctx_768t = _ctx_768t * jax.lax.rsqrt(jnp.mean(jnp.square(_ctx_768t)) + 1e-12) * 0.953939
        ctx_768 = -0.000191848 + 0.999787 * (_ctx_768t + 0.3 * jax.random.normal(jax.random.fold_in(_rk, 611), (64, 77, 96), jnp.float32))
        _validS = jnp.arange(128)[None, :] < _lenS[:, None]
        _validS2 = jnp.arange(77)[None, :] < _lenS2[:, None]
        _causal = jnp.tril(jnp.ones((128, 128), dtype=bool))
        mask_1x1xSxS2_bk0 = jnp.logical_not(jnp.broadcast_to(_validS2[0:1, None, None, :], (1, 1, 128, 77)))
        return (x, ctx_768, mask_1x1xSxS2_bk0)
    x, ctx_768, mask_1x1xSxS2_bk0 = _rec_inputs()

    def _L0_xattn_setup():
        import jax, jax.numpy as jnp
        import numpy as np
        B, T, Q_DIM, KV_DIM = (4, 256, 128, 96)
        HEADS, DIM_HEAD = (16, 64)
        INNER = HEADS * DIM_HEAD
        NUM_FRAMES, NUM_PATCHES = (8, 32)
        LN_EPS = 1e-05

        def diagonal_frame_mask(num_patches, num_frames):
            fid = np.repeat(np.arange(num_frames), num_patches)
            m = fid[:, None] == fid[None, :]
            return jnp.asarray(m[None, None])
        key = jax.random.key(seed)
        ks = jax.random.split(key, 6)
        s = lambda d: 1.0 / np.sqrt(d)
        return {'x': jax.random.normal(ks[0], (B, T, Q_DIM), jnp.float32), 'context': jax.random.normal(ks[1], (B, T, KV_DIM), jnp.float32), 'ln_gamma': jnp.ones((Q_DIM,), jnp.float32), 'ln_beta': jnp.zeros((Q_DIM,), jnp.float32), 'Wq': jax.random.normal(ks[2], (Q_DIM, INNER), jnp.float32) * s(Q_DIM), 'Wkv': jax.random.normal(ks[3], (KV_DIM, 2 * INNER), jnp.float32) * s(KV_DIM), 'Wo': jax.random.normal(ks[4], (INNER, Q_DIM), jnp.float32) * s(INNER), 'bo': jnp.zeros((Q_DIM,), jnp.float32), 'mask': diagonal_frame_mask(NUM_PATCHES, NUM_FRAMES)}
    _L0_xattn_all = _L0_xattn_setup()
    _L0_xattn_in = {k: v for k, v in _L0_xattn_all.items() if k in ('ln_gamma', 'ln_beta', 'Wq', 'Wkv', 'Wo', 'bo')}
    del _L0_xattn_all

    def _L0_ffn_setup():
        import jax, jax.numpy as jnp
        import numpy as np
        B, S, H, F, G = (8, 256, 128, 512, 128)
        EPS = 1e-05

        def _dequant(q, scales, g):
            K, N = q.shape
            w = (q.astype(jnp.float32) - 128.0).reshape(K // g, g, N) * scales[:, None, :]
            return w.reshape(K, N)
        key = jax.random.key(seed)
        ks = jax.random.split(key, 8)
        x = jax.random.normal(ks[0], (B, S, H), dtype=jnp.float32)
        ln_gamma = jnp.ones((H,), jnp.float32)
        ln_beta = jnp.zeros((H,), jnp.float32)
        fc1_q = jax.random.randint(ks[1], (H, F), 0, 32, dtype=jnp.int32)
        fc2_q = jax.random.randint(ks[2], (F, H), 0, 32, dtype=jnp.int32)
        fc1_scales = jax.random.uniform(ks[3], (H // G, F), jnp.float32) * 0.02 + 0.001
        fc2_scales = jax.random.uniform(ks[4], (F // G, H), jnp.float32) * 0.02 + 0.001
        fc1_bias = jax.random.normal(ks[5], (F,), jnp.float32) * 0.02
        fc2_bias = jax.random.normal(ks[6], (H,), jnp.float32) * 0.02
        return {'x': x, 'ln_gamma': ln_gamma, 'ln_beta': ln_beta, 'fc1_q': fc1_q, 'fc1_scales': fc1_scales, 'fc1_bias': fc1_bias, 'fc2_q': fc2_q, 'fc2_scales': fc2_scales, 'fc2_bias': fc2_bias}
    _L0_ffn_all = _L0_ffn_setup()
    _L0_ffn_in = {k: v for k, v in _L0_ffn_all.items() if k in ('ln_gamma', 'ln_beta', 'fc1_q', 'fc1_scales', 'fc1_bias', 'fc2_q', 'fc2_scales', 'fc2_bias')}
    del _L0_ffn_all

    def _L1_xattn_setup():
        import jax, jax.numpy as jnp
        import numpy as np
        HEADS = 8
        DIM_HEAD = 64
        SCALE = DIM_HEAD ** (-0.5)
        key = jax.random.key(seed)
        ks = jax.random.split(key, 7)
        B, Nq, Nc = (4, 256, 256)
        Dq, Dc = (128, 96)
        inner = HEADS * DIM_HEAD
        x = jax.random.normal(ks[0], (B, Nq, Dq), dtype=jnp.float32)
        context = jax.random.normal(ks[1], (B, Nc, Dc), dtype=jnp.float32)
        Wq = jax.random.normal(ks[2], (Dq, inner), dtype=jnp.float32) * Dq ** (-0.5)
        Wk = jax.random.normal(ks[3], (Dc, inner), dtype=jnp.float32) * Dc ** (-0.5)
        Wv = jax.random.normal(ks[4], (Dc, inner), dtype=jnp.float32) * Dc ** (-0.5)
        Wo = jax.random.normal(ks[5], (inner, Dq), dtype=jnp.float32) * inner ** (-0.5)
        bo = jax.random.normal(ks[6], (Dq,), dtype=jnp.float32) * 0.01
        return {'x': x, 'context': context, 'Wq': Wq, 'Wk': Wk, 'Wv': Wv, 'Wo': Wo, 'bo': bo}
    _L1_xattn_all = _L1_xattn_setup()
    _L1_xattn_in = {k: v for k, v in _L1_xattn_all.items() if k in ('Wq', 'Wk', 'Wv', 'Wo', 'bo')}
    del _L1_xattn_all

    def _L1_ffn_setup():
        import jax, jax.numpy as jnp
        import numpy as np
        QMIN, QMAX = (-128.0, 127.0)

        def _affine_quantize(x):
            amin, amax = (jnp.min(x), jnp.max(x))
            scale = jnp.maximum((amax - amin) / 255.0, 1e-08)
            zp = jnp.clip(jnp.round(-amin / scale) + QMIN, QMIN, QMAX)
            q = jnp.clip(jnp.round(x / scale) + zp, QMIN, QMAX)
            return (q, scale, zp)

        def _sym_quantize(w):
            scale = jnp.maximum(jnp.max(jnp.abs(w)) / 127.0, 1e-08)
            q = jnp.clip(jnp.round(w / scale), -127.0, 127.0)
            return (q, scale)

        def _qlinear(x, W, b):
            xq, sx, zx = _affine_quantize(x)
            wq, sw = _sym_quantize(W)
            acc = jnp.einsum('bsh,oh->bso', xq - zx, wq)
            return acc * (sx * sw) + b
        key = jax.random.key(seed)
        k1, k2, k3, k4, k5 = jax.random.split(key, 5)
        d, h = (128, 512)
        x = jax.random.normal(k1, (4, 512, d), dtype=jnp.float32)
        W1 = jax.random.normal(k2, (h, d), dtype=jnp.float32) * (1.0 / np.sqrt(d))
        b1 = jax.random.normal(k3, (h,), dtype=jnp.float32) * 0.02
        W2 = jax.random.normal(k4, (d, h), dtype=jnp.float32) * (1.0 / np.sqrt(h))
        b2 = jax.random.normal(k5, (d,), dtype=jnp.float32) * 0.02
        return {'x': x, 'W1': W1, 'b1': b1, 'W2': W2, 'b2': b2}
    _L1_ffn_all = _L1_ffn_setup()
    _L1_ffn_in = {k: v for k, v in _L1_ffn_all.items() if k in ('W1', 'b1', 'W2', 'b2')}
    del _L1_ffn_all

    def _L2_xattn_setup():
        import jax, jax.numpy as jnp
        import numpy as np
        HEADS = 16
        DIM_HEAD = 64
        key = jax.random.key(seed)
        ks = jax.random.split(key, 7)
        b, n, m = (2, 256, 128)
        query_dim, context_dim = (128, 96)
        inner = HEADS * DIM_HEAD
        s_q = 1.0 / np.sqrt(query_dim)
        s_c = 1.0 / np.sqrt(context_dim)
        s_i = 1.0 / np.sqrt(inner)
        return {'x': jax.random.normal(ks[0], (b, n, query_dim), jnp.float32), 'context': jax.random.normal(ks[1], (b, m, context_dim), jnp.float32), 'Wq': jax.random.normal(ks[2], (query_dim, inner), jnp.float32) * s_q, 'Wk': jax.random.normal(ks[3], (context_dim, inner), jnp.float32) * s_c, 'Wv': jax.random.normal(ks[4], (context_dim, inner), jnp.float32) * s_c, 'Wo': jax.random.normal(ks[5], (inner, query_dim), jnp.float32) * s_i, 'bo': jax.random.normal(ks[6], (query_dim,), jnp.float32) * 0.01}
    _L2_xattn_all = _L2_xattn_setup()
    _L2_xattn_in = {k: v for k, v in _L2_xattn_all.items() if k in ('Wq', 'Wk', 'Wv', 'Wo', 'bo')}
    del _L2_xattn_all

    def _L2_ffn_setup():
        import jax, jax.numpy as jnp
        import numpy as np
        B, S, D, E, H, K = (4, 256, 128, 8, 64, 2)
        key = jax.random.key(seed)
        ks = jax.random.split(key, 11)
        sc = 0.02
        return {'x': jax.random.normal(ks[0], (B, S, D), dtype=jnp.float32), 'gate_W': jax.random.normal(ks[1], (D, E), dtype=jnp.float32) * sc, 'W1': jax.random.normal(ks[2], (E, D, H), dtype=jnp.float32) * sc, 'b1': jnp.zeros((E, H), dtype=jnp.float32), 'W2': jax.random.normal(ks[3], (E, H, D), dtype=jnp.float32) * sc, 'b2': jnp.zeros((E, D), dtype=jnp.float32), 'Ws1': jax.random.normal(ks[4], (D, H), dtype=jnp.float32) * sc, 'bs1': jnp.zeros((H,), dtype=jnp.float32), 'Ws2': jax.random.normal(ks[5], (H, D), dtype=jnp.float32) * sc, 'bs2': jnp.zeros((D,), dtype=jnp.float32), 'route_scale': jnp.ones((), dtype=jnp.float32)}
    _L2_ffn_all = _L2_ffn_setup()
    _L2_ffn_in = {k: v for k, v in _L2_ffn_all.items() if k in ('gate_W', 'W1', 'b1', 'W2', 'b2', 'Ws1', 'bs1', 'Ws2', 'bs2', 'route_scale')}
    del _L2_ffn_all

    def _L3_xattn_setup():
        import jax, jax.numpy as jnp
        import numpy as np
        B, LQ, LK = (4, 256, 256)
        D1, D2, H = (128, 96, 128)
        key = jax.random.key(seed)
        ks = jax.random.split(key, 9)
        s1, s2, sh = (1.0 / np.sqrt(D1), 1.0 / np.sqrt(D2), 1.0 / np.sqrt(H))
        return {'query': jax.random.normal(ks[0], (B, LQ, D1), jnp.float32), 'key': jax.random.normal(ks[1], (B, LK, D2), jnp.float32), 'value': jax.random.normal(ks[2], (B, LK, D2), jnp.float32), 'Wq': jax.random.normal(ks[3], (D1, H), jnp.float32) * s1, 'bq': jax.random.normal(ks[4], (H,), jnp.float32) * s1, 'Wk': jax.random.normal(ks[5], (D2, H), jnp.float32) * s2, 'bk': jax.random.normal(ks[6], (H,), jnp.float32) * s2, 'Wv': jax.random.normal(ks[7], (D2, H), jnp.float32) * s2, 'bv': jax.random.normal(ks[8], (H,), jnp.float32) * s2}
    _L3_xattn_all = _L3_xattn_setup()
    _L3_xattn_in = {k: v for k, v in _L3_xattn_all.items() if k in ('Wq', 'bq', 'Wk', 'bk', 'Wv', 'bv')}
    del _L3_xattn_all

    def _L3_ffn_setup():
        import jax, jax.numpy as jnp
        import numpy as np
        B, S, D, F, E, TOP_K = (4, 256, 128, 512, 8, 2)
        LN_EPS = 1e-05
        key = jax.random.key(seed)
        ks = jax.random.split(key, 4)
        sc = lambda fan_in: 1.0 / np.sqrt(fan_in)
        return {'x': jax.random.normal(ks[0], (B, S, D), jnp.float32), 'W1': jax.random.normal(ks[1], (E, D, F), jnp.float32) * sc(D), 'b1': jnp.zeros((E, F), jnp.float32), 'W2': jax.random.normal(ks[2], (E, F, D), jnp.float32) * sc(F), 'b2': jnp.zeros((E, D), jnp.float32), 'Wr': jax.random.normal(ks[3], (D, E), jnp.float32) * sc(D), 'br': jnp.zeros((E,), jnp.float32), 'gamma': jnp.ones((D,), jnp.float32), 'beta': jnp.zeros((D,), jnp.float32)}
    _L3_ffn_all = _L3_ffn_setup()
    _L3_ffn_in = {k: v for k, v in _L3_ffn_all.items() if k in ('W1', 'b1', 'W2', 'b2', 'Wr', 'br', 'gamma', 'beta')}
    del _L3_ffn_all
    return {'x': x, 'ctx_768': ctx_768, 'mask_1x1xSxS2_bk0': mask_1x1xSxS2_bk0, 'L0_xattn_ln_gamma': _L0_xattn_in['ln_gamma'], 'L0_xattn_ln_beta': _L0_xattn_in['ln_beta'], 'L0_xattn_Wq': _L0_xattn_in['Wq'], 'L0_xattn_Wkv': _L0_xattn_in['Wkv'], 'L0_xattn_Wo': _L0_xattn_in['Wo'], 'L0_xattn_bo': _L0_xattn_in['bo'], 'L0_ffn_ln_gamma': _L0_ffn_in['ln_gamma'], 'L0_ffn_ln_beta': _L0_ffn_in['ln_beta'], 'L0_ffn_fc1_q': _L0_ffn_in['fc1_q'], 'L0_ffn_fc1_scales': _L0_ffn_in['fc1_scales'], 'L0_ffn_fc1_bias': _L0_ffn_in['fc1_bias'], 'L0_ffn_fc2_q': _L0_ffn_in['fc2_q'], 'L0_ffn_fc2_scales': _L0_ffn_in['fc2_scales'], 'L0_ffn_fc2_bias': _L0_ffn_in['fc2_bias'], 'L1_xattn_Wq': _L1_xattn_in['Wq'], 'L1_xattn_Wk': _L1_xattn_in['Wk'], 'L1_xattn_Wv': _L1_xattn_in['Wv'], 'L1_xattn_Wo': _L1_xattn_in['Wo'], 'L1_xattn_bo': _L1_xattn_in['bo'], 'L1_ffn_W1': _L1_ffn_in['W1'], 'L1_ffn_b1': _L1_ffn_in['b1'], 'L1_ffn_W2': _L1_ffn_in['W2'], 'L1_ffn_b2': _L1_ffn_in['b2'], 'L2_xattn_Wq': _L2_xattn_in['Wq'], 'L2_xattn_Wk': _L2_xattn_in['Wk'], 'L2_xattn_Wv': _L2_xattn_in['Wv'], 'L2_xattn_Wo': _L2_xattn_in['Wo'], 'L2_xattn_bo': _L2_xattn_in['bo'], 'L2_ffn_gate_W': _L2_ffn_in['gate_W'], 'L2_ffn_W1': _L2_ffn_in['W1'], 'L2_ffn_b1': _L2_ffn_in['b1'], 'L2_ffn_W2': _L2_ffn_in['W2'], 'L2_ffn_b2': _L2_ffn_in['b2'], 'L2_ffn_Ws1': _L2_ffn_in['Ws1'], 'L2_ffn_bs1': _L2_ffn_in['bs1'], 'L2_ffn_Ws2': _L2_ffn_in['Ws2'], 'L2_ffn_bs2': _L2_ffn_in['bs2'], 'L2_ffn_route_scale': _L2_ffn_in['route_scale'], 'L3_xattn_Wq': _L3_xattn_in['Wq'], 'L3_xattn_bq': _L3_xattn_in['bq'], 'L3_xattn_Wk': _L3_xattn_in['Wk'], 'L3_xattn_bk': _L3_xattn_in['bk'], 'L3_xattn_Wv': _L3_xattn_in['Wv'], 'L3_xattn_bv': _L3_xattn_in['bv'], 'L3_ffn_W1': _L3_ffn_in['W1'], 'L3_ffn_b1': _L3_ffn_in['b1'], 'L3_ffn_W2': _L3_ffn_in['W2'], 'L3_ffn_b2': _L3_ffn_in['b2'], 'L3_ffn_Wr': _L3_ffn_in['Wr'], 'L3_ffn_br': _L3_ffn_in['br'], 'L3_ffn_gamma': _L3_ffn_in['gamma'], 'L3_ffn_beta': _L3_ffn_in['beta']}

def reference(x, ctx_768, mask_1x1xSxS2_bk0, L0_xattn_ln_gamma, L0_xattn_ln_beta, L0_xattn_Wq, L0_xattn_Wkv, L0_xattn_Wo, L0_xattn_bo, L0_ffn_ln_gamma, L0_ffn_ln_beta, L0_ffn_fc1_q, L0_ffn_fc1_scales, L0_ffn_fc1_bias, L0_ffn_fc2_q, L0_ffn_fc2_scales, L0_ffn_fc2_bias, L1_xattn_Wq, L1_xattn_Wk, L1_xattn_Wv, L1_xattn_Wo, L1_xattn_bo, L1_ffn_W1, L1_ffn_b1, L1_ffn_W2, L1_ffn_b2, L2_xattn_Wq, L2_xattn_Wk, L2_xattn_Wv, L2_xattn_Wo, L2_xattn_bo, L2_ffn_gate_W, L2_ffn_W1, L2_ffn_b1, L2_ffn_W2, L2_ffn_b2, L2_ffn_Ws1, L2_ffn_bs1, L2_ffn_Ws2, L2_ffn_bs2, L2_ffn_route_scale, L3_xattn_Wq, L3_xattn_bq, L3_xattn_Wk, L3_xattn_bk, L3_xattn_Wv, L3_xattn_bv, L3_ffn_W1, L3_ffn_b1, L3_ffn_W2, L3_ffn_b2, L3_ffn_Wr, L3_ffn_br, L3_ffn_gamma, L3_ffn_beta):
    import jax
    import jax.numpy as jnp

    def _L0_xattn_ref(x, context, ln_gamma, ln_beta, Wq, Wkv, Wo, bo, mask):
        import jax, jax.numpy as jnp
        import numpy as np
        B, T, Q_DIM, KV_DIM = (4, 256, 128, 96)
        HEADS, DIM_HEAD = (16, 64)
        INNER = HEADS * DIM_HEAD
        NUM_FRAMES, NUM_PATCHES = (8, 32)
        LN_EPS = 1e-05

        def diagonal_frame_mask(num_patches, num_frames):
            fid = np.repeat(np.arange(num_frames), num_patches)
            m = fid[:, None] == fid[None, :]
            return jnp.asarray(m[None, None])
        mu = jnp.mean(x, axis=-1, keepdims=True)
        var = jnp.mean(jnp.square(x - mu), axis=-1, keepdims=True)
        xn = (x - mu) * jax.lax.rsqrt(var + LN_EPS) * ln_gamma + ln_beta
        scale = DIM_HEAD ** (-0.5)
        q = xn @ Wq
        kv = context @ Wkv
        k, v = jnp.split(kv, 2, axis=-1)
        split_heads = lambda t: t.reshape(t.shape[0], t.shape[1], HEADS, DIM_HEAD).transpose(0, 2, 1, 3)
        q, k, v = (split_heads(q), split_heads(k), split_heads(v))
        dots = jnp.einsum('bhnd,bhmd->bhnm', q, k) * scale
        dots = jnp.where(mask, dots, -jnp.inf)
        attn = jax.nn.softmax(dots, axis=-1)
        out = jnp.einsum('bhnm,bhmd->bhnd', attn, v)
        out = out.transpose(0, 2, 1, 3).reshape(x.shape[0], x.shape[1], INNER)
        return out @ Wo + bo

    def _L0_ffn_ref(x, ln_gamma, ln_beta, fc1_q, fc1_scales, fc1_bias, fc2_q, fc2_scales, fc2_bias):
        import jax, jax.numpy as jnp
        import numpy as np
        B, S, H, F, G = (8, 256, 128, 512, 128)
        EPS = 1e-05

        def _dequant(q, scales, g):
            K, N = q.shape
            w = (q.astype(jnp.float32) - 128.0).reshape(K // g, g, N) * scales[:, None, :]
            return w.reshape(K, N)
        residual = x
        mu = jnp.mean(x, axis=-1, keepdims=True)
        var = jnp.mean(jnp.square(x - mu), axis=-1, keepdims=True)
        h = (x - mu) * jax.lax.rsqrt(var + EPS) * ln_gamma + ln_beta
        hf = h.reshape(-1, H)
        w1 = _dequant(fc1_q, fc1_scales, G)
        y = hf @ w1 + fc1_bias
        y = jax.nn.silu(y)
        w2 = _dequant(fc2_q, fc2_scales, G)
        z = y @ w2 + fc2_bias
        return residual + 0.5 * z.reshape(residual.shape)

    def _L1_xattn_ref(x, context, Wq, Wk, Wv, Wo, bo):
        import jax, jax.numpy as jnp
        import numpy as np
        HEADS = 8
        DIM_HEAD = 64
        SCALE = DIM_HEAD ** (-0.5)
        B, Nq, _ = x.shape
        q = (x @ Wq).reshape(B, Nq, HEADS, DIM_HEAD)
        k = (context @ Wk).reshape(B, context.shape[1], HEADS, DIM_HEAD)
        v = (context @ Wv).reshape(B, context.shape[1], HEADS, DIM_HEAD)
        sim = jnp.einsum('bihd,bjhd->bhij', q, k) * SCALE
        attn = jax.nn.softmax(sim, axis=-1)
        out = jnp.einsum('bhij,bjhd->bihd', attn, v)
        out = out.reshape(B, Nq, HEADS * DIM_HEAD)
        return out @ Wo + bo

    def _L1_ffn_ref(x, W1, b1, W2, b2):
        import jax, jax.numpy as jnp
        import numpy as np
        QMIN, QMAX = (-128.0, 127.0)

        def _affine_quantize(x):
            amin, amax = (jnp.min(x), jnp.max(x))
            scale = jnp.maximum((amax - amin) / 255.0, 1e-08)
            zp = jnp.clip(jnp.round(-amin / scale) + QMIN, QMIN, QMAX)
            q = jnp.clip(jnp.round(x / scale) + zp, QMIN, QMAX)
            return (q, scale, zp)

        def _sym_quantize(w):
            scale = jnp.maximum(jnp.max(jnp.abs(w)) / 127.0, 1e-08)
            q = jnp.clip(jnp.round(w / scale), -127.0, 127.0)
            return (q, scale)

        def _qlinear(x, W, b):
            xq, sx, zx = _affine_quantize(x)
            wq, sw = _sym_quantize(W)
            acc = jnp.einsum('bsh,oh->bso', xq - zx, wq)
            return acc * (sx * sw) + b
        h = _qlinear(x, W1, b1)
        h = jax.nn.gelu(h, approximate=False)
        out = _qlinear(h, W2, b2)
        return out

    def _L2_xattn_ref(x, context, Wq, Wk, Wv, Wo, bo):
        import jax, jax.numpy as jnp
        import numpy as np
        HEADS = 16
        DIM_HEAD = 64
        b, n, _ = x.shape
        h, d = (HEADS, DIM_HEAD)
        scale = d ** (-0.5)
        q = (x @ Wq).reshape(b, n, h, d).transpose(0, 2, 1, 3)
        k = (context @ Wk).reshape(b, -1, h, d).transpose(0, 2, 1, 3)
        v = (context @ Wv).reshape(b, -1, h, d).transpose(0, 2, 1, 3)
        sim = jnp.einsum('bhid,bhjd->bhij', q, k) * scale
        attn = jax.nn.softmax(sim, axis=-1)
        out = jnp.einsum('bhij,bhjd->bhid', attn, v)
        out = out.transpose(0, 2, 1, 3).reshape(b, n, h * d)
        return out @ Wo + bo

    def _L2_ffn_ref(x, gate_W, W1, b1, W2, b2, Ws1, bs1, Ws2, bs2, route_scale):
        import jax, jax.numpy as jnp
        import numpy as np
        B, S, D, E, H, K = (4, 256, 128, 8, 64, 2)
        scores = jax.nn.sigmoid(x @ gate_W) * route_scale
        topk_scores, topk_idx = jax.lax.top_k(scores, K)
        topk_w = topk_scores / topk_scores.sum(-1, keepdims=True)
        onehot = jax.nn.one_hot(topk_idx, E, dtype=x.dtype)
        gate_full = jnp.einsum('bsk,bske->bse', topk_w, onehot)
        h = jax.nn.gelu(jnp.einsum('bsd,edh->bseh', x, W1) + b1, approximate=False)
        y = jnp.einsum('bseh,ehd->bsed', h, W2) + b2
        expert_out = jnp.einsum('bse,bsed->bsd', gate_full, y)
        shared = jax.nn.gelu(x @ Ws1 + bs1, approximate=False) @ Ws2 + bs2
        return expert_out + shared

    def _L3_xattn_ref(query, key, value, Wq, bq, Wk, bk, Wv, bv):
        import jax, jax.numpy as jnp
        import numpy as np
        B, LQ, LK = (4, 256, 256)
        D1, D2, H = (128, 96, 128)
        q = jnp.einsum('bqd,dh->bqh', query, Wq) + bq
        k = jnp.einsum('bkd,dh->bkh', key, Wk) + bk
        v = jnp.einsum('bkd,dh->bkh', value, Wv) + bv
        scores = jnp.einsum('bqh,bkh->bqk', q, k)
        weights = jax.nn.softmax(scores, axis=-1)
        return jnp.einsum('bqk,bkh->bqh', weights, v)

    def _L3_ffn_ref(x, W1, b1, W2, b2, Wr, br, gamma, beta):
        import jax, jax.numpy as jnp
        import numpy as np
        B, S, D, F, E, TOP_K = (4, 256, 128, 512, 8, 2)
        LN_EPS = 1e-05
        b, s, d = x.shape
        e = Wr.shape[1]
        rw = jax.nn.softmax(x.mean(axis=1) @ Wr + br, axis=-1)
        x_flat = x.reshape(-1, d)
        rw_tok = jnp.repeat(rw, s, axis=0)
        tk_w, tk_i = jax.lax.top_k(rw_tok, TOP_K)
        tk_w = jax.nn.softmax(tk_w, axis=-1)
        h = jax.nn.gelu(jnp.einsum('nd,edf->enf', x_flat, W1) + b1[:, None, :], approximate=False)
        expert_out = jnp.einsum('enf,efd->end', h, W2) + b2[:, None, :]
        onehot = jax.nn.one_hot(tk_i, e, dtype=x.dtype)
        cw = jnp.einsum('nk,nke->ne', tk_w, onehot)
        out = jnp.einsum('ne,end->nd', cw, expert_out).reshape(b, s, d)
        y = out + x
        mu = y.mean(axis=-1, keepdims=True)
        var = y.var(axis=-1, keepdims=True)
        return (y - mu) / jnp.sqrt(var + LN_EPS) * gamma + beta
    x = x + _L0_xattn_ref(_layernorm(x, axis=-1), ctx_768, L0_xattn_ln_gamma, L0_xattn_ln_beta, L0_xattn_Wq, L0_xattn_Wkv, L0_xattn_Wo, L0_xattn_bo, mask_1x1xSxS2_bk0)
    x = x + _L0_ffn_ref(_layernorm(x, axis=-1), L0_ffn_ln_gamma, L0_ffn_ln_beta, L0_ffn_fc1_q, L0_ffn_fc1_scales, L0_ffn_fc1_bias, L0_ffn_fc2_q, L0_ffn_fc2_scales, L0_ffn_fc2_bias)
    x = x + _L1_xattn_ref(_layernorm(x, axis=-1), ctx_768, L1_xattn_Wq, L1_xattn_Wk, L1_xattn_Wv, L1_xattn_Wo, L1_xattn_bo)
    x = x + _L1_ffn_ref(_layernorm(x, axis=-1), L1_ffn_W1, L1_ffn_b1, L1_ffn_W2, L1_ffn_b2)
    x = x + _L2_xattn_ref(_layernorm(x, axis=-1), ctx_768, L2_xattn_Wq, L2_xattn_Wk, L2_xattn_Wv, L2_xattn_Wo, L2_xattn_bo)
    x = x + _L2_ffn_ref(_layernorm(x, axis=-1), L2_ffn_gate_W, L2_ffn_W1, L2_ffn_b1, L2_ffn_W2, L2_ffn_b2, L2_ffn_Ws1, L2_ffn_bs1, L2_ffn_Ws2, L2_ffn_bs2, L2_ffn_route_scale)
    x = x + _L3_xattn_ref(_layernorm(x, axis=-1), ctx_768, ctx_768, L3_xattn_Wq, L3_xattn_bq, L3_xattn_Wk, L3_xattn_bk, L3_xattn_Wv, L3_xattn_bv)
    x = x + _L3_ffn_ref(_layernorm(x, axis=-1), L3_ffn_W1, L3_ffn_b1, L3_ffn_W2, L3_ffn_b2, L3_ffn_Wr, L3_ffn_br, L3_ffn_gamma, L3_ffn_beta)
    return x

_drawn_inputs = setup_inputs


def setup_inputs(seed=0):
    import zlib

    import numpy as np

    out = dict(_drawn_inputs(seed))
    spreads = {'L0_xattn_ln_gamma': (1.0, 0.2),
     'L0_xattn_ln_beta': (0.0, 0.1),
     'L0_xattn_bo': (0.0, 0.308),
     'L0_ffn_ln_gamma': (1.0, 0.2),
     'L0_ffn_ln_beta': (0.0, 0.1),
     'L2_ffn_b1': (0.0, 2.0),
     'L2_ffn_b2': (0.0, 2.0),
     'L2_ffn_bs1': (0.0, 2.0),
     'L2_ffn_bs2': (0.0, 2.0),
     'L3_ffn_b1': (0.0, 2.0),
     'L3_ffn_b2': (0.0, 2.0),
     'L3_ffn_br': (0.0, 2.0),
     'L3_ffn_gamma': (1.0, 0.6),
     'L3_ffn_beta': (0.0, 2.0)}
    factors = {'L0_ffn_fc1_scales': 3.425,
     'L0_ffn_fc1_bias': 43.191,
     'L0_ffn_fc2_bias': 48.458,
     'L1_xattn_Wq': 8.0,
     'L1_xattn_Wk': 8.0,
     'L1_xattn_Wv': 8.0,
     'L1_xattn_Wo': 8.0,
     'L1_xattn_bo': 200.0,
     'L1_ffn_W1': 8.0,
     'L1_ffn_b1': 64.0,
     'L1_ffn_W2': 8.0,
     'L1_ffn_b2': 200.0,
     'L2_xattn_Wq': 8.0,
     'L2_xattn_Wk': 8.0,
     'L2_xattn_Wv': 8.0,
     'L2_xattn_Wo': 8.0,
     'L2_xattn_bo': 200.0,
     'L2_ffn_gate_W': 64.0,
     'L2_ffn_W1': 64.0,
     'L2_ffn_W2': 64.0,
     'L2_ffn_Ws1': 64.0,
     'L2_ffn_Ws2': 64.0,
     'L3_xattn_Wq': 64.0,
     'L3_xattn_bq': 200.0,
     'L3_xattn_Wk': 64.0,
     'L3_xattn_bk': 200.0,
     'L3_xattn_Wv': 64.0,
     'L3_xattn_bv': 200.0,
     'L3_ffn_W1': 200.0,
     'L3_ffn_W2': 200.0,
     'L3_ffn_Wr': 200.0}
    for name, (base, spread) in spreads.items():
        noise = np.random.default_rng([zlib.crc32(name.encode()), seed]).standard_normal(out[name].shape)
        drawn = base * np.exp(spread * noise) if base else spread * noise
        out[name] = jnp.asarray(drawn.astype(out[name].dtype))
    for name, factor in factors.items():
        out[name] = (out[name] * factor).astype(out[name].dtype)
    return out
```

```python
from contextlib import ExitStack

import numpy as np

import concourse.bass as bass
import concourse.mybir as mybir

F32 = mybir.dt.float32
F32R = mybir.dt.float32r
BF16 = mybir.dt.bfloat16
ALU = mybir.AluOpType
ACT = mybir.ActivationFunctionType
AX = mybir.AxisListType
ds = bass.ds

P = 128
BATCH = 64
KEYS = 77
CDIM = 96
HEAD = 64
GT = 4
GROUPS = BATCH // GT
GCOLS = GT * KEYS
EPS = 1e-5
MAGIC = 1.5 * 2.0 ** 23
BANK = 512


class Counter:

    def __init__(self, sem, credit=0):
        self.sem, self.credit, self.base = sem, credit, credit

    def claim(self, total):
        c = Claim(self.sem, self.base, self.credit, total)
        self.base += total
        return c


class Claim:
    def __init__(self, sem, base, credit, total):
        self.sem, self.base, self.credit, self.total = sem, base, credit, total

    def at(self, n):
        return n + self.base

    def free(self, n):
        return n + 1 + (self.base - self.credit)


def for_groups(eng, body):
    with eng.Fori(0, GROUPS // 2 - 1) as i:
        body(2 * i, 0, 2)
        body(2 * i + 1, 1, 2)
    body(GROUPS - 2, 0, 1)
    body(GROUPS - 1, 1, 0)


def three_passes(eng, out, lhs, rhs, start=True, stop=True):
    eng.matmul(out, lhs[0], rhs[0], start=start, stop=False)
    eng.matmul(out, lhs[0], rhs[1], start=False, stop=False)
    return eng.matmul(out, lhs[1], rhs[0], start=False, stop=stop)


def bc(ap, n):
    return ap.unsqueeze(2).broadcast_to([ap.shape[0], ap.shape[1], n])


class Core:

    def __init__(self, nc, ctx, ins, out):
        self.nc, self.ctx, self.ins, self.out = nc, ctx, ins, out
        self.x = self.sb(ctx, "x", [P, BATCH, P], F32)
        self.ident = self.sb(ctx, "ident", [P, P], F32)
        self.ident_bf = self.sb(ctx, "ident_bf", [P, P], BF16)
        self.neg_half = self.sb(ctx, "neg_half", [P, GT], F32)
        self.eps = self.sb(ctx, "eps", [P, GT], F32)
        self.stats = self.sb(ctx, "ln_stats", [P, GT, 6], F32)
        self.mean_var = self.sb(ctx, "ln_mean_var", [P, GT, 2], F32)
        self.ln_var = self.sb(ctx, "ln_var", [P, GT], F32)
        self.rstd = self.sb(ctx, "ln_rstd", [P, GT], F32)
        self.rstd2 = self.sb(ctx, "ln_rstd2", [P, GT], F32)
        self.z = self.sb(ctx, "z", [P, GT, P], F32)
        self.ps_s = ctx.enter_context(nc.psum_tensor("ps_s", [P, 3, BANK], F32))
        self.ps_p = ctx.enter_context(nc.psum_tensor("ps_p", [P, 2, BANK], F32))
        self.ps_t = ctx.enter_context(nc.psum_tensor("ps_t", [P, 2, BANK], F32))
        self.ps_o = ctx.enter_context(nc.psum_tensor("ps_o", [P, BANK], F32))
        self.counters = {}
        self.credits = []

    def sb(self, ctx, name, shape, dt):
        return ctx.enter_context(self.nc.sbuf_tensor(name, shape, dt))

    def bank(self, n):
        if n < 3:
            return self.ps_s[:, n, :]
        if n < 5:
            return self.ps_p[:, n - 3, :]
        return self.ps_t[:, n - 5, :] if n < 7 else self.ps_o[:, :]

    def claim(self, name, total, credit=0, owner=None):
        if name not in self.counters:
            sem = self.ctx.enter_context(self.nc.semaphore(name))
            self.counters[name] = Counter(sem, credit)
            if credit:
                self.credits.append((owner, sem, credit))
        return self.counters[name].claim(total)

    def grant(self, owner, eng):
        for who, sem, credit in self.credits:
            if who == owner:
                eng.sem_inc(sem, credit)


class Chain:

    def __init__(self, claim):
        self.claim, self.n = claim, 0

    def step(self, eng, ins):
        ins.then_inc(self.claim.sem, 1)
        self.n += 1
        eng.wait_ge(self.claim.sem, self.claim.at(self.n))


class LayerNorm:

    def __init__(self, core, twice=False, bias=None, dest=None, once=None):
        self.dest = dest or (lambda g, k: core.z[:, k, :])
        self.core, self.twice, self.bias = core, twice, bias
        self.stats_ready = core.claim("stats_ready", GT * GROUPS)
        self.stats_seen = core.claim("stats_seen", GROUPS)
        self.aggr_ready = core.claim("aggr_ready", GT * GROUPS)
        self.once = once
        self.pool_steps = 2 if not twice else 7 if once is None else 6
        if once is not None:
            self.once_ready = core.claim("once_ready", GT * GROUPS)
            self.once_added = core.claim("once_added", GROUPS)
            self.pool_seen = core.claim("pool_seen", GROUPS)
        self.rstd_step = core.claim("rstd_step", self.pool_steps * GROUPS)
        self.z_ready = core.claim("z_ready", GT * GROUPS)
        self.bias_added = core.claim("bias_added", GROUPS) if bias is not None else None

    def vector_stats(self, eng, g):
        c = self.core
        for k in range(GT):
            eng.bn_stats(c.stats[:, k, :], c.x[:, ds(GT * g + k, 1), :].rearrange("p a d -> p (a d)"))\
               .then_inc(self.stats_ready.sem, 1)
        eng.wait_ge(self.stats_ready.sem, self.stats_ready.at(GT * g + GT))
        eng.sem_inc(self.stats_seen.sem, 1)
        for k in range(GT):
            eng.bn_aggr(c.mean_var[:, k, :], c.stats[:, k, :]).then_inc(self.aggr_ready.sem, 1)

    def pool(self, eng, g):
        c, n = self.core, 0

        def step(ins):
            nonlocal n
            ins.then_inc(self.rstd_step.sem, 1)
            n += 1
            eng.wait_ge(self.rstd_step.sem, self.rstd_step.at(self.pool_steps * g + n))

        eng.wait_ge(self.aggr_ready.sem, self.aggr_ready.at(GT * g + GT))
        step(eng.tensor_tensor(c.ln_var[:, :], c.mean_var[:, :, 1], c.eps[:, :], ALU.add))
        step(eng.tensor_tensor(c.rstd[:, :], c.ln_var[:, :], c.neg_half[:, :], ALU.pow))
        if self.twice:
            step(eng.tensor_tensor(c.ln_var[:, :], c.mean_var[:, :, 1], c.rstd[:, :], ALU.mult))
            step(eng.tensor_tensor(c.ln_var[:, :], c.ln_var[:, :], c.rstd[:, :], ALU.mult))
            step(eng.tensor_tensor(c.ln_var[:, :], c.ln_var[:, :], c.eps[:, :], ALU.add))
            step(eng.tensor_tensor(c.rstd2[:, :], c.ln_var[:, :], c.neg_half[:, :], ALU.pow))
            if self.once is None:
                step(eng.tensor_tensor(c.rstd[:, :], c.rstd[:, :], c.rstd2[:, :], ALU.mult))

    def pool_bias(self, eng, g):
        if self.bias is None:
            return
        c = self.core
        eng.wait_ge(self.z_ready.sem, self.z_ready.at(GT * g + GT))
        xg = c.x[:, ds(GT * g, GT), :]
        if self.once is not None:
            eng.tensor_tensor(xg, xg, self.once[:, :, :], ALU.add).then_inc(self.once_added.sem, 1)
            eng.wait_ge(self.once_added.sem, self.once_added.at(g + 1))
            eng.sem_inc(self.pool_seen.sem, 1)
        eng.tensor_tensor(xg, xg, self.bias[:, :].unsqueeze(1).broadcast_to([P, GT, P]), ALU.add)\
           .then_inc(self.bias_added.sem, 1)

    def vector_z(self, eng, g):
        c = self.core
        eng.wait_ge(self.rstd_step.sem, self.rstd_step.at(self.pool_steps * g + self.pool_steps))
        for k in range(GT):
            xk = c.x[:, ds(GT * g + k, 1), :].rearrange("p a d -> p (a d)")
            if self.once is None:
                eng.tensor_scalar(self.dest(g, k), xk, c.mean_var[:, k, 0:1], c.rstd[:, k:k + 1],
                                  ALU.subtract, ALU.mult).then_inc(self.z_ready.sem, 1)
                continue
            if k == 0 and not (isinstance(g, int) and g == 0):
                eng.wait_ge(self.once_added.sem, self.once_added.at(g))
            eng.tensor_scalar(self.once[:, k, :], xk, c.mean_var[:, k, 0:1], c.rstd[:, k:k + 1],
                              ALU.subtract, ALU.mult).then_inc(self.once_ready.sem, 1)
        if self.once is not None:
            for k in range(GT):
                eng.wait_ge(self.once_ready.sem, self.once_ready.at(GT * g + k + 1))
                eng.tensor_scalar(self.dest(g, k), self.once[:, k, :], c.rstd2[:, k:k + 1], None, ALU.mult)\
                   .then_inc(self.z_ready.sem, 1)


class Phase:

    def sync(self, eng):
        pass

    def gpsimd(self, eng):
        pass

    def scalar(self, eng):
        pass

    def vector(self, eng):
        pass

    def tensor(self, eng):
        pass


class Setup(Phase):

    PER = 6
    BANKS = -(-BATCH // PER)

    def __init__(self, core):
        self.core = core
        ctx = core.ctx
        self.scope = ExitStack()
        core.ct_scope = ExitStack()
        ctx.callback(core.ct_scope.close)
        core.ct_hi = core.sb(core.ct_scope, "ct_hi", [CDIM, BATCH * KEYS], F32R)
        core.ct_lo = core.sb(core.ct_scope, "ct_lo", [CDIM, BATCH * KEYS], F32R)
        self.rows = core.sb(self.scope, "ctx_rows", [KEYS, BATCH, CDIM], F32)
        self.x_loaded = core.claim("x_loaded", 16 * 8)
        self.ctx_loaded = core.claim("ctx_loaded", 16 * 4)
        self.const_ready = core.claim("const_ready", 5)
        self.ctx_turned = core.claim("turned", self.BANKS)
        self.hi_done = core.claim("split_hi", self.BANKS)
        self.lo_done = core.claim("split_lo", self.BANKS)
        self.done = core.claim("phase_done", 1)
        self.scope.close()

    def cols(self, n):
        return range(self.PER * n, min(BATCH, self.PER * n + self.PER))

    def sync(self, eng):
        c = self.core
        for q in range(4):
            b = slice(16 * q, 16 * q + 16)
            eng.dma_start(self.rows[:, b, :], c.ins["ctx_768"][b].rearrange("b k c -> k b c"))\
               .then_inc(self.ctx_loaded.sem, 16)
        for q in range(8):
            b = slice(8 * q, 8 * q + 8)
            eng.dma_start(c.x[:, b, :], c.ins["x"][b].rearrange("b t d -> t b d"))\
               .then_inc(self.x_loaded.sem, 16)

    def gpsimd(self, eng):
        c = self.core
        eng.memset(c.ident[:, :], 0.0).then_inc(self.const_ready.sem, 1)
        eng.wait_ge(self.const_ready.sem, self.const_ready.at(1))
        eng.affine_select(out=c.ident[:, :], in_=c.ident[:, :], compare_op=ALU.not_equal, fill=1.0,
                          base=0, pattern=[[-1, P]], channel_multiplier=1)\
           .then_inc(self.const_ready.sem, 1)
        eng.wait_ge(self.const_ready.sem, self.const_ready.at(2))
        eng.tensor_copy(c.ident_bf[:, :], c.ident[:, :]).then_inc(self.const_ready.sem, 1)
        eng.memset(c.neg_half[:, :], -0.5).then_inc(self.const_ready.sem, 1)
        eng.memset(c.eps[:, :], EPS).then_inc(self.const_ready.sem, 1)
        eng.wait_ge(self.const_ready.sem, self.const_ready.at(5))

    def tensor(self, eng):
        c = self.core
        eng.wait_ge(self.const_ready.sem, self.const_ready.at(3))
        for n in range(self.BANKS):
            eng.wait_ge(self.ctx_loaded.sem, self.ctx_loaded.at(16 * 4))
            if n >= 2:
                eng.wait_ge(self.lo_done.sem, self.lo_done.at(n - 1))
            for j, b in enumerate(self.cols(n)):
                mm = eng.transpose(c.ps_t[0:CDIM, n % 2, j * KEYS:(j + 1) * KEYS],
                                   self.rows[:, b, :], c.ident[0:KEYS, 0:KEYS])
            mm.then_inc(self.ctx_turned.sem, 1)

    def scalar(self, eng):
        c = self.core
        for n in range(self.BANKS):
            w = len(self.cols(n)) * KEYS
            s = slice(self.PER * n * KEYS, self.PER * n * KEYS + w)
            eng.wait_ge(self.ctx_turned.sem, self.ctx_turned.at(n + 1))
            eng.activation(c.ct_hi[:, s], c.ps_t[0:CDIM, n % 2, 0:w], ACT.Copy)\
               .then_inc(self.hi_done.sem, 1)

    def vector(self, eng):
        c = self.core
        for n in range(self.BANKS):
            w = len(self.cols(n)) * KEYS
            s = slice(self.PER * n * KEYS, self.PER * n * KEYS + w)
            eng.wait_ge(self.hi_done.sem, self.hi_done.at(n + 1))
            eng.tensor_tensor(c.ct_lo[:, s], c.ps_t[0:CDIM, n % 2, 0:w], c.ct_hi[:, s].bitcast(F32),
                              ALU.subtract).then_inc(self.lo_done.sem, 1)
        eng.wait_ge(self.x_loaded.sem, self.x_loaded.at(16 * 8))
        eng.wait_ge(self.const_ready.sem, self.const_ready.at(5))
        eng.wait_ge(self.lo_done.sem, self.lo_done.at(self.BANKS))
        eng.sem_inc(self.done.sem, 1)


class CrossAttention(Phase):

    def __init__(self, core, name, heads, wq, wk, wv, wo, bo, before, twice=False,
                 gamma=None, beta=None, mask=None):
        self.core, self.name, self.heads, self.before = core, name, heads, before
        self.src = dict(wq=wq, wk=wk, wv=wv, wo=wo, bo=bo, gamma=gamma, beta=beta, mask=mask)
        self.masked, self.affine = mask is not None, gamma is not None
        H = heads
        self.rows = H * KEYS
        self.chunks = -(-self.rows // P)
        self.uses = -(-self.chunks // GT)
        self.banks = [6, 6, 4] if H == 16 else [4, 4]
        self.NB = len(self.banks)
        self.pairs = H // 2
        self.half = H // 2
        self.cyc = 2 * GT * self.uses + 1
        sb, ctx = core.sb, ExitStack()
        self.scope = ctx
        n = lambda s: f"{name}_{s}"
        self.mt_hi = sb(ctx, n("mt_hi"), [CDIM, H, P], F32R)
        self.mt_lo = sb(ctx, n("mt_lo"), [CDIM, H, P], F32R)
        self.vo_hi = sb(ctx, n("vo_hi"), [CDIM, H, P], F32R)
        self.vo_lo = sb(ctx, n("vo_lo"), [CDIM, H, P], F32R)
        self.bias = sb(ctx, n("bias"), [P, P], F32)
        if self.affine:
            self.gb = sb(ctx, n("gamma_beta"), [P, 2], F32)
        if self.masked:
            self.mask_u8 = sb(ctx, n("mask_u8"), [P, KEYS], mybir.dt.uint8)
            self.mask_add = sb(ctx, n("mask_add"), [P, KEYS], BF16)
            self.some_key = sb(ctx, n("some_key"), [P, 2], F32)
        self.zt = sb(ctx, n("zt"), [P, 2, GT * P], F32)
        self.e = sb(ctx, n("e"), [P, 2, self.rows], F32)
        self.pt = sb(ctx, n("pt"), [P, self.chunks, P], F32)
        self.val = sb(ctx, n("val"), [P, self.chunks, P], F32)
        self.mx = sb(ctx, n("mx"), [P, H], F32)
        self.sm = sb(ctx, n("sm"), [P, H], F32)
        self.rs = sb(ctx, n("rs"), [P, H], F32)
        with ExitStack() as prep:
            self.wq = sb(prep, n("wq"), [P, H * HEAD], F32)
            self.wk = sb(prep, n("wk"), [CDIM, H * HEAD], F32)
            self.wv = sb(prep, n("wv"), [CDIM, H * HEAD], F32)
            self.wo = sb(prep, n("wo"), [P, self.pairs, P], F32)
            self.wt = sb(prep, n("wt"), [P, 2, P + 2 * CDIM], F32)
        self.keys = sb(ctx, n("keys"), [P, 2, GT, H, KEYS], F32)
        self.vals_t = sb(ctx, n("vals_t"), [P, 2, GT, H, KEYS], F32)
        ctx.close()

        T = BATCH
        cl = core.claim
        self.loads = 4 + 2 * self.affine + self.masked
        self.w_loaded = cl("w_loaded", 16 * self.loads)
        self.bias_loaded = cl("bias_loaded", 16)
        self.w_turned = cl("turned", self.pairs)
        self.wt_ready = cl("wt_ready", self.pairs)
        self.prod_done = cl("prod_done", self.pairs)
        self.hi_done = cl("split_hi", 4 * self.pairs)
        self.lo_done = cl("split_lo", 4 * self.pairs)
        self.mask_ready = cl("mask_ready", 5) if self.masked else None
        self.ln = LayerNorm(core, twice, self.bias)
        self.proj_done = cl("proj_done", 2 * H * GROUPS)
        self.proj_copied = cl("proj_copied", 2 * H * GROUPS, credit=2, owner="scalar")
        tn = 1 + self.uses + GROUPS * self.cyc - self.uses - 1
        self.t_done = cl("t_done", tn)
        self.t_copied = cl("t_copied", tn, credit=2, owner="scalar")
        self.scores_ready = cl("scores_ready", self.NB * T)
        self.max_ready = cl("max_ready", self.NB * T)
        self.shifted = cl("shifted", self.NB * T)
        self.exp_ready = cl("exp_ready", T)
        self.norm_steps = 3 if self.masked else 2
        self.norm_step = cl("norm_step", self.norm_steps * T)
        self.probs_ready = cl("probs_ready", T)
        self.sum_done = cl("sum_done", T)
        self.res_done = cl("res_done", T, credit=2, owner="vector")
        self.done = cl("phase_done", 1)

    def head_span(self, b):
        h0 = sum(self.banks[:b])
        return h0, self.banks[b]

    def proj_use(self, g, k, j):
        return g * (2 * self.heads) + k * self.half + j

    def head_of(self, k, j):
        return (k % 2) * self.half + j

    def spread(self, k):
        u, n = self.uses, self.half
        m = n if k == GT - 1 else n - u
        return range(u), range(u, m), range(m, n)

    def t_use(self, g, k, what, j, last):
        n = 1 + self.uses + g * self.cyc + 2 * self.uses * k + (1 if k > 1 and not last else 0)
        return n + (self.uses if what == 1 else 2 * self.uses if what == 2 else 0) + j

    def t_slot(self, par, k, what, j, last):
        return self.t_use(par, k, what, j, last) % 2

    def sync(self, eng):
        s = self.src
        eng.wait_ge(self.before.sem, self.before.at(1))
        sem = self.w_loaded.sem
        for dst, src in ((self.wq[:, :], s["wq"]), (self.wk[:, :], s["wk"]), (self.wv[:, :], s["wv"]),
                         (self.wo[:, :, :], s["wo"].rearrange("(p r) d -> r p d", r=P))):
            eng.dma_start(dst, src).then_inc(sem, 16)
        with self.core.nc.allow_non_contiguous_dma("single columns"):
            if self.affine:
                eng.dma_start(self.gb[:, 0:1], s["gamma"].unsqueeze(1)).then_inc(sem, 16)
                eng.dma_start(self.gb[:, 1:2], s["beta"].unsqueeze(1)).then_inc(sem, 16)
            if self.masked:
                eng.dma_start(self.mask_u8[:, :], s["mask"]).then_inc(sem, 16)
            eng.dma_start(self.bias[:, :], s["bo"].partition_broadcast(P)).then_inc(self.bias_loaded.sem, 16)

    def project(self, eng, g, k, j):
        c = self.core
        hi, lo = (self.vo_hi, self.vo_lo) if k >= 2 else (self.mt_hi, self.mt_lo)
        cols = ds(GCOLS * g, GCOLS)
        h, slot = self.head_of(k, j), self.proj_use(0, k, j) % 2
        eng.wait_ge(self.proj_copied.sem, self.proj_copied.free(self.proj_use(g, k, j)))
        three_passes(eng, c.ps_p[:, slot, 0:GCOLS], [w[:, h, :] for w in (hi, lo)],
                     [q[:, cols] for q in (c.ct_hi, c.ct_lo)]).then_inc(self.proj_done.sem, 1)

    def turn_z(self, eng, g, u, slot):
        c = self.core
        eng.wait_ge(self.ln.z_ready.sem, self.ln.z_ready.at(GT * g + GT))
        eng.wait_ge(self.t_copied.sem, self.t_copied.free(u))
        for k in range(GT):
            mm = eng.transpose(c.ps_t[:, slot, k * P:(k + 1) * P], c.z[:, k, :], c.ident[:, :])
        mm.then_inc(self.t_done.sem, 1)

    def turn_chunks(self, eng, j, src, use, slot):
        c = self.core
        eng.wait_ge(self.t_copied.sem, self.t_copied.free(use))
        for i in range(GT * j, min(GT * j + GT, self.chunks)):
            w = min(P, self.rows - P * i)
            mm = eng.transpose(c.ps_t[0:w, slot, (i % GT) * P:(i % GT + 1) * P],
                               src[:, P * i:P * i + w], c.ident[:, :])
        mm.then_inc(self.t_done.sem, 1)

    def scores(self, eng, t, zt, keys, first=False):
        c = self.core
        for b in range(self.NB):
            h0, nh = self.head_span(b)
            if not first:
                eng.wait_ge(self.shifted.sem, self.shifted.at(self.NB * (t - 1) + b + 1))
            o = c.ps_s[:, b, 0:nh * KEYS]
            if self.masked:
                eng.matmul(o, c.ident_bf[:, :],
                           self.mask_add[:, :].unsqueeze(1).broadcast_to([P, nh, KEYS]),
                           start=True, stop=False)
            eng.matmul(o, zt, keys[:, h0:h0 + nh, :], start=not self.masked, stop=True)\
               .then_inc(self.scores_ready.sem, 1)

    def weighted_sum(self, eng, t, k, prob_use):
        c = self.core
        eng.wait_ge(self.res_done.sem, self.res_done.at(t))
        for i in range(self.chunks):
            w = min(P, self.rows - P * i)
            if i % GT == 0:
                eng.wait_ge(self.t_copied.sem, self.t_copied.at(prob_use(i // GT) + 1))
            mm = eng.matmul(c.ps_o[:, (k % 2) * P:(k % 2 + 1) * P], self.pt[0:w, i, :],
                            self.val[0:w, i, :], start=(i == 0), stop=(i == self.chunks - 1))
        mm.then_inc(self.sum_done.sem, 1)

    def tensor(self, eng):
        c, H = self.core, self.heads
        eng.wait_ge(self.before.sem, self.before.at(1))
        eng.wait_ge(self.w_loaded.sem, self.w_loaded.at(16 * self.loads))

        def turn_weights(p):
            cols = slice(P * p, P * p + P)
            if p >= 2:
                eng.wait_ge(self.wt_ready.sem, self.wt_ready.at(p - 1))
            o = c.ps_t[:, p % 2, :]
            eng.transpose(o[:, 0:P], self.wq[:, cols], c.ident[:, :])
            eng.transpose(o[:, P:P + CDIM], self.wk[:, cols], c.ident[0:CDIM, 0:CDIM])
            eng.transpose(o[:, P + CDIM:P + 2 * CDIM], self.wv[:, cols], c.ident[0:CDIM, 0:CDIM])\
               .then_inc(self.w_turned.sem, 1)

        def products(p):
            eng.wait_ge(self.wt_ready.sem, self.wt_ready.at(p + 1))
            if p >= 1:
                eng.wait_ge(self.lo_done.sem, self.lo_done.at(4 * p))
            wt = self.wt[:, p % 2, :]
            for s in range(2):
                r = slice(HEAD * s, HEAD * s + HEAD)
                o = c.ps_s[0:CDIM, s, :]
                eng.matmul(o[:, 0:P], wt[r, P:P + CDIM], wt[r, 0:P], start=True, stop=True)
                mm = eng.matmul(o[:, P:2 * P], wt[r, P + CDIM:P + 2 * CDIM], self.wo[r, p, :],
                                start=True, stop=True)
            mm.then_inc(self.prod_done.sem, 1)

        turn_weights(0)
        for p in range(self.pairs):
            if p + 1 < self.pairs:
                turn_weights(p + 1)
            products(p)
        eng.wait_ge(self.lo_done.sem, self.lo_done.at(4 * self.pairs))
        eng.wait_ge(self.hi_done.sem, self.hi_done.at(4 * self.pairs))

        for k in range(GT):
            for j in range(self.half):
                self.project(eng, 0, k, j)
        self.turn_z(eng, 0, 0, 0)
        eng.wait_ge(self.t_copied.sem, self.t_copied.at(1))
        eng.wait_ge(self.proj_copied.sem, self.proj_copied.at(2 * H))
        if self.masked:
            eng.wait_ge(self.mask_ready.sem, self.mask_ready.at(5))
        self.scores(eng, 0, self.zt[:, 0, 0:P], self.keys[:, 0, 0], first=True)
        flat = lambda par, k: self.vals_t[:, par, k].rearrange("p h k -> p (h k)")
        for j in range(self.uses):
            self.turn_chunks(eng, j, flat(0, 0), 1 + j, (1 + j) % 2)
        self.scores(eng, 1, self.zt[:, 0, P:2 * P], self.keys[:, 0, 1])

        def body(g, par, left):
            last = left == 0
            for k in range(GT):
                t, n1, n2 = GT * g + k, (k + 1) % GT, (k + 2) % GT
                par1, par2 = par if n1 else 1 - par, par if n2 == k + 2 else 1 - par
                early, middle, late = [() if last else part for part in self.spread(k)]
                eng.wait_ge(self.probs_ready.sem, self.probs_ready.at(t + 1))
                for j in range(self.uses):
                    self.turn_chunks(eng, j, self.e[:, k % 2, :], self.t_use(g, k, 0, j, last),
                                     self.t_slot(par, k, 0, j, last))
                    if not last:
                        self.project(eng, g + 1, k, early[j])
                if not (last and k >= 2):
                    if k == 2:
                        eng.wait_ge(self.proj_copied.sem,
                                    self.proj_copied.at(self.proj_use(g + 1, 1, self.half - 1) + 1))
                        eng.wait_ge(self.t_copied.sem, self.t_copied.at(self.t_use(g, 1, 2, 0, last) + 1))
                    self.scores(eng, t + 2, self.zt[:, par2, n2 * P:(n2 + 1) * P], self.keys[:, par2, n2])
                for j in middle:
                    self.project(eng, g + 1, k, j)
                self.weighted_sum(eng, t, k, lambda j: self.t_use(g, k, 0, j, last))
                if not (last and k == GT - 1):
                    if n1 == 0:
                        eng.wait_ge(self.proj_copied.sem,
                                    self.proj_copied.at(self.proj_use(g + 1, k, self.half - 1) + 1))
                    for j in range(self.uses):
                        self.turn_chunks(eng, j, flat(par1, n1), self.t_use(g, k, 1, j, last),
                                         self.t_slot(par, k, 1, j, last))
                        if late:
                            self.project(eng, g + 1, k, late[j])
                if k == 1 and not last:
                    self.turn_z(eng, g + 1, self.t_use(g, k, 2, 0, last), self.t_slot(par, k, 2, 0, last))

        for_groups(eng, body)

    def copy_proj(self, eng, g, par, k, j):
        c = self.core
        dst = self.vals_t if k >= 2 else self.keys
        h, slot = self.head_of(k, j), self.proj_use(0, k, j) % 2
        eng.wait_ge(self.proj_done.sem, self.proj_done.at(self.proj_use(g, k, j) + 1))
        eng.activation(dst[:, par, :, h, :],
                       c.ps_p[:, slot, 0:GCOLS].rearrange("p (b k) -> p b k", b=GT), ACT.Copy)\
           .then_inc(self.proj_copied.sem, 1)

    def copy_zt(self, eng, par, u, slot):
        c = self.core
        eng.wait_ge(self.t_done.sem, self.t_done.at(u + 1))
        if self.affine:
            eng.activation(self.zt[:, par, :], c.ps_t[:, slot, :], ACT.Identity,
                           scale=self.gb[:, 0:1], bias=self.gb[:, 1:2]).then_inc(self.t_copied.sem, 1)
        else:
            eng.activation(self.zt[:, par, :], c.ps_t[:, slot, :], ACT.Copy)\
               .then_inc(self.t_copied.sem, 1)

    def copy_chunks(self, eng, j, dst, use, slot):
        c = self.core
        i0, i1 = GT * j, min(GT * j + GT, self.chunks)
        full = min(i1, self.rows // P)
        eng.wait_ge(self.t_done.sem, self.t_done.at(use + 1))
        src = c.ps_t[:, slot, :].rearrange("p (i d) -> p i d", i=GT)
        if full > i0:
            mm = eng.activation(dst[:, i0:full, :], src[:, 0:full - i0, :], ACT.Copy)
        if full < i1:
            w = self.rows - P * full
            mm = eng.activation(dst[0:w, full, :], src[0:w, full - i0, :], ACT.Copy)
        mm.then_inc(self.t_copied.sem, 1)

    def exponentials(self, eng, t, par):
        eng.wait_ge(self.shifted.sem, self.shifted.at(self.NB * (t + 1)))
        eng.activation(self.e[:, par, :], self.e[:, par, :], ACT.Exp).then_inc(self.exp_ready.sem, 1)

    def scalar(self, eng):
        c, H = self.core, self.heads
        eng.wait_ge(self.before.sem, self.before.at(1))
        for p in range(self.pairs):
            eng.wait_ge(self.w_turned.sem, self.w_turned.at(p + 1))
            if p >= 2:
                eng.wait_ge(self.prod_done.sem, self.prod_done.at(p - 1))
            eng.activation(self.wt[:, p % 2, :], c.ps_t[:, p % 2, 0:P + 2 * CDIM], ACT.Copy)\
               .then_inc(self.wt_ready.sem, 1)
        if self.affine:
            eng.wait_ge(self.w_loaded.sem, self.w_loaded.at(16 * self.loads))
        eng.wait_ge(self.prod_done.sem, self.prod_done.at(self.pairs))
        for k in range(GT):
            for j in range(self.half):
                self.copy_proj(eng, 0, 0, k, j)
        self.copy_zt(eng, 0, 0, 0)
        for j in range(self.uses):
            self.copy_chunks(eng, j, self.val, 1 + j, (1 + j) % 2)
        self.exponentials(eng, 0, 0)

        def body(g, par, left):
            last = left == 0
            for k in range(GT):
                t = GT * g + k
                more = not (last and k == GT - 1)
                early, middle, late = [() if last else part for part in self.spread(k)]
                if more and H == 8:
                    self.exponentials(eng, t + 1, (k + 1) % 2)
                for j in range(self.uses):
                    self.copy_chunks(eng, j, self.pt, self.t_use(g, k, 0, j, last),
                                     self.t_slot(par, k, 0, j, last))
                    if not last:
                        self.copy_proj(eng, g + 1, 1 - par, k, early[j])
                if more and H > 8:
                    self.exponentials(eng, t + 1, (k + 1) % 2)
                for j in middle:
                    self.copy_proj(eng, g + 1, 1 - par, k, j)
                if more:
                    for j in range(self.uses):
                        self.copy_chunks(eng, j, self.val, self.t_use(g, k, 1, j, last),
                                         self.t_slot(par, k, 1, j, last))
                        if late:
                            self.copy_proj(eng, g + 1, 1 - par, k, late[j])
                if k == 1 and not last:
                    self.copy_zt(eng, 1 - par, self.t_use(g, k, 2, 0, last),
                                 self.t_slot(par, k, 2, 0, last))

        for_groups(eng, body)

    def shift(self, eng, t, par):
        c = self.core
        view = lambda b, nh: c.ps_s[:, b, 0:nh * KEYS].rearrange("p (h k) -> p h k", h=nh)
        for b in range(self.NB):
            h0, nh = self.head_span(b)
            eng.wait_ge(self.scores_ready.sem, self.scores_ready.at(self.NB * t + b + 1))
            eng.tensor_reduce(self.mx[:, h0:h0 + nh], view(b, nh), AX.X, ALU.max)\
               .then_inc(self.max_ready.sem, 1)
        for b in range(self.NB):
            h0, nh = self.head_span(b)
            eng.wait_ge(self.max_ready.sem, self.max_ready.at(self.NB * t + b + 1))
            eng.tensor_tensor(
                self.e[:, par, h0 * KEYS:(h0 + nh) * KEYS].rearrange("p (h k) -> p h k", h=nh),
                view(b, nh), bc(self.mx[:, h0:h0 + nh], KEYS), ALU.subtract)\
               .then_inc(self.shifted.sem, 1)

    def normalise(self, eng, t, par):
        H = self.heads
        e = self.e[:, par, :].rearrange("p (h k) -> p h k", h=H)
        st, n = self.norm_step, self.norm_steps
        eng.wait_ge(self.exp_ready.sem, self.exp_ready.at(t + 1))
        eng.tensor_reduce(self.sm[:, :], e, AX.X, ALU.add).then_inc(st.sem, 1)
        eng.wait_ge(st.sem, st.at(n * t + 1))
        eng.reciprocal(self.rs[:, :], self.sm[:, :]).then_inc(st.sem, 1)
        eng.wait_ge(st.sem, st.at(n * t + 2))
        if self.masked:
            eng.tensor_scalar(self.rs[:, :], self.rs[:, :], self.some_key[:, 1:2], None, ALU.mult)\
               .then_inc(st.sem, 1)
            eng.wait_ge(st.sem, st.at(n * t + 3))
        eng.tensor_tensor(e, e, bc(self.rs[:, :], KEYS), ALU.mult).then_inc(self.probs_ready.sem, 1)

    def residual(self, eng, t, k):
        c = self.core
        eng.wait_ge(self.sum_done.sem, self.sum_done.at(t + 1))
        xt = c.x[:, ds(t, 1), :].rearrange("p a d -> p (a d)")
        eng.tensor_tensor(xt, c.ps_o[:, (k % 2) * P:(k % 2 + 1) * P], xt, ALU.add)\
           .then_inc(self.res_done.sem, 1)

    def vector(self, eng):
        c = self.core
        eng.wait_ge(self.before.sem, self.before.at(1))
        eng.wait_ge(self.w_loaded.sem, self.w_loaded.at(16 * self.loads))
        if self.masked:
            m = self.mask_ready
            eng.tensor_scalar(self.mask_add[:, :], self.mask_u8[:, :], -1.0, 1e30, ALU.add, ALU.mult)\
               .then_inc(m.sem, 1)
            eng.tensor_reduce(self.some_key[:, 0:1], self.mask_u8[:, :], AX.X, ALU.add).then_inc(m.sem, 1)
            eng.wait_ge(m.sem, m.at(2))
            eng.reciprocal(self.some_key[:, 1:2], self.some_key[:, 0:1]).then_inc(m.sem, 1)
            eng.wait_ge(m.sem, m.at(3))
            eng.tensor_scalar(self.some_key[:, 1:2], self.some_key[:, 1:2], 0.0, 1.0, ALU.mult, ALU.add)\
               .then_inc(m.sem, 1)
            eng.wait_ge(m.sem, m.at(4))
            eng.sem_inc(m.sem, 1)
        self.ln.vector_stats(eng, 0)
        hi, lo = self.hi_done, self.lo_done
        for p in range(self.pairs):
            eng.wait_ge(self.prod_done.sem, self.prod_done.at(p + 1))
            parts = [(s, w) for s in range(2) for w in range(2)]
            for s, w in parts:
                src = c.ps_s[0:CDIM, s, w * P:(w + 1) * P]
                dst = (self.mt_hi, self.vo_hi)[w][:, 2 * p + s, :]
                eng.tensor_scalar(dst, src, (HEAD ** -0.5, 1.0)[w], None, ALU.mult).then_inc(hi.sem, 1)
            for n, (s, w) in enumerate(parts):
                eng.wait_ge(hi.sem, hi.at(4 * p + n + 1))
                src = c.ps_s[0:CDIM, s, w * P:(w + 1) * P]
                h, l = (self.mt_hi, self.vo_hi)[w], (self.mt_lo, self.vo_lo)[w]
                eng.scalar_tensor_tensor(out=l[:, 2 * p + s, :], in0=src, scalar=(HEAD ** -0.5, 1.0)[w],
                                         in1=h[:, 2 * p + s, :].bitcast(F32), op0=ALU.mult,
                                         op1=ALU.subtract).then_inc(lo.sem, 1)
        self.ln.vector_z(eng, 0)
        self.shift(eng, 0, 0)
        self.shift(eng, 1, 1)
        self.normalise(eng, 0, 0)

        def body(g, par, left):
            last = left == 0
            for k in range(GT):
                t = GT * g + k
                more = not (last and k == GT - 1)
                if k == 0:
                    eng.wait_ge(self.ln.bias_added.sem, self.ln.bias_added.at(g + 1))
                if not last and k == 1:
                    self.ln.vector_z(eng, g + 1)
                if more and self.heads == 8:
                    self.normalise(eng, t + 1, (k + 1) % 2)
                if not (last and k >= 2):
                    self.shift(eng, t + 2, k % 2)
                if more and self.heads > 8:
                    self.normalise(eng, t + 1, (k + 1) % 2)
                self.residual(eng, t, k)
                if not last and k == 0:
                    self.ln.vector_stats(eng, g + 1)

        for_groups(eng, body)
        eng.wait_ge(self.res_done.sem, self.res_done.at(BATCH))
        eng.sem_inc(self.done.sem, 1)

    def gpsimd(self, eng):
        eng.wait_ge(self.before.sem, self.before.at(1))
        self.ln.pool(eng, 0)
        eng.wait_ge(self.bias_loaded.sem, self.bias_loaded.at(16))
        self.ln.pool_bias(eng, 0)
        with eng.Fori(1, GROUPS) as g:
            self.ln.pool(eng, g)
            self.ln.pool_bias(eng, g)


class Hidden(Phase):

    RING = 4

    def setup(self, before, widths, func, twice, bias, gated=False, once=None):
        core = self.core
        self.before, self.widths, self.func, self.gated = before, widths, func, gated
        self.C = len(widths)
        cl = core.claim
        self.ln = LayerNorm(core, twice, bias, once=once)
        G, C = GROUPS, self.C
        self.zt_turned = cl("zt_turned", G)
        self.zt_copied = cl("zt_copied", G)
        self.zt_hi_done = cl("zt_hi_done", G)
        self.zt_split = cl("zt_split", G)
        self.hid_done = cl("hid_done", C * G)
        self.act_done = cl("act_done", C * G)
        self.out_done = cl("out_done", G)
        self.added = cl("added", G, credit=2, owner="vector")
        self.done = cl("phase_done", 1)

    def buffers(self, ctx, n):
        sb = self.core.sb
        self.zt = sb(ctx, n + "zt", [P, GT * P], F32)
        self.zt_parts = [sb(ctx, f"{n}zt{h}", [P, 2, GT * P], F32R) for h in ("hi", "lo")]
        self.hid = sb(ctx, n + "hid", [P, 2, self.C, GT * P], F32)

    def hbank(self, c):
        return self.core.bank(c % self.RING)

    def obank(self, par):
        return self.core.bank(6 + par)

    def turn_z(self, eng, g, par):
        c = self.core
        eng.wait_ge(self.ln.z_ready.sem, self.ln.z_ready.at(GT * g + GT))
        for k in range(GT):
            mm = eng.transpose(c.bank(5)[:, k * P:(k + 1) * P], c.z[:, k, :], c.ident[:, :])
        mm.then_inc(self.zt_turned.sem, 1)

    def hidden(self, eng, g, par, first=False):
        eng.wait_ge(self.zt_split.sem, self.zt_split.at(g + 1))
        z = [p[:, par, :] for p in self.zt_parts]
        for c in range(self.C):
            if c >= self.RING:
                eng.wait_ge(self.act_done.sem, self.act_done.at(self.C * g + c - self.RING + 1))
            elif not first:
                older = max(j for j in range(self.C) if j % self.RING == c)
                eng.wait_ge(self.act_done.sem, self.act_done.at(self.C * (g - 1) + older + 1))
            w = self.widths[c]
            three_passes(eng, self.hbank(c)[0:w, :],
                         [q[:, c * P:c * P + w] for q in self.w1], z).then_inc(self.hid_done.sem, 1)

    def wait_hidden(self, eng, g):
        eng.wait_ge(self.act_done.sem, self.act_done.at(self.C * (g + 1)))

    def output(self, eng, g, par):
        self.wait_hidden(eng, g)
        eng.wait_ge(self.added.sem, self.added.free(g))
        for k in range(GT):
            o = self.obank(par)[:, k * P:(k + 1) * P]
            for c in range(self.C):
                w = self.widths[c]
                mm = eng.matmul(o, self.hid[0:w, par, c, k * P:(k + 1) * P], self.w2[0:w, c, :],
                                start=c == 0, stop=c == self.C - 1 and not self.gated)
            if self.gated:
                mm = self.gated_bias(eng, g, par, k, o)
        mm.then_inc(self.out_done.sem, 1)

    def tensor_walk(self, eng):
        self.turn_z(eng, 0, 0)
        self.hidden(eng, 0, 0, True)
        self.turn_z(eng, 1, 1)

        def step(g, par, left):
            if left > 0:
                self.hidden(eng, g + 1, 1 - par)
            if left > 1:
                self.turn_z(eng, g + 2, par)
            self.output(eng, g, par)

        for_groups(eng, step)

    def copy_zt(self, eng, g, par, first=False):
        if not first:
            eng.wait_ge(self.zt_split.sem, self.zt_split.at(g))
        eng.wait_ge(self.zt_turned.sem, self.zt_turned.at(g + 1))
        src = self.core.bank(5)
        if self.affine is not None:
            ins = eng.activation(self.zt[:, :], src, ACT.Identity, scale=self.affine[:, 0:1],
                                 bias=self.affine[:, 1:2])
        else:
            ins = eng.activation(self.zt[:, :], src, ACT.Copy)
        ins.then_inc(self.zt_copied.sem, 1)

    def activate(self, eng, g, par, first=False):
        eng.wait_ge(self.added.sem, self.added.free(g))
        for c in range(self.C):
            w = self.widths[c]
            eng.wait_ge(self.hid_done.sem, self.hid_done.at(self.C * g + c + 1))
            eng.activation(self.hid[0:w, par, c, :], self.hbank(c)[0:w, :], self.func,
                           bias=self.b1[0:w, c:c + 1]).then_inc(self.act_done.sem, 1)

    def scalar_walk(self, eng):
        self.copy_zt(eng, 0, 0, True)
        self.activate(eng, 0, 0, True)
        self.copy_zt(eng, 1, 1)

        def step(g, par, left):
            if left > 0:
                self.activate(eng, g + 1, 1 - par)
            if left > 1:
                self.copy_zt(eng, g + 2, par)

        for_groups(eng, step)

    def split_zt(self, eng, g, par):
        eng.wait_ge(self.zt_copied.sem, self.zt_copied.at(g + 1))
        hi, lo = (p[:, par, :] for p in self.zt_parts)
        eng.tensor_copy(hi, self.zt[:, :]).then_inc(self.zt_hi_done.sem, 1)
        eng.wait_ge(self.zt_hi_done.sem, self.zt_hi_done.at(g + 1))
        eng.tensor_tensor(lo, self.zt[:, :], hi.bitcast(F32), ALU.subtract).then_inc(self.zt_split.sem, 1)

    def apply_gates(self, eng, g, par):
        pass

    def add_output(self, eng, g, par):
        c = self.core
        eng.wait_ge(self.out_done.sem, self.out_done.at(g + 1))
        if self.ln.bias_added is not None:
            eng.wait_ge(self.ln.bias_added.sem, self.ln.bias_added.at(g + 1))
        xg = c.x[:, ds(GT * g, GT), :]
        eng.tensor_tensor(xg, self.obank(par).rearrange("p (k d) -> p k d", k=GT), xg, ALU.add)\
           .then_inc(self.added.sem, 1)

    def vector_walk(self, eng):
        self.ln.vector_z(eng, 0)
        self.split_zt(eng, 0, 0)
        self.ln.vector_stats(eng, 1)
        self.ln.vector_z(eng, 1)
        self.apply_gates(eng, 0, 0)
        self.split_zt(eng, 1, 1)

        def step(g, par, left):
            if left > 1:
                self.ln.vector_stats(eng, g + 2)
                self.ln.vector_z(eng, g + 2)
            if left > 0:
                self.apply_gates(eng, g + 1, 1 - par)
            if left > 1:
                self.split_zt(eng, g + 2, par)
            self.add_output(eng, g, par)

        for_groups(eng, step)
        eng.wait_ge(self.added.sem, self.added.at(GROUPS))
        eng.sem_inc(self.done.sem, 1)

    def gpsimd(self, eng):
        eng.wait_ge(self.before.sem, self.before.at(1))
        self.ln.pool(eng, 0)
        self.wait_bias(eng)
        self.ln.pool_bias(eng, 0)
        with eng.Fori(1, GROUPS) as g:
            self.ln.pool(eng, g)
            self.ln.pool_bias(eng, g)


class SiluFfn(Hidden):

    F = 512

    def __init__(self, core, before):
        self.core = core
        self.i = {k[len("L0_ffn_"):]: v for k, v in core.ins.items() if k.startswith("L0_ffn_")}
        C = self.F // P
        sb, ctx = core.sb, ExitStack()
        self.affine = sb(ctx, "f0_gb", [P, 2], F32)
        self.b1 = sb(ctx, "f0_b1", [P, C], F32)
        self.bias = sb(ctx, "f0_b2", [P, P], F32)
        self.q1 = sb(ctx, "f0_q1", [P, self.F], mybir.dt.int32)
        self.q2 = sb(ctx, "f0_q2", [P, C, P], mybir.dt.int32)
        self.s1 = sb(ctx, "f0_s1", [P, self.F], F32)
        self.w2 = self.s2 = sb(ctx, "f0_w2", [P, C, P], F32)
        self.w1 = [sb(ctx, f"f0_w1{h}", [P, self.F], F32R) for h in ("hi", "lo")]
        self.once = sb(ctx, "f0_once", [P, GT, P], F32)
        self.setup(before, [P] * C, ACT.Silu, True, self.bias, once=self.once)
        self.buffers(ctx, "f0_")
        ctx.close()
        self.loaded = core.claim("w_loaded", 16 * 8)
        self.prep = core.claim("prep_step", 6)

    def sync(self, eng):
        i = self.i
        eng.wait_ge(self.before.sem, self.before.at(1))
        with self.core.nc.allow_non_contiguous_dma("small columns"):
            for dst, src in (
                    (self.q1[:, :], i["fc1_q"]), (self.s1[:, :], i["fc1_scales"][0].partition_broadcast(P)),
                    (self.q2[:, :, :], i["fc2_q"].rearrange("(c p) d -> p c d", p=P)),
                    (self.s2[:, :, :].rearrange("p c d -> p (c d)"),
                     i["fc2_scales"].rearrange("c d -> (c d)").partition_broadcast(P)),
                    (self.affine[:, 0:1], i["ln_gamma"].unsqueeze(1)),
                    (self.affine[:, 1:2], i["ln_beta"].unsqueeze(1)),
                    (self.b1[:, :], i["fc1_bias"].rearrange("(c p) -> p c", p=P)),
                    (self.bias[:, :], i["fc2_bias"].partition_broadcast(P))):
                eng.dma_start(dst, src).then_inc(self.loaded.sem, 16)

    def wait_bias(self, eng):
        eng.wait_ge(self.prep.sem, self.prep.at(4))

    def vector(self, eng):
        eng.wait_ge(self.before.sem, self.before.at(1))
        self.ln.vector_stats(eng, 0)
        eng.wait_ge(self.loaded.sem, self.loaded.at(16 * 8))
        p = self.prep
        for q, s in ((self.q1, self.s1), (self.q2, self.s2)):
            q, s = q[:], s[:]
            eng.scalar_tensor_tensor(out=s, in0=q, scalar=-128.0, in1=s, op0=ALU.add, op1=ALU.mult)\
               .then_inc(p.sem, 1)
        eng.wait_ge(p.sem, p.at(2))
        eng.tensor_scalar(self.s2[:], self.s2[:], 0.5, None, ALU.mult).then_inc(p.sem, 1)
        eng.tensor_scalar(self.bias[:, :], self.bias[:, :], 0.5, None, ALU.mult).then_inc(p.sem, 1)
        eng.wait_ge(p.sem, p.at(4))
        eng.tensor_copy(self.w1[0][:], self.s1[:]).then_inc(p.sem, 1)
        eng.wait_ge(p.sem, p.at(5))
        eng.tensor_tensor(self.w1[1][:], self.s1[:], self.w1[0][:].bitcast(F32), ALU.subtract)\
           .then_inc(p.sem, 1)
        self.vector_walk(eng)

    def tensor(self, eng):
        eng.wait_ge(self.before.sem, self.before.at(1))
        eng.wait_ge(self.prep.sem, self.prep.at(6))
        self.tensor_walk(eng)

    def scalar(self, eng):
        eng.wait_ge(self.before.sem, self.before.at(1))
        eng.wait_ge(self.loaded.sem, self.loaded.at(16 * 8))
        self.scalar_walk(eng)


class QuantFfn(Phase):

    F = 512

    def __init__(self, core, before):
        self.core, self.before = core, before
        i = core.ins
        self.src = {k: i["L1_ffn_" + k] for k in ("W1", "b1", "W2", "b2")}
        self.C = C = self.F // P
        sb, ctx = core.sb, ExitStack()
        n = lambda s: "f1_" + s
        self.w = sb(ctx, n("w"), [P, 2, C, P], F32)
        self.wq = sb(ctx, n("wq"), [P, 2, C, P], BF16)
        self.wt = sb(ctx, n("wt"), [P, 2, C, P], BF16)
        self.b1 = sb(ctx, n("b1"), [P, C], F32)
        self.bias = sb(ctx, n("b2"), [P, P], F32)
        self.zall = sb(ctx, n("z"), [P, BATCH, P], F32)
        self.zq = sb(ctx, n("zq"), [P, 2, GT, P], BF16)
        self.zqt = sb(ctx, n("zqt"), [P, GROUPS * GT * P], BF16)
        self.zu = sb(ctx, n("zu"), [P, 2, GT * P], F32)
        self.h = sb(ctx, n("h"), [P, 2, C, GT * P], F32)
        self.hq = sb(ctx, n("hq"), [P, 2, C, GT * P], BF16)
        self.rng = sb(ctx, n("rng"), [P, 2, 2, GROUPS], F32)
        self.red = sb(ctx, n("red"), [P, 3, 2], F32)
        self.all = sb(ctx, n("all"), [P, 3, 2], F32)
        self.sc = sb(ctx, n("sc"), [P, 2, 8], F32)
        self.ws = sb(ctx, n("ws"), [P, 2, 2], F32)
        ctx.close()
        cl, G = core.claim, GROUPS
        self.loaded = cl("w_loaded", 16 * 4)
        self.ln = LayerNorm(core, False, self.bias,
                            lambda g, k: self.zall[:, ds(GT * g + k, 1), :].rearrange("p a d -> p (a d)"))
        self.chain = Chain(cl("quant_step", 60))
        self.reduce_ready = cl("reduce_ready", 3)
        self.reduced = cl("reduced", 3)
        self.wq_ready = cl("wq_ready", 1)
        self.wt_turned = cl("turned", 2)
        self.wt_ready = cl("wt_ready", 2)
        self.scale_ready = cl("scale_ready", 2)
        self.zq_step = cl("zq_step", 3 * G)
        self.zq_turned = cl("zt_turned", G)
        self.zqt_ready = cl("zt_copied", G)
        self.hid_done = cl("hid_done", 2 * C * G)
        self.act_done = cl("act_done", 2 * C * G)
        self.ranged = cl("ranged", 2 * G)
        self.hq_step = cl("hq_step", 3 * G)
        self.out_done = cl("out_done", G)
        self.added = cl("added", G, credit=2, owner="vector")
        self.done = cl("phase_done", 1)

    def sync(self, eng):
        s, sem = self.src, self.loaded.sem
        eng.wait_ge(self.before.sem, self.before.at(1))
        with self.core.nc.allow_non_contiguous_dma("small columns"):
            eng.dma_start(self.w[:, 0], s["W1"].rearrange("(c p) d -> p c d", p=P)).then_inc(sem, 16)
            eng.dma_start(self.w[:, 1], s["W2"].rearrange("p (c h) -> p c h", c=self.C)).then_inc(sem, 16)
            eng.dma_start(self.b1[:, :], s["b1"].rearrange("(c p) -> p c", p=P)).then_inc(sem, 16)
            eng.dma_start(self.bias[:, :], s["b2"].partition_broadcast(P)).then_inc(sem, 16)

    def gpsimd(self, eng):
        eng.wait_ge(self.before.sem, self.before.at(1))

        def over_partitions(n):
            eng.wait_ge(self.reduce_ready.sem, self.reduce_ready.at(n + 1))
            eng.partition_all_reduce(self.all[:, n, :], self.red[:, n, :], P,
                                     bass.bass_isa.ReduceOp.max).then_inc(self.reduced.sem, 1)

        over_partitions(0)
        eng.wait_ge(self.loaded.sem, self.loaded.at(16 * 4))
        with eng.Fori(0, GROUPS) as g:
            self.ln.pool(eng, g)
            self.ln.pool_bias(eng, g)
        over_partitions(1)
        over_partitions(2)

    def scales(self, eng, n):
        mx, neg_mn = self.all[:, 1 + n, 0:1], self.all[:, 1 + n, 1:2]
        sc = lambda j: self.sc[:, n, j:j + 1]
        do = lambda ins: self.chain.step(eng, ins)
        do(eng.tensor_tensor(sc(5), mx, neg_mn, ALU.add))
        do(eng.tensor_scalar(sc(0), sc(5), 1.0 / 255.0, 1e-8, ALU.mult, ALU.max))
        do(eng.reciprocal(sc(1), sc(0)))
        do(eng.tensor_tensor(sc(5), neg_mn, sc(1), ALU.mult))
        do(eng.tensor_scalar(sc(5), sc(5), MAGIC, MAGIC, ALU.add, ALU.subtract))
        do(eng.tensor_scalar(sc(5), sc(5), -128.0, -128.0, ALU.add, ALU.max))
        do(eng.tensor_scalar(sc(5), sc(5), 127.0, -1.0, ALU.min, ALU.mult))
        do(eng.tensor_scalar(sc(2), sc(5), -128.0, None, ALU.add))
        do(eng.tensor_scalar(sc(3), sc(5), 127.0, None, ALU.add))
        do(eng.tensor_tensor(sc(4), sc(0), self.ws[:, 0, n:n + 1], ALU.mult))
        eng.sem_inc(self.scale_ready.sem, 1)

    def quantise(self, eng, n, src, tmp, dst, claim, g):
        sc = lambda j: self.sc[:, n, j:j + 1]
        eng.tensor_scalar(tmp, src, sc(1), sc(2), ALU.mult, ALU.max).then_inc(claim.sem, 1)
        eng.wait_ge(claim.sem, claim.at(3 * g + 1))
        eng.tensor_scalar(tmp, tmp, sc(3), MAGIC, ALU.min, ALU.add).then_inc(claim.sem, 1)
        eng.wait_ge(claim.sem, claim.at(3 * g + 2))
        eng.tensor_scalar(dst, tmp, MAGIC, None, ALU.subtract).then_inc(claim.sem, 1)

    def ranges(self, eng, n, g, src):
        eng.tensor_reduce(self.rng[:, n, 0, ds(g, 1)], src, AX.X, ALU.max).then_inc(self.ranged.sem, 1)
        eng.tensor_reduce(self.rng[:, n, 1, ds(g, 1)], src, AX.X, ALU.min, negate=True)\
           .then_inc(self.ranged.sem, 1)

    def total_range(self, eng, n):
        self.chain.step(eng, eng.tensor_reduce(self.red[:, 1 + n, :], self.rng[:, n], AX.X, ALU.max))
        eng.sem_inc(self.reduce_ready.sem, 1)

    def vector(self, eng):
        c, C = self.core, self.C
        do = lambda ins: self.chain.step(eng, ins)
        eng.wait_ge(self.before.sem, self.before.at(1))
        eng.wait_ge(self.loaded.sem, self.loaded.at(16 * 4))
        for w in range(2):
            do(eng.tensor_reduce(self.red[:, 0, w:w + 1], self.w[:, w].rearrange("p c d -> p (c d)"), AX.X,
                                 ALU.max, apply_absolute_value=True))
        eng.sem_inc(self.reduce_ready.sem, 1)
        self.ln.vector_stats(eng, 0)
        eng.wait_ge(self.reduced.sem, self.reduced.at(1))
        do(eng.tensor_scalar(self.ws[:, 0, :], self.all[:, 0, :], 1.0 / 127.0, 1e-8, ALU.mult, ALU.max))
        do(eng.reciprocal(self.ws[:, 1, :], self.ws[:, 0, :]))
        for w in range(2):
            do(eng.tensor_scalar(self.w[:, w], self.w[:, w], self.ws[:, 1, w:w + 1], -127.0, ALU.mult, ALU.max))
        do(eng.tensor_scalar(self.w[:], self.w[:], 127.0, MAGIC, ALU.min, ALU.add))
        eng.tensor_scalar(self.wq[:], self.w[:], MAGIC, None, ALU.subtract).then_inc(self.wq_ready.sem, 1)

        with eng.Fori(0, GROUPS - 1) as g:
            self.ln.vector_z(eng, g)
            self.ln.vector_stats(eng, g + 1)
            eng.wait_ge(self.ln.z_ready.sem, self.ln.z_ready.at(GT * g + GT))
            self.ranges(eng, 0, g, self.zall[:, ds(GT * g, GT), :].rearrange("p k d -> p (k d)"))
        self.ln.vector_z(eng, GROUPS - 1)
        eng.wait_ge(self.ln.z_ready.sem, self.ln.z_ready.at(GT * GROUPS))
        self.ranges(eng, 0, GROUPS - 1, self.zall[:, BATCH - GT:BATCH, :].rearrange("p k d -> p (k d)"))
        eng.wait_ge(self.ranged.sem, self.ranged.at(2 * GROUPS))
        self.total_range(eng, 0)
        eng.wait_ge(self.reduced.sem, self.reduced.at(2))
        self.scales(eng, 0)

        def quantise_z(g, par):
            self.quantise(eng, 0, self.zall[:, ds(GT * g, GT), :].rearrange("p k d -> p (k d)"),
                          self.zu[:, par], self.zq[:, par].rearrange("p k d -> p (k d)"), self.zq_step, g)

        def range_h(g, par):
            eng.wait_ge(self.act_done.sem, self.act_done.at(C * g + C))
            self.ranges_h(eng, g, par)

        quantise_z(0, 0)
        quantise_z(1, 1)

        def step(g, par, left):
            if left > 1:
                eng.wait_ge(self.zqt_ready.sem, self.zqt_ready.at(g + 1))
                quantise_z(g + 2, par)
            range_h(g, par)

        for_groups(eng, step)
        eng.wait_ge(self.ranged.sem, self.ranged.at(4 * GROUPS))
        self.total_range(eng, 1)
        eng.wait_ge(self.reduced.sem, self.reduced.at(3))
        self.scales(eng, 1)

        def quantise_h(g, par):
            eng.wait_ge(self.act_done.sem, self.act_done.at(C * (GROUPS + g) + C))
            h = self.h[:, par].rearrange("p c t -> p (c t)")
            self.quantise(eng, 1, h, h, self.hq[:, par].rearrange("p c t -> p (c t)"), self.hq_step, g)

        quantise_h(0, 0)

        def step(g, par, left):
            if left > 0:
                quantise_h(g + 1, 1 - par)
            eng.wait_ge(self.out_done.sem, self.out_done.at(g + 1))
            xg = c.x[:, ds(GT * g, GT), :].rearrange("p k d -> p (k d)")
            eng.scalar_tensor_tensor(out=xg, in0=c.bank(7 - 3 * par), scalar=self.sc[:, 1, 4:5], in1=xg,
                                     op0=ALU.mult, op1=ALU.add).then_inc(self.added.sem, 1)

        for_groups(eng, step)
        eng.wait_ge(self.added.sem, self.added.at(GROUPS))
        eng.sem_inc(self.done.sem, 1)

    def ranges_h(self, eng, g, par):
        h = self.h[:, par].rearrange("p c t -> p (c t)")
        eng.tensor_reduce(self.rng[:, 1, 0, ds(g, 1)], h, AX.X, ALU.max).then_inc(self.ranged.sem, 1)
        eng.tensor_reduce(self.rng[:, 1, 1, ds(g, 1)], h, AX.X, ALU.min, negate=True)\
           .then_inc(self.ranged.sem, 1)

    def tensor(self, eng):
        c, C = self.core, self.C
        eng.wait_ge(self.before.sem, self.before.at(1))
        eng.wait_ge(self.wq_ready.sem, self.wq_ready.at(1))
        turned = lambda b, k: c.bank(b)[:, 0:GT * P // 2].bitcast(BF16)[:, k * P:(k + 1) * P]
        for w in range(2):
            for k in range(C):
                mm = eng.transpose(turned(5 + w, k), self.wq[:, w, k, :], c.ident_bf[:, :])
            mm.then_inc(self.wt_turned.sem, 1)
        eng.wait_ge(self.wt_ready.sem, self.wt_ready.at(2))

        def turn_z(g, par):
            eng.wait_ge(self.zq_step.sem, self.zq_step.at(3 * g + 3))
            for k in range(GT):
                mm = eng.transpose(turned(5 + par, k), self.zq[:, par, k, :], c.ident_bf[:, :])
            mm.then_inc(self.zq_turned.sem, 1)

        def hidden(g, n, first=False):
            for k in range(C):
                if not first:
                    eng.wait_ge(self.act_done.sem, self.act_done.at(C * (n - 1) + k + 1))
                eng.matmul(c.bank(k), self.wt[:, 0, k, :], self.zqt[:, ds(GT * P * g, GT * P)],
                           start=True, stop=True).then_inc(self.hid_done.sem, 1)

        turn_z(0, 0)
        turn_z(1, 1)
        eng.wait_ge(self.zqt_ready.sem, self.zqt_ready.at(1))
        hidden(0, 0, True)

        def step(g, par, left):
            if left > 1:
                turn_z(g + 2, par)
            if left > 0:
                eng.wait_ge(self.zqt_ready.sem, self.zqt_ready.at(g + 2))
                hidden(g + 1, g + 1)

        for_groups(eng, step)
        hidden(0, GROUPS)

        def step(g, par, left):
            if left > 0:
                hidden(g + 1, GROUPS + g + 1)
            eng.wait_ge(self.hq_step.sem, self.hq_step.at(3 * g + 3))
            eng.wait_ge(self.added.sem, self.added.free(g))
            for k in range(GT):
                for j in range(C):
                    mm = eng.matmul(c.bank(7 - 3 * par)[:, k * P:(k + 1) * P],
                                    self.hq[:, par, j, k * P:(k + 1) * P], self.wt[:, 1, j, :],
                                    start=(j == 0), stop=(j == C - 1))
            mm.then_inc(self.out_done.sem, 1)

        for_groups(eng, step)

    def scalar(self, eng):
        c, C = self.core, self.C
        eng.wait_ge(self.before.sem, self.before.at(1))
        for w in range(2):
            eng.wait_ge(self.wt_turned.sem, self.wt_turned.at(w + 1))
            eng.activation(self.wt[:, w].rearrange("p c d -> p (c d)"),
                           c.bank(5 + w)[:, 0:GT * P // 2].bitcast(BF16), ACT.Copy)\
               .then_inc(self.wt_ready.sem, 1)

        def copy_z(g, par):
            eng.wait_ge(self.zq_turned.sem, self.zq_turned.at(g + 1))
            eng.activation(self.zqt[:, ds(GT * P * g, GT * P)],
                           c.bank(5 + par)[:, 0:GT * P // 2].bitcast(BF16), ACT.Copy)\
               .then_inc(self.zqt_ready.sem, 1)

        def gelu(n, par):
            for k in range(C):
                eng.wait_ge(self.hid_done.sem, self.hid_done.at(C * n + k + 1))
                eng.activation(self.h[:, par, k, :], c.bank(k), ACT.Gelu, scale=self.sc[:, 0, 4:5],
                               bias=self.b1[:, k:k + 1]).then_inc(self.act_done.sem, 1)

        copy_z(0, 0)
        copy_z(1, 1)
        eng.wait_ge(self.scale_ready.sem, self.scale_ready.at(1))
        gelu(0, 0)

        def step(g, par, left):
            if left > 1:
                copy_z(g + 2, par)
            if left > 0:
                eng.wait_ge(self.ranged.sem, self.ranged.at(2 * (GROUPS + g)))
                gelu(g + 1, 1 - par)

        for_groups(eng, step)
        eng.wait_ge(self.ranged.sem, self.ranged.at(4 * GROUPS))
        gelu(GROUPS, 0)
        gelu(GROUPS + 1, 1)

        def step(g, par, left):
            if left > 1:
                eng.wait_ge(self.hq_step.sem, self.hq_step.at(3 * g + 3))
                gelu(GROUPS + g + 2, par)

        for_groups(eng, step)


class TopTwo:

    def __init__(self, core, ctx, name, chain):
        sb = core.sb
        n = lambda s: f"{name}_{s}"
        self.chain = chain
        self.rank = sb(ctx, n("rank"), [P, 8], F32)
        self.one = [sb(ctx, n(f"one{j}"), [P, BATCH, 8], F32) for j in range(2)]
        self.tmp = sb(ctx, n("tmp"), [P, BATCH, 8], F32)
        self.rest = sb(ctx, n("rest"), [P, BATCH, 8], F32)
        self.best = sb(ctx, n("best"), [P, 2, BATCH], F32)
        self.first = sb(ctx, n("first"), [P, 2, BATCH], F32)

    def gpsimd(self, eng, ready):
        for e in range(8):
            ins = eng.memset(self.rank[:, e:e + 1], float(8 - e))
        ins.then_inc(ready.sem, 1)

    def vector(self, eng, score):
        do = lambda ins: self.chain.step(eng, ins)
        rank = self.rank[:, :].unsqueeze(1).broadcast_to([P, BATCH, 8])
        tmp = self.tmp[:, :, :]
        for j in range(2):
            src = score if j == 0 else self.rest[:, :, :]
            do(eng.tensor_reduce(self.best[:, j, :], src, AX.X, ALU.max))
            do(eng.tensor_tensor(tmp, src, bc(self.best[:, j, :], 8), ALU.is_ge))
            do(eng.tensor_tensor(tmp, tmp, rank, ALU.mult))
            do(eng.tensor_reduce(self.first[:, j, :], tmp, AX.X, ALU.max))
            do(eng.tensor_tensor(self.one[j][:, :, :], rank, bc(self.first[:, j, :], 8), ALU.is_equal))
            if j == 0:
                do(eng.tensor_scalar(tmp, self.one[0][:, :, :], -1e30, None, ALU.mult))
                do(eng.tensor_tensor(self.rest[:, :, :], tmp, score, ALU.add))


class GatedFfn(Hidden):

    E = 8
    H = 64
    RING = 3

    def __init__(self, core, before):
        self.core = core
        i = {k[len("L2_ffn_"):]: v for k, v in core.ins.items() if k.startswith("L2_ffn_")}
        self.i = i
        sb, ctx = core.sb, ExitStack()
        n = lambda s: "f2_" + s
        self.C = 5
        self.affine = None
        self.b1 = sb(ctx, n("b1"), [P, 5], F32)
        self.bias = sb(ctx, n("bs2"), [P, P], F32)
        self.b2 = sb(ctx, n("b2"), [self.E, P], F32)
        self.gw = sb(ctx, n("gate_w"), [P, self.E], F32)
        self.rs = sb(ctx, n("route_scale"), [P, 1], F32)
        self.w1f = sb(ctx, n("w1"), [P, 4 * P + self.H], F32)
        self.w2 = sb(ctx, n("w2"), [P, 5, P], F32)
        self.w1 = [sb(ctx, n("w1" + h), [P, 4 * P + self.H], F32R) for h in ("hi", "lo")]
        self.chain = Chain(core.claim("gate_step", 60))
        self.top = TopTwo(core, ctx, n("top"), self.chain)
        self.score = sb(ctx, n("score"), [P, BATCH, self.E], F32)
        self.gates = sb(ctx, n("gates"), [P, BATCH, self.E], F32)
        self.gate_t = sb(ctx, n("gate_t"), [self.E, 2, GT * P], F32)
        self.gate_g = sb(ctx, n("gate_g"), [P, 2, GT, self.E, self.H], F32)
        self.zs = sb(ctx, n("zs"), [P, 2, GT * P], F32)
        self.setup(before, [P] * 4 + [self.H], ACT.Gelu, False, None, gated=True)
        self.ln0 = self.ln
        self.ln = LayerNorm(core, False, self.bias)
        self.buffers(ctx, n(""))
        ctx.close()
        cl, G = core.claim, GROUPS
        self.loads = 14
        self.loaded = cl("w_loaded", 16 * self.loads)
        self.rank_ready = cl("rank_ready", 1)
        self.zs_turned = cl("t_done", G)
        self.zs_copied = cl("t_copied", G, credit=2, owner="scalar")
        self.logit_done = cl("logit_done", 1)
        self.exp_ready = cl("exp_ready", 1)
        self.w_ready = cl("wt_ready", 1)
        self.gates_ready = cl("gates_ready", 1)
        self.gate_staged = cl("gate_staged", G)
        self.gate_turned = cl("gate_turned", 5 * G)
        self.gate_taken = cl("gate_taken", 5 * G, credit=2, owner="vector")

    def sync(self, eng):
        i, sem = self.i, self.loaded.sem
        eng.wait_ge(self.before.sem, self.before.at(1))
        ld = lambda dst, src: eng.dma_start(dst, src).then_inc(sem, 16)
        with self.core.nc.allow_non_contiguous_dma("small columns"):
            ld(self.w1f[:, 0:4 * P].rearrange("d (e h) -> d e h", h=self.H), i["W1"].rearrange("e d h -> d e h"))
            ld(self.w1f[:, 4 * P:], i["Ws1"])
            for c in range(4):
                ld(self.w2[:, c, :], i["W2"][2 * c:2 * c + 2].rearrange("e h d -> (e h) d"))
            ld(self.w2[0:self.H, 4, :], i["Ws2"])
            for s in range(2):
                ld(self.b1[self.H * s:self.H * (s + 1), 0:4],
                   i["b1"].rearrange("(c s) h -> s h c", s=2)[s])
            ld(self.b1[0:self.H, 4:5], i["bs1"].unsqueeze(1))
            ld(self.bias[:, :], i["bs2"].partition_broadcast(P))
            ld(self.b2[:, :], i["b2"])
            ld(self.gw[:, :], i["gate_W"])
            ld(self.rs[:, :], i["route_scale"].partition_broadcast(P))

    def gpsimd(self, eng):
        eng.wait_ge(self.before.sem, self.before.at(1))
        self.top.gpsimd(eng, self.rank_ready)
        with eng.Fori(0, GROUPS) as g:
            self.ln0.pool(eng, g)
        eng.wait_ge(self.loaded.sem, self.loaded.at(16 * self.loads))

        def step(g, par, left):
            self.ln.pool(eng, g)
            self.ln.pool_bias(eng, g)
            eng.tensor_copy(self.gate_g[:, par].rearrange("p k e h -> p (k e) h"),
                            bc(self.gates[:, ds(GT * g, GT), :].rearrange("p k e -> p (k e)"), self.H))\
               .then_inc(self.gate_staged.sem, 1)

        eng.wait_ge(self.gates_ready.sem, self.gates_ready.at(1))
        for_groups(eng, step)

    def wait_hidden(self, eng, g):
        super().wait_hidden(eng, g)
        eng.wait_ge(self.gate_taken.sem, self.gate_taken.at(5 * g + 5))

    def gated_bias(self, eng, g, par, k, o):
        return eng.matmul(o, self.gate_t[:, par, k * P:(k + 1) * P], self.b2[:, :], start=False, stop=True)

    def tensor(self, eng):
        c = self.core
        eng.wait_ge(self.before.sem, self.before.at(1))
        eng.wait_ge(self.loaded.sem, self.loaded.at(16 * self.loads))

        def turn(g, par):
            eng.wait_ge(self.ln0.z_ready.sem, self.ln0.z_ready.at(GT * g + GT))
            eng.wait_ge(self.zs_copied.sem, self.zs_copied.free(g))
            for k in range(GT):
                mm = eng.transpose(c.ps_t[:, par, k * P:(k + 1) * P], c.z[:, k, :], c.ident[:, :])
            mm.then_inc(self.zs_turned.sem, 1)

        turn(0, 0)

        def step(g, par, left):
            if left > 0:
                turn(g + 1, 1 - par)
            eng.wait_ge(self.zs_copied.sem, self.zs_copied.at(g + 1))
            for k in range(GT):
                mm = eng.matmul(c.ps_o[:, ds(self.E * GT * g + self.E * k, self.E)],
                                self.zs[:, par, k * P:(k + 1) * P], self.gw[:, :], start=True, stop=True)
            if left == 0:
                mm.then_inc(self.logit_done.sem, 1)

        for_groups(eng, step)
        eng.wait_ge(self.w_ready.sem, self.w_ready.at(1))
        eng.wait_ge(self.gates_ready.sem, self.gates_ready.at(1))
        self.tensor_walk(eng)

    def hidden(self, eng, g, par, first=False):
        c = self.core
        super().hidden(eng, g, par, first)
        eng.wait_ge(self.gate_staged.sem, self.gate_staged.at(g + 1))
        for j in range(5):
            eng.wait_ge(self.gate_taken.sem, self.gate_taken.free(5 * g + j))
            o = c.bank(3 + (5 * par + j) % 2)
            for k in range(GT):
                if j < 4:
                    mm = eng.transpose(o[:, k * P:(k + 1) * P],
                                       self.gate_g[:, par, k, 2 * j:2 * j + 2, :].rearrange("p e h -> p (e h)"),
                                       c.ident[:, :])
                else:
                    mm = eng.transpose(o[0:self.E, k * P:(k + 1) * P], self.gate_g[:, par, k, :, 0],
                                       c.ident[:, :])
            mm.then_inc(self.gate_turned.sem, 1)

    def scalar(self, eng):
        c = self.core
        eng.wait_ge(self.before.sem, self.before.at(1))
        eng.wait_ge(self.loaded.sem, self.loaded.at(16 * self.loads))

        def step(g, par, left):
            eng.wait_ge(self.zs_turned.sem, self.zs_turned.at(g + 1))
            eng.activation(self.zs[:, par], c.ps_t[:, par, :], ACT.Copy).then_inc(self.zs_copied.sem, 1)

        for_groups(eng, step)
        eng.wait_ge(self.logit_done.sem, self.logit_done.at(1))
        eng.activation(self.score[:, :, :].rearrange("p b e -> p (b e)"), c.ps_o[:, :], ACT.Exp, scale=-1.0)\
           .then_inc(self.exp_ready.sem, 1)
        self.scalar_walk(eng)

    def apply_gates(self, eng, g, par):
        c = self.core
        for j in range(5):
            eng.wait_ge(self.gate_turned.sem, self.gate_turned.at(5 * g + j + 1))
            o = c.bank(3 + (5 * par + j) % 2)
            if j < 4:
                eng.wait_ge(self.act_done.sem, self.act_done.at(5 * g + j + 1))
                h = self.hid[:, par, j, :]
                ins = eng.tensor_tensor(h, o, h, ALU.mult)
            else:
                ins = eng.tensor_copy(self.gate_t[:, par], o[0:self.E, :])
            ins.then_inc(self.gate_taken.sem, 1)

    def vector(self, eng):
        c = self.core
        do = lambda ins: self.chain.step(eng, ins)
        eng.wait_ge(self.before.sem, self.before.at(1))
        self.ln0.vector_stats(eng, 0)
        self.ln0.vector_z(eng, 0)
        with eng.Fori(0, GROUPS - 1) as g:
            self.ln0.vector_stats(eng, g + 1)
            eng.wait_ge(self.zs_turned.sem, self.zs_turned.at(g + 1))
            self.ln0.vector_z(eng, g + 1)
        eng.wait_ge(self.loaded.sem, self.loaded.at(16 * self.loads))
        hi, lo = self.w1
        do(eng.tensor_copy(hi[:], self.w1f[:]))
        do(eng.tensor_tensor(lo[:], self.w1f[:], hi[:].bitcast(F32), ALU.subtract))
        eng.sem_inc(self.w_ready.sem, 1)
        sc = self.score[:, :, :]
        eng.wait_ge(self.exp_ready.sem, self.exp_ready.at(1))
        do(eng.tensor_scalar(sc, sc, 1.0, None, ALU.add))
        do(eng.reciprocal(sc, sc))
        do(eng.tensor_scalar(sc, sc, self.rs[:, 0:1], None, ALU.mult))
        eng.wait_ge(self.rank_ready.sem, self.rank_ready.at(1))
        self.top.vector(eng, sc)
        best, first = self.top.best, self.top.first
        do(eng.tensor_tensor(first[:, 0, :], best[:, 0, :], best[:, 1, :], ALU.add))
        do(eng.reciprocal(first[:, 0, :], first[:, 0, :]))
        for j in range(2):
            do(eng.tensor_tensor(best[:, j, :], best[:, j, :], first[:, 0, :], ALU.mult))
            one = self.top.one[j][:, :, :]
            do(eng.tensor_tensor(one, one, bc(best[:, j, :], 8), ALU.mult))
        do(eng.tensor_tensor(self.gates[:, :, :], self.top.one[0][:, :, :], self.top.one[1][:, :, :], ALU.add))
        eng.sem_inc(self.gates_ready.sem, 1)
        self.ln.vector_stats(eng, 0)
        self.vector_walk(eng)




class WideAttention(Phase):

    def __init__(self, core, before):
        self.core, self.before = core, before
        i = {k[len("L3_xattn_"):]: v for k, v in core.ins.items() if k.startswith("L3_xattn_")}
        self.i = i
        sb, ctx = core.sb, ExitStack()
        n = lambda s: "a3_" + s
        self.wq = sb(ctx, n("wq"), [P, P], F32)
        self.wk = sb(ctx, n("wk"), [CDIM, P], F32)
        self.wv = sb(ctx, n("wv"), [CDIM, P], F32)
        self.wkp = [sb(ctx, n("wk" + h), [CDIM, P], F32R) for h in ("hi", "lo")]
        self.wvp = [sb(ctx, n("wv" + h), [CDIM, P], F32R) for h in ("hi", "lo")]
        self.bq = sb(ctx, n("bq"), [P, 1], F32)
        self.bk = sb(ctx, n("bk"), [P, 1], F32)
        self.bias = sb(ctx, n("bv"), [P, P], F32)
        self.zt = sb(ctx, n("zt"), [P, 2, GT * P], F32)
        self.qt = sb(ctx, n("qt"), [P, 2, GT * P], F32)
        self.kt = sb(ctx, n("kt"), [P, 2, GCOLS], F32)
        self.vt = sb(ctx, n("vt"), [P, 2, GCOLS], F32)
        self.v = sb(ctx, n("v"), [KEYS, 2, GT, P], F32)
        self.e = sb(ctx, n("e"), [P, 2, GCOLS], F32)
        self.pt = sb(ctx, n("pt"), [KEYS, 2, GT, P], F32)
        self.stat = sb(ctx, n("stat"), [P, 3, GT], F32)
        ctx.close()
        cl, G = core.claim, GROUPS
        self.loaded = cl("w_loaded", 16 * 6)
        self.ln = LayerNorm(core, False, self.bias)
        self.chain = Chain(cl("wide_step", 4))
        self.w_ready = cl("wt_ready", 1)
        self.made = cl("t_done", 5 * G)
        self.copied = cl("t_copied", 5 * G)
        self.scores_ready = cl("scores_ready", G)
        self.max_ready = cl("max_ready", G)
        self.shifted = cl("shifted", G)
        self.exp_ready = cl("exp_ready", G)
        self.norm_step = cl("norm_step", 2 * G)
        self.probs_ready = cl("probs_ready", G)
        self.pt_turned = cl("zt_turned", G)
        self.pt_copied = cl("zt_copied", G)
        self.out_done = cl("out_done", G)
        self.added = cl("added", G, credit=2, owner="vector")
        self.done = cl("phase_done", 1)

    def sync(self, eng):
        i, sem = self.i, self.loaded.sem
        eng.wait_ge(self.before.sem, self.before.at(1))
        with self.core.nc.allow_non_contiguous_dma("small columns"):
            for dst, src in ((self.wq, i["Wq"]), (self.wk, i["Wk"]), (self.wv, i["Wv"]),
                             (self.bq, i["bq"].unsqueeze(1)), (self.bk, i["bk"].unsqueeze(1)),
                             (self.bias, i["bv"].partition_broadcast(P))):
                eng.dma_start(dst[:, :], src).then_inc(sem, 16)

    def gpsimd(self, eng):
        eng.wait_ge(self.before.sem, self.before.at(1))
        eng.wait_ge(self.loaded.sem, self.loaded.at(16 * 6))
        with eng.Fori(0, GROUPS) as g:
            self.ln.pool(eng, g)
            self.ln.pool_bias(eng, g)

    def tensor(self, eng):
        c = self.core
        eng.wait_ge(self.before.sem, self.before.at(1))
        eng.wait_ge(self.w_ready.sem, self.w_ready.at(1))

        def prepare(g, par, first=False):
            cols = ds(GCOLS * g, GCOLS)
            eng.wait_ge(self.ln.z_ready.sem, self.ln.z_ready.at(GT * g + GT))
            if not first:
                eng.wait_ge(self.copied.sem, self.copied.at(5 * g))
            for k in range(GT):
                mm = eng.transpose(c.bank(0)[:, k * P:(k + 1) * P], c.z[:, k, :], c.ident[:, :])
            mm.then_inc(self.made.sem, 1)
            ct = [c.ct_hi[:, cols], c.ct_lo[:, cols]]
            for b, w in ((1, self.wkp), (2, self.wvp)):
                three_passes(eng, c.bank(b)[:, 0:GCOLS], [q[:, :] for q in w], ct).then_inc(self.made.sem, 1)
            eng.wait_ge(self.copied.sem, self.copied.at(5 * g + 1))
            eng.matmul(c.bank(3), self.wq[:, :], self.zt[:, par], start=True, stop=True)\
               .then_inc(self.made.sem, 1)
            eng.wait_ge(self.copied.sem, self.copied.at(5 * g + 3))
            for k in range(GT):
                mm = eng.transpose(c.bank(5)[0:KEYS, k * P:(k + 1) * P],
                                   self.vt[:, par, k * KEYS:(k + 1) * KEYS], c.ident[:, :])
            mm.then_inc(self.made.sem, 1)

        def scores(g, par, first=False):
            eng.wait_ge(self.copied.sem, self.copied.at(5 * g + 4))
            if not first:
                eng.wait_ge(self.shifted.sem, self.shifted.at(g))
            for k in range(GT):
                mm = eng.matmul(c.bank(4)[:, k * KEYS:(k + 1) * KEYS], self.qt[:, par, k * P:(k + 1) * P],
                                self.kt[:, par, k * KEYS:(k + 1) * KEYS], start=True, stop=True)
            mm.then_inc(self.scores_ready.sem, 1)

        prepare(0, 0, True)
        scores(0, 0, True)

        def step(g, par, left):
            if left > 0:
                prepare(g + 1, 1 - par)
            eng.wait_ge(self.probs_ready.sem, self.probs_ready.at(g + 1))
            for k in range(GT):
                mm = eng.transpose(c.bank(6)[0:KEYS, k * P:(k + 1) * P],
                                   self.e[:, par, k * KEYS:(k + 1) * KEYS], c.ident[:, :])
            mm.then_inc(self.pt_turned.sem, 1)
            if left > 0:
                scores(g + 1, 1 - par)
            eng.wait_ge(self.pt_copied.sem, self.pt_copied.at(g + 1))
            eng.wait_ge(self.copied.sem, self.copied.at(5 * g + 5))
            eng.wait_ge(self.added.sem, self.added.at(g))
            for k in range(GT):
                mm = eng.matmul(c.bank(7)[:, k * P:(k + 1) * P], self.pt[:, par, k, :], self.v[:, par, k, :],
                                start=True, stop=True)
            mm.then_inc(self.out_done.sem, 1)

        for_groups(eng, step)

    def scalar(self, eng):
        c = self.core
        eng.wait_ge(self.before.sem, self.before.at(1))
        eng.wait_ge(self.loaded.sem, self.loaded.at(16 * 6))

        def prepare(g, par):
            for n in range(5):
                eng.wait_ge(self.made.sem, self.made.at(5 * g + n + 1))
                dst, src, bias = ((self.zt[:, par], c.bank(0), None),
                                  (self.kt[:, par], c.bank(1)[:, 0:GCOLS], self.bk),
                                  (self.vt[:, par], c.bank(2)[:, 0:GCOLS], None),
                                  (self.qt[:, par], c.bank(3), self.bq),
                                  (self.v[:, par].rearrange("p k d -> p (k d)"), c.bank(5)[0:KEYS, :], None))[n]
                if bias is None:
                    ins = eng.activation(dst, src, ACT.Copy)
                else:
                    ins = eng.activation(dst, src, ACT.Identity, bias=bias[:, 0:1])
                ins.then_inc(self.copied.sem, 1)

        def exponentials(g, par):
            eng.wait_ge(self.shifted.sem, self.shifted.at(g + 1))
            eng.activation(self.e[:, par], self.e[:, par], ACT.Exp).then_inc(self.exp_ready.sem, 1)

        prepare(0, 0)
        exponentials(0, 0)

        def step(g, par, left):
            if left > 0:
                prepare(g + 1, 1 - par)
            eng.wait_ge(self.pt_turned.sem, self.pt_turned.at(g + 1))
            eng.activation(self.pt[:, par].rearrange("p k t -> p (k t)"), c.bank(6)[0:KEYS, :], ACT.Copy)\
               .then_inc(self.pt_copied.sem, 1)
            if left > 0:
                exponentials(g + 1, 1 - par)

        for_groups(eng, step)

    def softmax_front(self, eng, g, par):
        c = self.core
        s = c.bank(4)[:, 0:GCOLS].rearrange("p (k s) -> p k s", k=GT)
        eng.wait_ge(self.scores_ready.sem, self.scores_ready.at(g + 1))
        eng.tensor_reduce(self.stat[:, 0, :], s, AX.X, ALU.max).then_inc(self.max_ready.sem, 1)
        eng.wait_ge(self.max_ready.sem, self.max_ready.at(g + 1))
        eng.tensor_tensor(self.e[:, par].rearrange("p (k s) -> p k s", k=GT), s,
                          bc(self.stat[:, 0, :], KEYS), ALU.subtract).then_inc(self.shifted.sem, 1)

    def softmax_back(self, eng, g, par):
        e, st = self.e[:, par].rearrange("p (k s) -> p k s", k=GT), self.norm_step
        eng.wait_ge(self.exp_ready.sem, self.exp_ready.at(g + 1))
        eng.tensor_reduce(self.stat[:, 1, :], e, AX.X, ALU.add).then_inc(st.sem, 1)
        eng.wait_ge(st.sem, st.at(2 * g + 1))
        eng.reciprocal(self.stat[:, 2, :], self.stat[:, 1, :]).then_inc(st.sem, 1)
        eng.wait_ge(st.sem, st.at(2 * g + 2))
        eng.tensor_tensor(e, e, bc(self.stat[:, 2, :], KEYS), ALU.mult).then_inc(self.probs_ready.sem, 1)

    def vector(self, eng):
        c = self.core
        do = lambda ins: self.chain.step(eng, ins)
        eng.wait_ge(self.before.sem, self.before.at(1))
        self.ln.vector_stats(eng, 0)
        eng.wait_ge(self.loaded.sem, self.loaded.at(16 * 6))
        for f, (hi, lo) in ((self.wk, self.wkp), (self.wv, self.wvp)):
            do(eng.tensor_copy(hi[:, :], f[:, :]))
            do(eng.tensor_tensor(lo[:, :], f[:, :], hi[:, :].bitcast(F32), ALU.subtract))
        eng.sem_inc(self.w_ready.sem, 1)
        self.ln.vector_z(eng, 0)
        self.ln.vector_stats(eng, 1)
        self.softmax_front(eng, 0, 0)
        self.ln.vector_z(eng, 1)
        self.softmax_back(eng, 0, 0)

        def step(g, par, left):
            if left > 1:
                self.ln.vector_stats(eng, g + 2)
            if left > 0:
                self.softmax_front(eng, g + 1, 1 - par)
            if left > 1:
                self.ln.vector_z(eng, g + 2)
            eng.wait_ge(self.out_done.sem, self.out_done.at(g + 1))
            eng.wait_ge(self.ln.bias_added.sem, self.ln.bias_added.at(g + 1))
            xg = c.x[:, ds(GT * g, GT), :].rearrange("p k d -> p (k d)")
            eng.tensor_tensor(xg, c.bank(7), xg, ALU.add).then_inc(self.added.sem, 1)
            if left > 0:
                self.softmax_back(eng, g + 1, 1 - par)

        for_groups(eng, step)
        eng.wait_ge(self.added.sem, self.added.at(GROUPS))
        eng.sem_inc(self.done.sem, 1)


class RoutedFfn(Phase):

    E = 8
    F = 512
    U = 2 * GT

    def __init__(self, core, before):
        self.core, self.before = core, before
        self.i = {k[len("L3_ffn_"):]: v for k, v in core.ins.items() if k.startswith("L3_ffn_")}
        core.ct_scope.close()
        sb, ctx, E, F = core.sb, ExitStack(), self.E, self.F
        n = lambda s: "f3_" + s
        self.C = C = F // P
        self.w1 = [sb(ctx, n("w1" + h), [P, E * F], F32R) for h in ("hi", "lo")]
        self.w2 = sb(ctx, n("w2"), [P, E * C * P], F32)
        self.b1 = sb(ctx, n("b1parts"), [2, E * F], F32R)
        self.b2 = sb(ctx, n("b2"), [E, P], F32)
        self.wr = sb(ctx, n("wr"), [P, E], F32)
        self.br = sb(ctx, n("br"), [P, E], F32)
        self.gamma = sb(ctx, n("gamma"), [P, P], F32)
        self.beta = sb(ctx, n("beta"), [P, P], F32)
        self.ones = sb(ctx, n("ones"), [P, P], F32)
        self.ones_r = sb(ctx, n("ones_r"), [2, P], F32R)
        self.sign = sb(ctx, n("sign"), [2, 1], F32)
        self.mean_all = sb(ctx, n("mean"), [P, BATCH], F32)
        self.rstd_all = sb(ctx, n("rstd"), [P, BATCH], F32)
        self.zmean = sb(ctx, n("zmean"), [P, BATCH], F32)
        self.weight = sb(ctx, n("weight"), [P, BATCH, 2], F32)
        self.offset = sb(ctx, n("offset"), [P, BATCH, 2], mybir.dt.int32)
        self.by_expert = sb(ctx, n("by_expert"), [E, BATCH], F32)
        self.by_expert_g = sb(ctx, n("by_expert_g"), [E, 2, GT], F32)
        self.st = sb(ctx, n("y_stats"), [P, GT, 6], F32)
        self.mv = sb(ctx, n("y_mean_var"), [P, GT, 2], F32)
        self.yr = sb(ctx, n("y_rstd"), [P, 2, GT], F32)
        self.z = sb(ctx, n("z"), [P, 2, GT, P], F32)
        self.chain = Chain(core.claim("route_step", 60))
        with ExitStack() as early:
            self.wf = sb(early, n("wf"), [P, E * F], F32)
            self.b1f = sb(early, n("b1f"), [2, 2, E * F], F32)
        with ExitStack() as early:
            self.top = TopTwo(core, early, n("top"), self.chain)
            self.score = sb(early, n("score"), [P, BATCH, E], F32)
        self.zt = sb(ctx, n("zt"), [P, GT * P], F32)
        self.ztp = [sb(ctx, n("zt" + h), [P, 2, GT * P], F32R) for h in ("hi", "lo")]
        self.h = sb(ctx, n("h"), [P, 2, F], F32)
        self.ht = sb(ctx, n("ht"), [P, 2, F], F32)
        ctx.close()
        cl, G, NU = core.claim, GROUPS, 2 * BATCH
        self.loaded = cl("w_loaded", 16 * 8)
        self.w2_loaded = cl("w2_loaded", 16)
        self.const_done = cl("rank_ready", 1)
        self.ln = LayerNorm(core, False, None)
        self.saved = cl("stats_saved", 2 * G)
        self.means_done = cl("t_done", G)
        self.zmean_ready = cl("wt_ready", 1)
        self.logit_done = cl("logit_done", 1)
        self.exp_go = cl("shifted", 2)
        self.exp_ready = cl("exp_ready", 2)
        self.routed = cl("gates_ready", 1)
        self.zb_ready = cl("zb_ready", GT * G)
        self.zt_turned = cl("zt_turned", G)
        self.zt_copied = cl("zt_copied", G)
        self.zt_hi_done = cl("zt_hi_done", G)
        self.zt_split = cl("zt_split", G)
        self.hid_done = cl("hid_done", NU)
        self.act_done = cl("act_done", NU)
        self.h_turned = cl("gate_turned", NU)
        self.h_copied = cl("h_copied", NU)
        self.bg_ready = cl("gate_staged", G)
        self.out_done = cl("out_done", G)
        self.y_ready = cl("added", G, credit=2, owner="vector")
        self.y_stats = cl("y_stats", GT * G)
        self.y_seen = cl("stats_seen", G)
        self.y_aggr = cl("y_aggr", GT * G)
        self.y_rstd = cl("y_rstd", 2 * G)
        self.y_norm = cl("y_norm", GT * G)
        self.pool_seen = cl("pool_seen", G)
        self.y_pool = cl("y_pool", 3 * G)
        self.done = cl("phase_done", 1)

    def sync(self, eng):
        i, sem = self.i, self.loaded.sem
        eng.wait_ge(self.before.sem, self.before.at(1))
        ld = lambda dst, src: eng.dma_start(dst, src).then_inc(sem, 16)
        ld(self.wf[:, :].rearrange("d (e f) -> d e f", e=self.E), i["W1"].rearrange("e d f -> d e f"))
        b1 = i["b1"].rearrange("(a e) f -> a (e f)", a=1)
        ld(self.b1f[0:1, 0, :], b1)
        ld(self.b1f[1:2, 0, :], b1)
        ld(self.b2[:, :], i["b2"])
        ld(self.wr[:, :], i["Wr"])
        ld(self.br[:, :], i["br"].partition_broadcast(P))
        ld(self.gamma[:, :], i["gamma"].partition_broadcast(P))
        ld(self.beta[:, :], i["beta"].partition_broadcast(P))
        eng.dma_start(self.w2[:, :].rearrange("p (a d) -> p a d", d=P),
                      i["W2"].rearrange("e (c p) d -> p (e c) d", p=P)).then_inc(self.w2_loaded.sem, 16)

    def gpsimd(self, eng):
        c = self.core
        eng.wait_ge(self.before.sem, self.before.at(1))
        with eng.Fori(0, GROUPS) as g:
            self.ln.pool(eng, g)
        eng.wait_ge(self.zmean_ready.sem, self.zmean_ready.at(1))
        self.top.gpsimd(eng, self.const_done)

        def finish(g, par):
            eng.wait_ge(self.y_aggr.sem, self.y_aggr.at(GT * g + GT))
            eng.tensor_tensor(c.ln_var[:, :], self.mv[:, :, 1], c.eps[:, :], ALU.add)\
               .then_inc(self.y_rstd.sem, 1)
            eng.wait_ge(self.y_rstd.sem, self.y_rstd.at(2 * g + 1))
            eng.tensor_tensor(self.yr[:, par], c.ln_var[:, :], c.neg_half[:, :], ALU.pow)\
               .then_inc(self.y_rstd.sem, 1)
            y = self.z[:, par]
            row = lambda a: a[:, :].unsqueeze(1).broadcast_to([P, GT, P])
            eng.wait_ge(self.y_norm.sem, self.y_norm.at(GT * g + GT))
            eng.tensor_tensor(y, y, row(self.gamma), ALU.mult).then_inc(self.y_pool.sem, 1)
            eng.wait_ge(self.y_pool.sem, self.y_pool.at(3 * g + 1))
            eng.tensor_tensor(y, y, row(self.beta), ALU.add).then_inc(self.y_pool.sem, 1)
            eng.wait_ge(self.y_pool.sem, self.y_pool.at(3 * g + 2))
            eng.sem_inc(self.pool_seen.sem, 1)
            xg = c.x[:, ds(GT * g, GT), :]
            eng.tensor_tensor(xg, xg, y, ALU.add).then_inc(self.y_pool.sem, 1)

        for_groups(eng, lambda g, par, left: finish(g, par))
        eng.wait_ge(self.y_pool.sem, self.y_pool.at(3 * GROUPS))
        eng.sem_inc(self.done.sem, 1)

    def tensor(self, eng):
        c, C, F, U = self.core, self.C, self.F, self.U
        eng.wait_ge(self.before.sem, self.before.at(1))
        with eng.Fori(0, GROUPS) as g:
            eng.wait_ge(self.ln.z_ready.sem, self.ln.z_ready.at(GT * g + GT))
            for k in range(GT):
                mm = eng.matmul(c.ps_o[:, ds(GT * g + k, 1)], c.z[:, k, :], self.ones[:, 0:1],
                                start=True, stop=True)
            mm.then_inc(self.means_done.sem, 1)
        eng.wait_ge(self.zmean_ready.sem, self.zmean_ready.at(1))
        for b in range(BATCH):
            mm = eng.matmul(c.bank(6)[:, self.E * b:self.E * (b + 1)],
                            self.zmean[:, b:b + 1].broadcast_to([P, P]), self.wr[:, :],
                            start=True, stop=True)
        mm.then_inc(self.logit_done.sem, 1)

        def turn_z(g, par):
            eng.wait_ge(self.zb_ready.sem, self.zb_ready.at(GT * g + GT))
            for k in range(GT):
                mm = eng.transpose(c.bank(5)[:, k * P:(k + 1) * P], self.z[:, par, k, :], c.ident[:, :])
            mm.then_inc(self.zt_turned.sem, 1)

        def hidden(u, j, par):
            off = eng.value_load(self.offset[0:1].rearrange("p b s -> p (b s)")[:, ds(u, 1)],
                                 min_val=0, max_val=F * (self.E - 1))
            k = j // 2
            o = c.bank(j % 2)
            eng.matmul(o, self.ones_r[:, :], self.b1[:, ds(off, F)], start=True, stop=False)
            three_passes(eng, o, [q[:, par, k * P:(k + 1) * P] for q in self.ztp],
                         [q[:, ds(off, F)] for q in self.w1], start=False).then_inc(self.hid_done.sem, 1)

        def turn(u, j):
            eng.wait_ge(self.act_done.sem, self.act_done.at(u + 1))
            for k in range(C):
                mm = eng.transpose(c.bank(2 + j % 2)[:, k * P:(k + 1) * P],
                                   self.h[:, j % 2, k * P:(k + 1) * P], c.ident[:, :])
            mm.then_inc(self.h_turned.sem, 1)

        def output(u, j, g, par):
            k, s = j // 2, j % 2
            off = eng.value_load(self.offset[0:1].rearrange("p b s -> p (b s)")[:, ds(u, 1)],
                                 min_val=0, max_val=F * (self.E - 1))
            o = c.bank(6 + par)[:, k * P:(k + 1) * P]
            if j == 0:
                eng.wait_ge(self.y_ready.sem, self.y_ready.free(g))
                eng.wait_ge(self.bg_ready.sem, self.bg_ready.at(g + 1))
            if s == 0:
                eng.matmul(o, self.by_expert_g[:, par, k:k + 1].broadcast_to([self.E, P]), self.b2[:, :],
                           start=True, stop=False)
            eng.wait_ge(self.h_copied.sem, self.h_copied.at(u + 1))
            for q in range(C):
                mm = eng.matmul(o, self.ht[:, s, q * P:(q + 1) * P], self.w2[:, ds(off + q * P, P)],
                                start=False, stop=(s == 1 and q == C - 1))
            if j == U - 1:
                mm.then_inc(self.out_done.sem, 1)

        eng.wait_ge(self.routed.sem, self.routed.at(1))
        eng.wait_ge(self.w2_loaded.sem, self.w2_loaded.at(16))
        turn_z(0, 0)
        eng.wait_ge(self.zt_split.sem, self.zt_split.at(1))
        hidden(0, 0, 0)
        hidden(1, 1, 0)
        turn(0, 0)

        def step(g, par, left):
            for j in range(U):
                u = U * g + j
                if j < U - 2:
                    hidden(u + 2, j + 2, par)
                elif left > 0:
                    if j == U - 2:
                        eng.wait_ge(self.zt_split.sem, self.zt_split.at(g + 2))
                    hidden(u + 2, j + 2 - U, 1 - par)
                if j < U - 1 or left > 0:
                    turn(u + 1, (j + 1) % U)
                output(u, j, g, par)
                if j == U - 4 and left > 0:
                    turn_z(g + 1, 1 - par)

        for_groups(eng, step)

    def scalar(self, eng):
        c, U = self.core, self.U
        eng.wait_ge(self.before.sem, self.before.at(1))
        sc = self.score[:, :, :]
        eng.wait_ge(self.exp_go.sem, self.exp_go.at(1))
        eng.activation(sc, sc, ACT.Exp).then_inc(self.exp_ready.sem, 1)
        eng.wait_ge(self.exp_go.sem, self.exp_go.at(2))
        w = self.weight[:, :, 1]
        eng.activation(w, w, ACT.Exp).then_inc(self.exp_ready.sem, 1)

        def copy_zt(g, first=False):
            eng.wait_ge(self.zt_turned.sem, self.zt_turned.at(g + 1))
            eng.activation(self.zt[:, :], c.bank(5), ACT.Copy).then_inc(self.zt_copied.sem, 1)

        def gelu(u, j):
            eng.wait_ge(self.hid_done.sem, self.hid_done.at(u + 1))
            eng.activation(self.h[:, j % 2, :], c.bank(j % 2), ACT.Gelu).then_inc(self.act_done.sem, 1)

        def scaled(u, j):
            w = self.weight[:, :, :].rearrange("p b s -> p (b s)")[:, ds(u, 1)]
            eng.wait_ge(self.h_turned.sem, self.h_turned.at(u + 1))
            eng.activation(self.ht[:, j % 2, :], c.bank(2 + j % 2), ACT.Copy, scale=w)\
               .then_inc(self.h_copied.sem, 1)

        eng.wait_ge(self.routed.sem, self.routed.at(1))
        copy_zt(0)
        gelu(0, 0)
        gelu(1, 1)
        scaled(0, 0)

        def step(g, par, left):
            for j in range(U):
                u = U * g + j
                if j < U - 2 or left > 0:
                    gelu(u + 2, j + 2)
                if j < U - 1 or left > 0:
                    scaled(u + 1, j + 1)
                if j == U - 4 and left > 0:
                    copy_zt(g + 1)

        for_groups(eng, step)

    def vector(self, eng):
        c, U, E, F = self.core, self.U, self.E, self.F
        do = lambda ins: self.chain.step(eng, ins)
        eng.wait_ge(self.before.sem, self.before.at(1))
        do(eng.memset(self.ones[:, :], 1.0))
        do(eng.tensor_copy(self.ones_r[:, :], self.ones[0:2, :]))
        do(eng.tensor_tensor(self.sign[:, :], c.ident[0:2, 0:1], c.ident[0:2, 1:2], ALU.subtract))
        self.ln.vector_stats(eng, 0)
        eng.wait_ge(self.loaded.sem, self.loaded.at(16 * 8))
        do(eng.tensor_copy(self.w1[0][:, :], self.wf[:, :]))
        do(eng.tensor_tensor(self.w1[1][:, :], self.wf[:, :], self.w1[0][:, :].bitcast(F32), ALU.subtract))
        b, hi = self.b1f[:, 0, :], self.b1f[:, 1, :]
        do(eng.tensor_copy(self.b1[:, :], b))
        do(eng.tensor_copy(hi, self.b1[:, :].bitcast(F32)))
        do(eng.tensor_scalar(b, b, c.ident[0:2, 1:2], None, ALU.mult))
        do(eng.scalar_tensor_tensor(out=self.b1[:, :], in0=hi, scalar=self.sign[:, 0:1], in1=b,
                                    op0=ALU.mult, op1=ALU.add))

        def first_pass(g, more):
            self.ln.vector_z(eng, g)
            eng.tensor_copy(self.mean_all[:, ds(GT * g, GT)], c.mean_var[:, :, 0]).then_inc(self.saved.sem, 1)
            eng.tensor_copy(self.rstd_all[:, ds(GT * g, GT)], c.rstd[:, :]).then_inc(self.saved.sem, 1)
            if more:
                eng.wait_ge(self.saved.sem, self.saved.at(2 * g + 2))
                self.ln.vector_stats(eng, g + 1)
            eng.wait_ge(self.means_done.sem, self.means_done.at(g + 1))

        with eng.Fori(0, GROUPS - 1) as g:
            first_pass(g, True)
        first_pass(GROUPS - 1, False)
        eng.tensor_scalar(self.zmean[:, :], c.ps_o[:, 0:BATCH], 1.0 / P, None, ALU.mult)\
           .then_inc(self.zmean_ready.sem, 1)

        sc, tmp, red = self.score[:, :, :], self.top.tmp[:, :, :], self.top.first[:, 0, :]
        eng.wait_ge(self.logit_done.sem, self.logit_done.at(1))
        do(eng.tensor_tensor(sc, c.bank(6).rearrange("p (b e) -> p b e", e=E),
                             self.br[:, :].unsqueeze(1).broadcast_to([P, BATCH, E]), ALU.add))
        do(eng.tensor_reduce(red, sc, AX.X, ALU.max))
        do(eng.tensor_tensor(sc, sc, bc(red, E), ALU.subtract))
        eng.sem_inc(self.exp_go.sem, 1)
        eng.wait_ge(self.exp_ready.sem, self.exp_ready.at(1))
        do(eng.tensor_reduce(red, sc, AX.X, ALU.add))
        do(eng.reciprocal(red, red))
        do(eng.tensor_tensor(sc, sc, bc(red, E), ALU.mult))
        eng.wait_ge(self.const_done.sem, self.const_done.at(1))
        self.top.vector(eng, sc)
        best, first, one = self.top.best, self.top.first, self.top.one
        w0, w1 = self.weight[:, :, 0], self.weight[:, :, 1]
        do(eng.tensor_tensor(w1, best[:, 1, :], best[:, 0, :], ALU.subtract))
        eng.sem_inc(self.exp_go.sem, 1)
        for s in range(2):
            do(eng.tensor_scalar(self.offset[:, :, s], first[:, s, :], -float(F), float(E * F),
                                 ALU.mult, ALU.add))
        eng.wait_ge(self.exp_ready.sem, self.exp_ready.at(2))
        do(eng.tensor_scalar(w0, w1, 1.0, None, ALU.add))
        do(eng.reciprocal(w0, w0))
        do(eng.tensor_tensor(w1, w1, w0, ALU.mult))
        for s, w in enumerate((w0, w1)):
            do(eng.tensor_tensor(one[s][:, :, :], one[s][:, :, :], bc(w, E), ALU.mult))
        do(eng.tensor_tensor(tmp, one[0][:, :, :], one[1][:, :, :], ALU.add))
        t8 = self.top.tmp[0:E, :, :]
        do(eng.tensor_tensor(t8, t8, c.ident[0:E, 0:E].unsqueeze(1).broadcast_to([E, BATCH, E]), ALU.mult))
        do(eng.tensor_reduce(self.by_expert[:, :], t8, AX.X, ALU.add))
        eng.sem_inc(self.routed.sem, 1)

        def make_z(g, par):
            for k in range(GT):
                col = ds(GT * g + k, 1)
                eng.tensor_scalar(self.z[:, par, k, :], c.x[:, col, :].rearrange("p a d -> p (a d)"),
                                  self.mean_all[:, col], self.rstd_all[:, col], ALU.subtract, ALU.mult)\
                   .then_inc(self.zb_ready.sem, 1)
            eng.tensor_copy(self.by_expert_g[:, par], self.by_expert[:, ds(GT * g, GT)])\
               .then_inc(self.bg_ready.sem, 1)

        def split_zt(g, par):
            eng.wait_ge(self.zt_copied.sem, self.zt_copied.at(g + 1))
            hi, lo = (p[:, par] for p in self.ztp)
            eng.tensor_copy(hi, self.zt[:, :]).then_inc(self.zt_hi_done.sem, 1)
            eng.wait_ge(self.zt_hi_done.sem, self.zt_hi_done.at(g + 1))
            eng.tensor_tensor(lo, self.zt[:, :], hi.bitcast(F32), ALU.subtract).then_inc(self.zt_split.sem, 1)

        def y_front(g, par):
            y = self.z[:, par].rearrange("p k d -> p (k d)")
            eng.wait_ge(self.out_done.sem, self.out_done.at(g + 1))
            eng.tensor_tensor(y, c.bank(6 + par), y, ALU.add).then_inc(self.y_ready.sem, 1)
            eng.wait_ge(self.y_ready.sem, self.y_ready.at(g + 1))
            for k in range(GT):
                eng.bn_stats(self.st[:, k, :], self.z[:, par, k, :]).then_inc(self.y_stats.sem, 1)
            eng.wait_ge(self.y_stats.sem, self.y_stats.at(GT * g + GT))
            eng.sem_inc(self.y_seen.sem, 1)
            for k in range(GT):
                eng.bn_aggr(self.mv[:, k, :], self.st[:, k, :]).then_inc(self.y_aggr.sem, 1)

        def y_back(g, par):
            eng.wait_ge(self.y_rstd.sem, self.y_rstd.at(2 * g + 2))
            for k in range(GT):
                y = self.z[:, par, k, :]
                eng.tensor_scalar(y, y, self.mv[:, k, 0:1], self.yr[:, par, k:k + 1], ALU.subtract, ALU.mult)\
                   .then_inc(self.y_norm.sem, 1)

        make_z(0, 0)
        split_zt(0, 0)

        def step(g, par, left, first=False):
            for j in range(U):
                if j == 0 and not first:
                    y_back(g - 1, 1 - par)
                if j == 3 and left > 0:
                    if not first:
                        eng.wait_ge(self.y_pool.sem, self.y_pool.at(3 * g))
                    make_z(g + 1, 1 - par)
                if j == 5 and left > 0:
                    split_zt(g + 1, 1 - par)
            y_front(g, par)

        step(0, 0, 2, True)
        step(1, 1, 2)
        with eng.Fori(1, GROUPS // 2 - 1) as i:
            step(2 * i, 0, 2)
            step(2 * i + 1, 1, 2)
        step(GROUPS - 2, 0, 1)
        step(GROUPS - 1, 1, 0)
        y_back(GROUPS - 1, 1)


class Finish(Phase):
    def __init__(self, core, before):
        self.core, self.before = core, before
        self.stored = core.claim("stored", 16 * 8)

    def sync(self, eng):
        c = self.core
        eng.wait_ge(self.before.sem, self.before.at(1))
        for q in range(8):
            b = slice(8 * q, 8 * q + 8)
            eng.dma_start(c.out[b].rearrange("b t d -> t b d"), c.x[:, b, :]).then_inc(self.stored.sem, 16)
        eng.wait_ge(self.stored.sem, self.stored.at(16 * 8))


def cross_attention_ffn_kernel(nc, ins, out):
    with ExitStack() as ctx:
        core = Core(nc, ctx, ins, out)
        phases = build_phases(core)
        block = ctx.enter_context(nc.Block())

        @block.sync
        def _(sp):
            for ph in phases:
                ph.sync(sp)

        @block.gpsimd
        def _(pool):
            core.grant("gpsimd", pool)
            for ph in phases:
                ph.gpsimd(pool)

        @block.scalar
        def _(act):
            core.grant("scalar", act)
            for ph in phases:
                ph.scalar(act)

        @block.vector
        def _(dve):
            core.grant("vector", dve)
            for ph in phases:
                ph.vector(dve)

        @block.tensor
        def _(pe):
            for ph in phases:
                ph.tensor(pe)


def build_phases(core):
    i = core.ins
    setup = Setup(core)
    phases, last = [setup], setup.done

    def add(make, *args, **kw):
        nonlocal last
        phases.append(make(core, *args, before=last, **kw))
        last = phases[-1].done

    wkv = i["L0_xattn_Wkv"]
    add(CrossAttention, "a0", 16, i["L0_xattn_Wq"], wkv[:, 0:1024], wkv[:, 1024:2048],
        i["L0_xattn_Wo"], i["L0_xattn_bo"], twice=True,
        gamma=i["L0_xattn_ln_gamma"], beta=i["L0_xattn_ln_beta"],
        mask=i["mask_1x1xSxS2_bk0"].rearrange("a b q k -> (a b q) k"))
    add(SiluFfn)
    for name, heads in (("L1", 8), ("L2", 16)):
        add(CrossAttention, "a" + name[1], heads, *(i[f"{name}_xattn_{w}"] for w in ("Wq", "Wk", "Wv", "Wo", "bo")))
        add(QuantFfn if name == "L1" else GatedFfn)
    add(WideAttention)
    add(RoutedFfn)
    phases.append(Finish(core, last))
    return phases


_INS = ['x', 'ctx_768', 'mask_1x1xSxS2_bk0', 'L0_xattn_ln_gamma', 'L0_xattn_ln_beta', 'L0_xattn_Wq',
        'L0_xattn_Wkv', 'L0_xattn_Wo', 'L0_xattn_bo', 'L0_ffn_ln_gamma', 'L0_ffn_ln_beta',
        'L0_ffn_fc1_q', 'L0_ffn_fc1_scales', 'L0_ffn_fc1_bias', 'L0_ffn_fc2_q', 'L0_ffn_fc2_scales',
        'L0_ffn_fc2_bias', 'L1_xattn_Wq', 'L1_xattn_Wk', 'L1_xattn_Wv', 'L1_xattn_Wo', 'L1_xattn_bo',
        'L1_ffn_W1', 'L1_ffn_b1', 'L1_ffn_W2', 'L1_ffn_b2', 'L2_xattn_Wq', 'L2_xattn_Wk',
        'L2_xattn_Wv', 'L2_xattn_Wo', 'L2_xattn_bo', 'L2_ffn_gate_W', 'L2_ffn_W1', 'L2_ffn_b1',
        'L2_ffn_W2', 'L2_ffn_b2', 'L2_ffn_Ws1', 'L2_ffn_bs1', 'L2_ffn_Ws2', 'L2_ffn_bs2',
        'L2_ffn_route_scale', 'L3_xattn_Wq', 'L3_xattn_bq', 'L3_xattn_Wk', 'L3_xattn_bk',
        'L3_xattn_Wv', 'L3_xattn_bv', 'L3_ffn_W1', 'L3_ffn_b1', 'L3_ffn_W2', 'L3_ffn_b2',
        'L3_ffn_Wr', 'L3_ffn_br', 'L3_ffn_gamma', 'L3_ffn_beta']


def _arrays(inputs):
    arrays = {}
    for name in _INS:
        a = np.ascontiguousarray(inputs[name])
        arrays[f"in_{name}_dram"] = a.reshape(a.shape or (1,))
    return arrays


def _build(nc, arrays):
    aps = {}
    for name in _INS:
        a = arrays[f"in_{name}_dram"]
        aps[name] = nc.dram_tensor(f"in_{name}_dram", a.shape, mybir.dt.from_np(a.dtype),
                                   kind="ExternalInput").ap()
    out = nc.dram_tensor("out_0_dram", (BATCH, P, P), F32, kind="ExternalOutput").ap()
    cross_attention_ffn_kernel(nc, aps, out)


def kernel(**inputs):
    import concourse.bacc as _bacc
    from concourse.bass_utils import run_bass_kernel_spmd as _run

    nc = _bacc.Bacc("TRN2", target_bir_lowering=False, num_devices=1)
    arrays = _arrays(inputs)
    _build(nc, arrays)
    r = _run(nc, [arrays], core_ids=[0])
    return r.results[0]["out_0_dram"]
```

```python
from contextlib import ExitStack

import numpy as np

import concourse.bass as bass
import concourse.mybir as mybir

F32 = mybir.dt.float32
F32R = mybir.dt.float32r
BF16 = mybir.dt.bfloat16
ALU = mybir.AluOpType
ACT = mybir.ActivationFunctionType
AX = mybir.AxisListType
ds = bass.ds

P = 128
BATCH = 64
KEYS = 77
CDIM = 96
HEAD = 64
GT = 4
GROUPS = BATCH // GT
GCOLS = GT * KEYS
EPS = 1e-5
MAGIC = 1.5 * 2.0 ** 23
BANK = 512


class Counter:

    def __init__(self, sem, credit=0):
        self.sem, self.credit, self.base = sem, credit, credit

    def claim(self, total):
        c = Claim(self.sem, self.base, self.credit, total)
        self.base += total
        return c


class Claim:
    def __init__(self, sem, base, credit, total):
        self.sem, self.base, self.credit, self.total = sem, base, credit, total

    def at(self, n):
        return n + self.base

    def free(self, n):
        return n + 1 + (self.base - self.credit)


def for_groups(eng, body, peel=1):
    with eng.Fori(0, GROUPS // 2 - peel) as i:
        body(2 * i, 0, 2 * peel)
        body(2 * i + 1, 1, 2 * peel)
    for left in range(2 * peel - 1, -1, -1):
        body(GROUPS - 1 - left, 1 - left % 2, left)


def three_passes(eng, out, lhs, rhs, start=True, stop=True):
    eng.matmul(out, lhs[0], rhs[0], start=start, stop=False)
    eng.matmul(out, lhs[0], rhs[1], start=False, stop=False)
    return eng.matmul(out, lhs[1], rhs[0], start=False, stop=stop)


def bc(ap, n):
    return ap.unsqueeze(2).broadcast_to([ap.shape[0], ap.shape[1], n])


class Core:

    def __init__(self, nc, ctx, ins, out):
        self.nc, self.ctx, self.ins, self.out = nc, ctx, ins, out
        self.x = self.sb(ctx, "x", [P, BATCH, P], F32)
        self.ident = self.sb(ctx, "ident", [P, P], F32)
        self.ident_bf = self.sb(ctx, "ident_bf", [P, P], BF16)
        self.neg_half = self.sb(ctx, "neg_half", [P, GT], F32)
        self.eps = self.sb(ctx, "eps", [P, GT], F32)
        self.stats = self.sb(ctx, "ln_stats", [P, GT, 6], F32)
        self.mean_var = self.sb(ctx, "ln_mean_var", [P, GT, 2], F32)
        self.ln_var = self.sb(ctx, "ln_var", [P, GT], F32)
        self.rstd = self.sb(ctx, "ln_rstd", [P, GT], F32)
        self.rstd2 = self.sb(ctx, "ln_rstd2", [P, GT], F32)
        self.z = self.sb(ctx, "z", [P, GT, P], F32)
        self.ps_s = ctx.enter_context(nc.psum_tensor("ps_s", [P, 3, BANK], F32))
        self.ps_p = ctx.enter_context(nc.psum_tensor("ps_p", [P, 2, BANK], F32))
        self.ps_t = ctx.enter_context(nc.psum_tensor("ps_t", [P, 2, BANK], F32))
        self.ps_o = ctx.enter_context(nc.psum_tensor("ps_o", [P, BANK], F32))
        self.counters = {}
        self.credits = []

    def sb(self, ctx, name, shape, dt):
        return ctx.enter_context(self.nc.sbuf_tensor(name, shape, dt))

    def bank(self, n):
        if n < 3:
            return self.ps_s[:, n, :]
        if n < 5:
            return self.ps_p[:, n - 3, :]
        return self.ps_t[:, n - 5, :] if n < 7 else self.ps_o[:, :]

    def claim(self, name, total, credit=0, owner=None):
        if name not in self.counters:
            sem = self.ctx.enter_context(self.nc.semaphore(name))
            self.counters[name] = Counter(sem, credit)
            if credit:
                self.credits.append((owner, sem, credit))
        return self.counters[name].claim(total)

    def grant(self, owner, eng):
        for who, sem, credit in self.credits:
            if who == owner:
                eng.sem_inc(sem, credit)


class Chain:

    def __init__(self, claim):
        self.claim, self.n = claim, 0

    def step(self, eng, ins):
        ins.then_inc(self.claim.sem, 1)
        self.n += 1
        eng.wait_ge(self.claim.sem, self.claim.at(self.n))


class LayerNorm:

    def __init__(self, core, twice=False, bias=None, dest=None, once=None):
        self.dest = dest or (lambda g, k: core.z[:, k, :])
        self.core, self.twice, self.bias = core, twice, bias
        self.stats_ready = core.claim("stats_ready", GT * GROUPS)
        self.stats_seen = core.claim("stats_seen", GROUPS)
        self.aggr_ready = core.claim("aggr_ready", GT * GROUPS)
        self.once = once
        self.pool_steps = 2 if not twice else 7 if once is None else 6
        if once is not None:
            self.once_ready = core.claim("once_ready", GT * GROUPS)
            self.once_added = core.claim("once_added", GROUPS)
            self.pool_seen = core.claim("pool_seen", GROUPS)
        self.rstd_step = core.claim("rstd_step", self.pool_steps * GROUPS)
        self.z_ready = core.claim("z_ready", GT * GROUPS)
        self.bias_added = core.claim("bias_added", GROUPS) if bias is not None else None

    def vector_stats(self, eng, g):
        c = self.core
        for k in range(GT):
            eng.bn_stats(c.stats[:, k, :], c.x[:, ds(GT * g + k, 1), :].rearrange("p a d -> p (a d)"))\
               .then_inc(self.stats_ready.sem, 1)
        eng.wait_ge(self.stats_ready.sem, self.stats_ready.at(GT * g + GT))
        eng.sem_inc(self.stats_seen.sem, 1)
        for k in range(GT):
            eng.bn_aggr(c.mean_var[:, k, :], c.stats[:, k, :]).then_inc(self.aggr_ready.sem, 1)

    def pool(self, eng, g):
        c, n = self.core, 0

        def step(ins):
            nonlocal n
            ins.then_inc(self.rstd_step.sem, 1)
            n += 1
            eng.wait_ge(self.rstd_step.sem, self.rstd_step.at(self.pool_steps * g + n))

        eng.wait_ge(self.aggr_ready.sem, self.aggr_ready.at(GT * g + GT))
        step(eng.tensor_tensor(c.ln_var[:, :], c.mean_var[:, :, 1], c.eps[:, :], ALU.add))
        step(eng.tensor_tensor(c.rstd[:, :], c.ln_var[:, :], c.neg_half[:, :], ALU.pow))
        if self.twice:
            step(eng.tensor_tensor(c.ln_var[:, :], c.mean_var[:, :, 1], c.rstd[:, :], ALU.mult))
            step(eng.tensor_tensor(c.ln_var[:, :], c.ln_var[:, :], c.rstd[:, :], ALU.mult))
            step(eng.tensor_tensor(c.ln_var[:, :], c.ln_var[:, :], c.eps[:, :], ALU.add))
            step(eng.tensor_tensor(c.rstd2[:, :], c.ln_var[:, :], c.neg_half[:, :], ALU.pow))
            if self.once is None:
                step(eng.tensor_tensor(c.rstd[:, :], c.rstd[:, :], c.rstd2[:, :], ALU.mult))

    def pool_bias(self, eng, g):
        if self.bias is None:
            return
        c = self.core
        eng.wait_ge(self.z_ready.sem, self.z_ready.at(GT * g + GT))
        xg = c.x[:, ds(GT * g, GT), :]
        if self.once is not None:
            eng.tensor_tensor(xg, xg, self.once[:, :, :], ALU.add).then_inc(self.once_added.sem, 1)
            eng.wait_ge(self.once_added.sem, self.once_added.at(g + 1))
            eng.sem_inc(self.pool_seen.sem, 1)
        eng.tensor_tensor(xg, xg, self.bias[:, :].unsqueeze(1).broadcast_to([P, GT, P]), ALU.add)\
           .then_inc(self.bias_added.sem, 1)

    def vector_z(self, eng, g):
        c = self.core
        eng.wait_ge(self.rstd_step.sem, self.rstd_step.at(self.pool_steps * g + self.pool_steps))
        for k in range(GT):
            xk = c.x[:, ds(GT * g + k, 1), :].rearrange("p a d -> p (a d)")
            if self.once is None:
                eng.tensor_scalar(self.dest(g, k), xk, c.mean_var[:, k, 0:1], c.rstd[:, k:k + 1],
                                  ALU.subtract, ALU.mult).then_inc(self.z_ready.sem, 1)
                continue
            if k == 0 and not (isinstance(g, int) and g == 0):
                eng.wait_ge(self.once_added.sem, self.once_added.at(g))
            eng.tensor_scalar(self.once[:, k, :], xk, c.mean_var[:, k, 0:1], c.rstd[:, k:k + 1],
                              ALU.subtract, ALU.mult).then_inc(self.once_ready.sem, 1)
        if self.once is not None:
            for k in range(GT):
                eng.wait_ge(self.once_ready.sem, self.once_ready.at(GT * g + k + 1))
                eng.tensor_scalar(self.dest(g, k), self.once[:, k, :], c.rstd2[:, k:k + 1], None, ALU.mult)\
                   .then_inc(self.z_ready.sem, 1)


class BatchStats:

    PARTS = 4
    TILES = BATCH // PARTS

    def __init__(self, core, ctx, name):
        self.core = core
        self.stats = core.sb(ctx, name + "_stats", [P, BATCH, 6], F32)
        self.mv = core.sb(ctx, name + "_mean_var", [P, BATCH, 2], F32)
        self.rstd = core.sb(ctx, name + "_rstd", [P, BATCH], F32)
        self.stats_ready = core.claim("stats_ready", BATCH)
        self.stats_seen = core.claim("stats_seen", self.PARTS)
        self.aggr_ready = core.claim("aggr_ready", BATCH)
        self.std_ready = core.claim("std_ready", self.PARTS)
        self.rstd_ready = core.claim("rstd_step", self.PARTS)

    def mean_of(self, b):
        return self.mv[:, ds(b, 1), :].rearrange("p a s -> p (a s)")[:, 0:1]

    def rstd_of(self, b):
        return self.rstd[:, ds(b, 1)]

    def vector(self, eng):
        row = lambda t, b: t[:, ds(b, 1), :].rearrange("p a d -> p (a d)")

        def invert(q):
            part = self.rstd[:, self.TILES * q:self.TILES * (q + 1)]
            eng.wait_ge(self.std_ready.sem, self.std_ready.at(q + 1))
            eng.reciprocal(part, part).then_inc(self.rstd_ready.sem, 1)

        for q in range(self.PARTS):
            with eng.Fori(self.TILES // GT * q, self.TILES // GT * (q + 1)) as g:
                for k in range(GT):
                    eng.bn_stats(row(self.stats, GT * g + k), row(self.core.x, GT * g + k))\
                       .then_inc(self.stats_ready.sem, 1)
            eng.wait_ge(self.stats_ready.sem, self.stats_ready.at(self.TILES * (q + 1)))
            eng.sem_inc(self.stats_seen.sem, 1)
            for b in range(self.TILES * q, self.TILES * (q + 1)):
                eng.bn_aggr(self.mv[:, b, :], self.stats[:, b, :]).then_inc(self.aggr_ready.sem, 1)
            if q > 0:
                invert(q - 1)
        invert(self.PARTS - 1)
        self.wait(eng)

    def scalar(self, eng):
        for q in range(self.PARTS):
            part = slice(self.TILES * q, self.TILES * (q + 1))
            eng.wait_ge(self.aggr_ready.sem, self.aggr_ready.at(self.TILES * (q + 1)))
            eng.activation(self.rstd[:, part], self.mv[:, part, 1], ACT.Sqrt, bias=self.core.eps[:, 0:1])\
               .then_inc(self.std_ready.sem, 1)

    def wait(self, eng, part=PARTS - 1):
        eng.wait_ge(self.rstd_ready.sem, self.rstd_ready.at(part + 1))


class SavedLayerNorm(LayerNorm):

    def __init__(self, core, batch, bias=None, dest=None):
        self.core, self.batch, self.bias, self.once = core, batch, bias, None
        self.dest = dest or (lambda g, k: core.z[:, k, :])
        self.z_ready = core.claim("z_ready", GT * GROUPS)
        self.bias_added = core.claim("bias_added", GROUPS) if bias is not None else None

    def vector_stats(self, eng, g):
        pass

    def pool(self, eng, g):
        pass

    def vector_z(self, eng, g):
        for k in range(GT):
            b = GT * g + k
            eng.tensor_scalar(self.dest(g, k), self.core.x[:, ds(b, 1), :].rearrange("p a d -> p (a d)"),
                              self.batch.mean_of(b), self.batch.rstd_of(b), ALU.subtract, ALU.mult)\
               .then_inc(self.z_ready.sem, 1)


class Phase:

    def sync(self, eng):
        pass

    def gpsimd(self, eng):
        pass

    def scalar(self, eng):
        pass

    def vector(self, eng):
        pass

    def tensor(self, eng):
        pass


class Setup(Phase):

    PER = 6
    BANKS = -(-BATCH // PER)
    RING = 4

    def __init__(self, core):
        self.core = core
        ctx = core.ctx
        self.scope = ExitStack()
        core.ct_scope = ExitStack()
        ctx.callback(core.ct_scope.close)
        core.ct_hi = core.sb(core.ct_scope, "ct_hi", [CDIM, BATCH * KEYS], F32R)
        core.ct_lo = core.sb(core.ct_scope, "ct_lo", [CDIM, BATCH * KEYS], F32R)
        self.rows = core.sb(self.scope, "ctx_rows", [KEYS, BATCH, CDIM], F32)
        self.x_loaded = core.claim("x_loaded", 16 * 8)
        self.ctx_loaded = core.claim("ctx_loaded", 16 * 4)
        self.const_ready = core.claim("const_ready", 5)
        self.ctx_turned = core.claim("turned", self.BANKS)
        self.hi_done = core.claim("split_hi", self.BANKS)
        self.lo_done = core.claim("split_lo", self.BANKS)
        self.done = core.claim("phase_done", 1)
        self.scope.close()

    def cols(self, n):
        return range(self.PER * n, min(BATCH, self.PER * n + self.PER))

    def sync(self, eng):
        c = self.core
        for q in range(4):
            b = slice(16 * q, 16 * q + 16)
            eng.dma_start(self.rows[:, b, :], c.ins["ctx_768"][b].rearrange("b k c -> k b c"))\
               .then_inc(self.ctx_loaded.sem, 16)

    def load_x(self, eng):
        c = self.core
        for q in range(8):
            b = slice(8 * q, 8 * q + 8)
            eng.dma_start(c.x[:, b, :], c.ins["x"][b].rearrange("b t d -> t b d"))\
               .then_inc(self.x_loaded.sem, 16)

    def wait_x(self, eng):
        eng.wait_ge(self.x_loaded.sem, self.x_loaded.at(16 * 8))

    def gpsimd(self, eng):
        c = self.core
        eng.memset(c.ident[:, :], 0.0).then_inc(self.const_ready.sem, 1)
        eng.wait_ge(self.const_ready.sem, self.const_ready.at(1))
        eng.affine_select(out=c.ident[:, :], in_=c.ident[:, :], compare_op=ALU.not_equal, fill=1.0,
                          base=0, pattern=[[-1, P]], channel_multiplier=1)\
           .then_inc(self.const_ready.sem, 1)
        eng.wait_ge(self.const_ready.sem, self.const_ready.at(2))
        eng.tensor_copy(c.ident_bf[:, :], c.ident[:, :]).then_inc(self.const_ready.sem, 1)
        eng.memset(c.neg_half[:, :], -0.5).then_inc(self.const_ready.sem, 1)
        eng.memset(c.eps[:, :], EPS).then_inc(self.const_ready.sem, 1)
        eng.wait_ge(self.const_ready.sem, self.const_ready.at(5))

    def tensor(self, eng):
        c = self.core
        eng.wait_ge(self.const_ready.sem, self.const_ready.at(3))
        for n in range(self.BANKS):
            eng.wait_ge(self.ctx_loaded.sem, self.ctx_loaded.at(16 * 4))
            if n >= self.RING:
                eng.wait_ge(self.lo_done.sem, self.lo_done.at(n - self.RING + 1))
            for j, b in enumerate(self.cols(n)):
                mm = eng.transpose(c.bank(n % self.RING)[0:CDIM, j * KEYS:(j + 1) * KEYS],
                                   self.rows[:, b, :], c.ident[0:KEYS, 0:KEYS])
            mm.then_inc(self.ctx_turned.sem, 1)

    def scalar(self, eng):
        c = self.core
        for n in range(self.BANKS):
            w = len(self.cols(n)) * KEYS
            s = slice(self.PER * n * KEYS, self.PER * n * KEYS + w)
            eng.wait_ge(self.ctx_turned.sem, self.ctx_turned.at(n + 1))
            eng.activation(c.ct_hi[:, s], c.bank(n % self.RING)[0:CDIM, 0:w], ACT.Copy)\
               .then_inc(self.hi_done.sem, 1)

    def vector(self, eng):
        c = self.core
        for n in range(self.BANKS):
            w = len(self.cols(n)) * KEYS
            s = slice(self.PER * n * KEYS, self.PER * n * KEYS + w)
            eng.wait_ge(self.hi_done.sem, self.hi_done.at(n + 1))
            eng.tensor_tensor(c.ct_lo[:, s], c.bank(n % self.RING)[0:CDIM, 0:w], c.ct_hi[:, s].bitcast(F32),
                              ALU.subtract).then_inc(self.lo_done.sem, 1)
        eng.wait_ge(self.const_ready.sem, self.const_ready.at(5))
        eng.wait_ge(self.lo_done.sem, self.lo_done.at(self.BANKS))
        eng.sem_inc(self.done.sem, 1)


class CrossAttention(Phase):

    def __init__(self, core, name, heads, wq, wk, wv, wo, bo, before, twice=False,
                 gamma=None, beta=None, mask=None, setup=None):
        self.core, self.name, self.heads, self.before = core, name, heads, before
        self.setup = setup
        self.src = dict(wq=wq, wk=wk, wv=wv, wo=wo, bo=bo, gamma=gamma, beta=beta, mask=mask)
        self.masked, self.affine = mask is not None, gamma is not None
        H = heads
        self.rows = H * KEYS
        self.chunks = -(-self.rows // P)
        self.uses = -(-self.chunks // GT)
        self.banks = [6, 6, 4] if H == 16 else [4, 4]
        self.NB = len(self.banks)
        self.pairs = H // 2
        self.half = H // 2
        self.cyc = 2 * GT * self.uses + 1
        sb, ctx = core.sb, ExitStack()
        self.scope = ctx
        n = lambda s: f"{name}_{s}"
        self.mt_hi = sb(ctx, n("mt_hi"), [CDIM, H, P], F32R)
        self.mt_lo = sb(ctx, n("mt_lo"), [CDIM, H, P], F32R)
        self.vo_hi = sb(ctx, n("vo_hi"), [CDIM, H, P], F32R)
        self.vo_lo = sb(ctx, n("vo_lo"), [CDIM, H, P], F32R)
        self.bias = sb(ctx, n("bias"), [P, P], F32)
        if self.affine:
            self.gb = sb(ctx, n("gamma_beta"), [P, 2], F32)
        if self.masked:
            self.mask_u8 = sb(ctx, n("mask_u8"), [P, KEYS], mybir.dt.uint8)
            self.mask_add = sb(ctx, n("mask_add"), [P, KEYS], F32)
            self.some_key = sb(ctx, n("some_key"), [P, 2], F32)
        self.zt = sb(ctx, n("zt"), [P, 2, GT * P], F32)
        self.e = sb(ctx, n("e"), [P, 2, self.rows], F32)
        self.pt = sb(ctx, n("pt"), [P, self.chunks, P], F32)
        self.val = sb(ctx, n("val"), [P, self.chunks, P], F32)
        self.mx = sb(ctx, n("mx"), [P, H], F32)
        self.sm = sb(ctx, n("sm"), [P, H], F32)
        self.rs = sb(ctx, n("rs"), [P, H], F32)
        with ExitStack() as prep:
            self.wq = sb(prep, n("wq"), [P, H * HEAD], F32)
            self.wk = sb(prep, n("wk"), [CDIM, H * HEAD], F32)
            self.wv = sb(prep, n("wv"), [CDIM, H * HEAD], F32)
            self.wo = sb(prep, n("wo"), [P, self.pairs, P], F32)
            self.wt = sb(prep, n("wt"), [P, 2, P + 2 * CDIM], F32)
        self.keys = sb(ctx, n("keys"), [P, 2, GT, H, KEYS], F32)
        self.vals_t = sb(ctx, n("vals_t"), [P, 2, GT, H, KEYS], F32)
        ctx.close()

        T = BATCH
        cl = core.claim
        self.loads = 4 + 2 * self.affine + self.masked
        self.w_loaded = cl("w_loaded", 16 * self.loads)
        self.bias_loaded = cl("bias_loaded", 16)
        self.w_turned = cl("turned", self.pairs)
        self.wt_ready = cl("wt_ready", self.pairs)
        self.prod_done = cl("prod_done", self.pairs)
        self.hi_done = cl("split_hi", 4 * self.pairs)
        self.lo_done = cl("split_lo", 4 * self.pairs)
        self.mask_ready = cl("mask_ready", 5) if self.masked else None
        self.ln = LayerNorm(core, twice, self.bias)
        self.proj_done = cl("proj_done", 2 * H * GROUPS)
        self.proj_copied = cl("proj_copied", 2 * H * GROUPS, credit=2, owner="scalar")
        tn = 1 + self.uses + GROUPS * self.cyc - self.uses - 1
        self.t_done = cl("t_done", tn)
        self.t_copied = cl("t_copied", tn, credit=2, owner="scalar")
        self.scores_ready = cl("scores_ready", self.NB * T)
        self.max_ready = cl("max_ready", self.NB * T)
        self.shifted = cl("shifted", self.NB * T)
        self.mask_added = cl("mask_added", self.NB * T) if self.masked else None
        self.exp_ready = cl("exp_ready", T)
        self.norm_steps = 3 if self.masked else 2
        self.norm_step = cl("norm_step", self.norm_steps * T)
        self.probs_ready = cl("probs_ready", T)
        self.sum_done = cl("sum_done", T)
        self.res_done = cl("res_done", T, credit=2, owner="vector")
        self.done = cl("phase_done", 1)

    def head_span(self, b):
        h0 = sum(self.banks[:b])
        return h0, self.banks[b]

    def proj_use(self, g, k, j):
        return g * (2 * self.heads) + k * self.half + j

    def head_of(self, k, j):
        return (k % 2) * self.half + j

    def spread(self, k):
        u, n = self.uses, self.half
        m = n if k == GT - 1 else n - u
        return range(u), range(u, m), range(m, n)

    def t_use(self, g, k, what, j, last):
        n = 1 + self.uses + g * self.cyc + 2 * self.uses * k + (1 if k > 1 and not last else 0)
        return n + (self.uses if what == 1 else 2 * self.uses if what == 2 else 0) + j

    def t_slot(self, par, k, what, j, last):
        return self.t_use(par, k, what, j, last) % 2

    def sync(self, eng):
        s = self.src
        if not self.setup:
            eng.wait_ge(self.before.sem, self.before.at(1))
        sem = self.w_loaded.sem
        for dst, src in ((self.wq[:, :], s["wq"]), (self.wk[:, :], s["wk"]), (self.wv[:, :], s["wv"]),
                         (self.wo[:, :, :], s["wo"].rearrange("(p r) d -> r p d", r=P))):
            eng.dma_start(dst, src).then_inc(sem, 16)
        with self.core.nc.allow_non_contiguous_dma("single columns"):
            if self.affine:
                eng.dma_start(self.gb[:, 0:1], s["gamma"].unsqueeze(1)).then_inc(sem, 16)
                eng.dma_start(self.gb[:, 1:2], s["beta"].unsqueeze(1)).then_inc(sem, 16)
            if self.masked:
                eng.dma_start(self.mask_u8[:, :], s["mask"]).then_inc(sem, 16)
            eng.dma_start(self.bias[:, :], s["bo"].partition_broadcast(P)).then_inc(self.bias_loaded.sem, 16)
        if self.setup:
            self.setup.load_x(eng)

    def products_bank(self, p, s):
        return (self.core.ps_s if p % 2 == 0 else self.core.ps_p)[0:CDIM, s, :]

    def first_bank(self, u):
        return self.core.bank(u % 5)[:, 0:GCOLS]

    def project_first(self, eng, k, j):
        c, u, h = self.core, self.proj_use(0, k, j), self.head_of(k, j)
        hi, lo = (self.vo_hi, self.vo_lo) if k >= 2 else (self.mt_hi, self.mt_lo)
        if u >= 5:
            eng.wait_ge(self.proj_copied.sem, self.proj_copied.at(u - 4))
        three_passes(eng, self.first_bank(u), [w[:, h, :] for w in (hi, lo)],
                     [q[:, 0:GCOLS] for q in (c.ct_hi, c.ct_lo)]).then_inc(self.proj_done.sem, 1)

    def project(self, eng, g, k, j):
        c = self.core
        hi, lo = (self.vo_hi, self.vo_lo) if k >= 2 else (self.mt_hi, self.mt_lo)
        cols = ds(GCOLS * g, GCOLS)
        h, slot = self.head_of(k, j), self.proj_use(0, k, j) % 2
        eng.wait_ge(self.proj_copied.sem, self.proj_copied.free(self.proj_use(g, k, j)))
        three_passes(eng, c.ps_p[:, slot, 0:GCOLS], [w[:, h, :] for w in (hi, lo)],
                     [q[:, cols] for q in (c.ct_hi, c.ct_lo)]).then_inc(self.proj_done.sem, 1)

    def turn_z(self, eng, g, u, slot):
        c = self.core
        eng.wait_ge(self.ln.z_ready.sem, self.ln.z_ready.at(GT * g + GT))
        eng.wait_ge(self.t_copied.sem, self.t_copied.free(u))
        for k in range(GT):
            mm = eng.transpose(c.ps_t[:, slot, k * P:(k + 1) * P], c.z[:, k, :], c.ident[:, :])
        mm.then_inc(self.t_done.sem, 1)

    def turn_chunks(self, eng, j, src, use, slot):
        c = self.core
        eng.wait_ge(self.t_copied.sem, self.t_copied.free(use))
        for i in range(GT * j, min(GT * j + GT, self.chunks)):
            w = min(P, self.rows - P * i)
            mm = eng.transpose(c.ps_t[0:w, slot, (i % GT) * P:(i % GT + 1) * P],
                               src[:, P * i:P * i + w], c.ident[:, :])
        mm.then_inc(self.t_done.sem, 1)

    def scores(self, eng, t, zt, keys, first=False):
        c = self.core
        for b in range(self.NB):
            h0, nh = self.head_span(b)
            if not first:
                eng.wait_ge(self.shifted.sem, self.shifted.at(self.NB * (t - 1) + b + 1))
            o = c.ps_s[:, b, 0:nh * KEYS]
            eng.matmul(o, zt, keys[:, h0:h0 + nh, :], start=True, stop=True)\
               .then_inc(self.scores_ready.sem, 1)

    def weighted_sum(self, eng, t, k, prob_use):
        c = self.core
        eng.wait_ge(self.res_done.sem, self.res_done.at(t))
        for i in range(self.chunks):
            w = min(P, self.rows - P * i)
            if i % GT == 0:
                eng.wait_ge(self.t_copied.sem, self.t_copied.at(prob_use(i // GT) + 1))
            mm = eng.matmul(c.ps_o[:, (k % 2) * P:(k % 2 + 1) * P], self.pt[0:w, i, :],
                            self.val[0:w, i, :], start=(i == 0), stop=(i == self.chunks - 1))
        mm.then_inc(self.sum_done.sem, 1)

    def tensor(self, eng):
        c, H = self.core, self.heads
        eng.wait_ge(self.before.sem, self.before.at(1))
        eng.wait_ge(self.w_loaded.sem, self.w_loaded.at(16 * self.loads))

        def turn_weights(p):
            cols = slice(P * p, P * p + P)
            if p >= 2:
                eng.wait_ge(self.wt_ready.sem, self.wt_ready.at(p - 1))
            o = c.ps_t[:, p % 2, :]
            eng.transpose(o[:, 0:P], self.wq[:, cols], c.ident[:, :])
            eng.transpose(o[:, P:P + CDIM], self.wk[:, cols], c.ident[0:CDIM, 0:CDIM])
            eng.transpose(o[:, P + CDIM:P + 2 * CDIM], self.wv[:, cols], c.ident[0:CDIM, 0:CDIM])\
               .then_inc(self.w_turned.sem, 1)

        def products(p):
            eng.wait_ge(self.wt_ready.sem, self.wt_ready.at(p + 1))
            if p >= 2:
                eng.wait_ge(self.lo_done.sem, self.lo_done.at(4 * (p - 1)))
            wt = self.wt[:, p % 2, :]
            for s in range(2):
                r = slice(HEAD * s, HEAD * s + HEAD)
                o = self.products_bank(p, s)
                eng.matmul(o[:, 0:P], wt[r, P:P + CDIM], wt[r, 0:P], start=True, stop=True)
                mm = eng.matmul(o[:, P:2 * P], wt[r, P + CDIM:P + 2 * CDIM], self.wo[r, p, :],
                                start=True, stop=True)
            mm.then_inc(self.prod_done.sem, 1)

        turn_weights(0)
        for p in range(self.pairs):
            if p + 1 < self.pairs:
                turn_weights(p + 1)
            products(p)
        eng.wait_ge(self.lo_done.sem, self.lo_done.at(4 * self.pairs))
        eng.wait_ge(self.hi_done.sem, self.hi_done.at(4 * self.pairs))

        for k in range(GT):
            for j in range(self.half):
                self.project_first(eng, k, j)
        self.turn_z(eng, 0, 0, 0)
        eng.wait_ge(self.t_copied.sem, self.t_copied.at(1))
        eng.wait_ge(self.proj_copied.sem, self.proj_copied.at(2 * H))
        self.scores(eng, 0, self.zt[:, 0, 0:P], self.keys[:, 0, 0], first=True)
        flat = lambda par, k: self.vals_t[:, par, k].rearrange("p h k -> p (h k)")
        for j in range(self.uses):
            self.turn_chunks(eng, j, flat(0, 0), 1 + j, (1 + j) % 2)
        self.scores(eng, 1, self.zt[:, 0, P:2 * P], self.keys[:, 0, 1])

        def body(g, par, left):
            last = left == 0
            for k in range(GT):
                t, n1, n2 = GT * g + k, (k + 1) % GT, (k + 2) % GT
                par1, par2 = par if n1 else 1 - par, par if n2 == k + 2 else 1 - par
                early, middle, late = [() if last else part for part in self.spread(k)]
                eng.wait_ge(self.probs_ready.sem, self.probs_ready.at(t + 1))
                for j in range(self.uses):
                    self.turn_chunks(eng, j, self.e[:, k % 2, :], self.t_use(g, k, 0, j, last),
                                     self.t_slot(par, k, 0, j, last))
                    if not last:
                        self.project(eng, g + 1, k, early[j])
                if not (last and k >= 2):
                    if k == 2:
                        eng.wait_ge(self.proj_copied.sem,
                                    self.proj_copied.at(self.proj_use(g + 1, 1, self.half - 1) + 1))
                        eng.wait_ge(self.t_copied.sem, self.t_copied.at(self.t_use(g, 1, 2, 0, last) + 1))
                    self.scores(eng, t + 2, self.zt[:, par2, n2 * P:(n2 + 1) * P], self.keys[:, par2, n2])
                for j in middle:
                    self.project(eng, g + 1, k, j)
                self.weighted_sum(eng, t, k, lambda j: self.t_use(g, k, 0, j, last))
                if not (last and k == GT - 1):
                    if n1 == 0:
                        eng.wait_ge(self.proj_copied.sem,
                                    self.proj_copied.at(self.proj_use(g + 1, k, self.half - 1) + 1))
                    for j in range(self.uses):
                        self.turn_chunks(eng, j, flat(par1, n1), self.t_use(g, k, 1, j, last),
                                         self.t_slot(par, k, 1, j, last))
                        if late:
                            self.project(eng, g + 1, k, late[j])
                if k == 1 and not last:
                    self.turn_z(eng, g + 1, self.t_use(g, k, 2, 0, last), self.t_slot(par, k, 2, 0, last))

        for_groups(eng, body)

    def copy_proj(self, eng, g, par, k, j, first=False):
        c = self.core
        dst = self.vals_t if k >= 2 else self.keys
        h, slot = self.head_of(k, j), self.proj_use(0, k, j) % 2
        eng.wait_ge(self.proj_done.sem, self.proj_done.at(self.proj_use(g, k, j) + 1))
        src = self.first_bank(self.proj_use(0, k, j)) if first else c.ps_p[:, slot, 0:GCOLS]
        eng.activation(dst[:, par, :, h, :], src.rearrange("p (b k) -> p b k", b=GT), ACT.Copy)\
           .then_inc(self.proj_copied.sem, 1)

    def copy_zt(self, eng, par, u, slot):
        c = self.core
        eng.wait_ge(self.t_done.sem, self.t_done.at(u + 1))
        if self.affine:
            eng.activation(self.zt[:, par, :], c.ps_t[:, slot, :], ACT.Identity,
                           scale=self.gb[:, 0:1], bias=self.gb[:, 1:2]).then_inc(self.t_copied.sem, 1)
        else:
            eng.activation(self.zt[:, par, :], c.ps_t[:, slot, :], ACT.Copy)\
               .then_inc(self.t_copied.sem, 1)

    def copy_chunks(self, eng, j, dst, use, slot):
        c = self.core
        i0, i1 = GT * j, min(GT * j + GT, self.chunks)
        full = min(i1, self.rows // P)
        eng.wait_ge(self.t_done.sem, self.t_done.at(use + 1))
        src = c.ps_t[:, slot, :].rearrange("p (i d) -> p i d", i=GT)
        if full > i0:
            mm = eng.activation(dst[:, i0:full, :], src[:, 0:full - i0, :], ACT.Copy)
        if full < i1:
            w = self.rows - P * full
            mm = eng.activation(dst[0:w, full, :], src[0:w, full - i0, :], ACT.Copy)
        mm.then_inc(self.t_copied.sem, 1)

    def exponentials(self, eng, t, par):
        eng.wait_ge(self.shifted.sem, self.shifted.at(self.NB * (t + 1)))
        eng.activation(self.e[:, par, :], self.e[:, par, :], ACT.Exp).then_inc(self.exp_ready.sem, 1)

    def scalar(self, eng):
        c, H = self.core, self.heads
        eng.wait_ge(self.before.sem, self.before.at(1))
        for p in range(self.pairs + 1):
            if p < self.pairs:
                eng.wait_ge(self.w_turned.sem, self.w_turned.at(p + 1))
                if p >= 2:
                    eng.wait_ge(self.prod_done.sem, self.prod_done.at(p - 1))
                eng.activation(self.wt[:, p % 2, :], c.ps_t[:, p % 2, 0:P + 2 * CDIM], ACT.Copy)\
                   .then_inc(self.wt_ready.sem, 1)
            if p >= 1:
                eng.wait_ge(self.prod_done.sem, self.prod_done.at(p))
                for s in range(2):
                    for w in range(2):
                        eng.activation((self.mt_hi, self.vo_hi)[w][:, 2 * (p - 1) + s, :],
                                       self.products_bank(p - 1, s)[:, w * P:(w + 1) * P], ACT.Copy,
                                       scale=(HEAD ** -0.5, 1.0)[w]).then_inc(self.hi_done.sem, 1)
        if self.affine:
            eng.wait_ge(self.w_loaded.sem, self.w_loaded.at(16 * self.loads))
        eng.wait_ge(self.prod_done.sem, self.prod_done.at(self.pairs))
        for k in range(GT):
            for j in range(self.half):
                self.copy_proj(eng, 0, 0, k, j, True)
        self.copy_zt(eng, 0, 0, 0)
        for j in range(self.uses):
            self.copy_chunks(eng, j, self.val, 1 + j, (1 + j) % 2)
        self.exponentials(eng, 0, 0)

        def body(g, par, left):
            last = left == 0
            for k in range(GT):
                t = GT * g + k
                more = not (last and k == GT - 1)
                early, middle, late = [() if last else part for part in self.spread(k)]
                if more and H == 8:
                    self.exponentials(eng, t + 1, (k + 1) % 2)
                for j in range(self.uses):
                    self.copy_chunks(eng, j, self.pt, self.t_use(g, k, 0, j, last),
                                     self.t_slot(par, k, 0, j, last))
                    if not last:
                        self.copy_proj(eng, g + 1, 1 - par, k, early[j])
                if more and H > 8:
                    self.exponentials(eng, t + 1, (k + 1) % 2)
                for j in middle:
                    self.copy_proj(eng, g + 1, 1 - par, k, j)
                if more:
                    for j in range(self.uses):
                        self.copy_chunks(eng, j, self.val, self.t_use(g, k, 1, j, last),
                                         self.t_slot(par, k, 1, j, last))
                        if late:
                            self.copy_proj(eng, g + 1, 1 - par, k, late[j])
                if k == 1 and not last:
                    self.copy_zt(eng, 1 - par, self.t_use(g, k, 2, 0, last),
                                 self.t_slot(par, k, 2, 0, last))

        for_groups(eng, body)

    def shift(self, eng, t, par):
        c = self.core
        by_head = lambda a, nh: a.rearrange("p (h k) -> p h k", h=nh)
        source = []
        for b in range(self.NB):
            h0, nh = self.head_span(b)
            bank = by_head(c.ps_s[:, b, 0:nh * KEYS], nh)
            dest = by_head(self.e[:, par, h0 * KEYS:(h0 + nh) * KEYS], nh)
            source.append((h0, nh, dest if self.masked else bank, dest))
            eng.wait_ge(self.scores_ready.sem, self.scores_ready.at(self.NB * t + b + 1))
            if self.masked:
                eng.tensor_tensor(dest, bank, self.mask_add[:, :].unsqueeze(1).broadcast_to([P, nh, KEYS]),
                                  ALU.add).then_inc(self.mask_added.sem, 1)
            else:
                eng.tensor_reduce(self.mx[:, h0:h0 + nh], bank, AX.X, ALU.max).then_inc(self.max_ready.sem, 1)
        if self.masked:
            for b, (h0, nh, src, _) in enumerate(source):
                eng.wait_ge(self.mask_added.sem, self.mask_added.at(self.NB * t + b + 1))
                eng.tensor_reduce(self.mx[:, h0:h0 + nh], src, AX.X, ALU.max).then_inc(self.max_ready.sem, 1)
        for b, (h0, nh, src, dest) in enumerate(source):
            eng.wait_ge(self.max_ready.sem, self.max_ready.at(self.NB * t + b + 1))
            eng.tensor_tensor(dest, src, bc(self.mx[:, h0:h0 + nh], KEYS), ALU.subtract)\
               .then_inc(self.shifted.sem, 1)

    def normalise(self, eng, t, par):
        H = self.heads
        e = self.e[:, par, :].rearrange("p (h k) -> p h k", h=H)
        st, n = self.norm_step, self.norm_steps
        eng.wait_ge(self.exp_ready.sem, self.exp_ready.at(t + 1))
        eng.tensor_reduce(self.sm[:, :], e, AX.X, ALU.add).then_inc(st.sem, 1)
        eng.wait_ge(st.sem, st.at(n * t + 1))
        eng.reciprocal(self.rs[:, :], self.sm[:, :]).then_inc(st.sem, 1)
        eng.wait_ge(st.sem, st.at(n * t + 2))
        if self.masked:
            eng.tensor_scalar(self.rs[:, :], self.rs[:, :], self.some_key[:, 1:2], None, ALU.mult)\
               .then_inc(st.sem, 1)
            eng.wait_ge(st.sem, st.at(n * t + 3))
        eng.tensor_tensor(e, e, bc(self.rs[:, :], KEYS), ALU.mult).then_inc(self.probs_ready.sem, 1)

    def residual(self, eng, t, k):
        c = self.core
        eng.wait_ge(self.sum_done.sem, self.sum_done.at(t + 1))
        xt = c.x[:, ds(t, 1), :].rearrange("p a d -> p (a d)")
        eng.tensor_tensor(xt, c.ps_o[:, (k % 2) * P:(k % 2 + 1) * P], xt, ALU.add)\
           .then_inc(self.res_done.sem, 1)

    def vector(self, eng):
        c = self.core
        eng.wait_ge(self.before.sem, self.before.at(1))
        eng.wait_ge(self.w_loaded.sem, self.w_loaded.at(16 * self.loads))
        if self.masked:
            m = self.mask_ready
            eng.tensor_scalar(self.mask_add[:, :], self.mask_u8[:, :], -1.0, 1e30, ALU.add, ALU.mult)\
               .then_inc(m.sem, 1)
            eng.tensor_reduce(self.some_key[:, 0:1], self.mask_u8[:, :], AX.X, ALU.add).then_inc(m.sem, 1)
            eng.wait_ge(m.sem, m.at(2))
            eng.reciprocal(self.some_key[:, 1:2], self.some_key[:, 0:1]).then_inc(m.sem, 1)
            eng.wait_ge(m.sem, m.at(3))
            eng.tensor_scalar(self.some_key[:, 1:2], self.some_key[:, 1:2], 0.0, 1.0, ALU.mult, ALU.add)\
               .then_inc(m.sem, 1)
            eng.wait_ge(m.sem, m.at(4))
            eng.sem_inc(m.sem, 1)
        if not self.setup:
            self.ln.vector_stats(eng, 0)
        for p in range(self.pairs):
            for s, w in [(s, w) for s in range(2) for w in range(2)]:
                eng.wait_ge(self.hi_done.sem, self.hi_done.at(4 * p + 2 * s + 2))
                h, l = ((self.mt_hi, self.mt_lo), (self.vo_hi, self.vo_lo))[w]
                eng.scalar_tensor_tensor(out=l[:, 2 * p + s, :],
                                         in0=self.products_bank(p, s)[:, w * P:(w + 1) * P],
                                         scalar=(HEAD ** -0.5, 1.0)[w],
                                         in1=h[:, 2 * p + s, :].bitcast(F32), op0=ALU.mult,
                                         op1=ALU.subtract).then_inc(self.lo_done.sem, 1)
        if self.setup:
            self.setup.wait_x(eng)
            self.ln.vector_stats(eng, 0)
        self.ln.vector_z(eng, 0)
        self.ln.vector_stats(eng, 1)
        self.shift(eng, 0, 0)
        self.shift(eng, 1, 1)
        self.normalise(eng, 0, 0)

        def body(g, par, left):
            last = left == 0
            for k in range(GT):
                t = GT * g + k
                more = not (last and k == GT - 1)
                if k == 0:
                    eng.wait_ge(self.ln.bias_added.sem, self.ln.bias_added.at(g + 1))
                if not last and k == 1:
                    self.ln.vector_z(eng, g + 1)
                if more:
                    self.normalise(eng, t + 1, (k + 1) % 2)
                if not (last and k >= 2):
                    self.shift(eng, t + 2, k % 2)
                self.residual(eng, t, k)
                if left > 1 and k == GT - 1:
                    self.ln.vector_stats(eng, g + 2)

        for_groups(eng, body)
        eng.wait_ge(self.res_done.sem, self.res_done.at(BATCH))
        eng.sem_inc(self.done.sem, 1)

    def gpsimd(self, eng):
        eng.wait_ge(self.before.sem, self.before.at(1))
        self.ln.pool(eng, 0)
        eng.wait_ge(self.bias_loaded.sem, self.bias_loaded.at(16))
        self.ln.pool_bias(eng, 0)
        with eng.Fori(1, GROUPS) as g:
            self.ln.pool(eng, g)
            self.ln.pool_bias(eng, g)


class Hidden(Phase):

    RING = 4

    def setup(self, before, widths, func, ln, gated=False):
        core = self.core
        self.before, self.widths, self.func, self.gated = before, widths, func, gated
        self.C = len(widths)
        cl = core.claim
        self.ln = ln
        G, C = GROUPS, self.C
        self.zt_turned = cl("zt_turned", G)
        self.zt_copied = cl("zt_copied", G)
        self.zt_hi_done = cl("zt_hi_done", G)
        self.zt_split = cl("zt_split", G)
        self.hid_done = cl("hid_done", C * G)
        self.act_done = cl("act_done", C * G)
        self.out_done = cl("out_done", G)
        self.added = cl("added", G, credit=2, owner="vector")
        self.done = cl("phase_done", 1)

    def buffers(self, ctx, n):
        sb = self.core.sb
        self.zt = sb(ctx, n + "zt", [P, GT * P], F32)
        self.zt_parts = [sb(ctx, f"{n}zt{h}", [P, 2, GT * P], F32R) for h in ("hi", "lo")]
        self.hid = sb(ctx, n + "hid", [P, 2, self.C, GT * P], F32)

    def hbank(self, c):
        return self.core.bank(c % self.RING)

    def obank(self, par):
        return self.core.bank(6 + par)

    def turn_z(self, eng, g, par):
        c = self.core
        eng.wait_ge(self.ln.z_ready.sem, self.ln.z_ready.at(GT * g + GT))
        for k in range(GT):
            mm = eng.transpose(c.bank(5)[:, k * P:(k + 1) * P], c.z[:, k, :], c.ident[:, :])
        mm.then_inc(self.zt_turned.sem, 1)

    def hidden(self, eng, g, par, first=False):
        eng.wait_ge(self.zt_split.sem, self.zt_split.at(g + 1))
        z = [p[:, par, :] for p in self.zt_parts]
        for c in range(self.C):
            if c >= self.RING:
                eng.wait_ge(self.act_done.sem, self.act_done.at(self.C * g + c - self.RING + 1))
            elif not first:
                older = max(j for j in range(self.C) if j % self.RING == c)
                eng.wait_ge(self.act_done.sem, self.act_done.at(self.C * (g - 1) + older + 1))
            w = self.widths[c]
            three_passes(eng, self.hbank(c)[0:w, :],
                         [q[:, c * P:c * P + w] for q in self.w1], z).then_inc(self.hid_done.sem, 1)

    def wait_hidden(self, eng, g):
        eng.wait_ge(self.act_done.sem, self.act_done.at(self.C * (g + 1)))

    def output(self, eng, g, par, tiles=range(GT)):
        if 0 in tiles:
            self.wait_hidden(eng, g)
            eng.wait_ge(self.added.sem, self.added.free(g))
        for k in tiles:
            o = self.obank(par)[:, k * P:(k + 1) * P]
            for c in range(self.C):
                w = self.widths[c]
                mm = eng.matmul(o, self.hid[0:w, par, c, k * P:(k + 1) * P], self.w2[0:w, c, :],
                                start=c == 0, stop=c == self.C - 1 and not self.gated)
            if self.gated:
                mm = self.gated_bias(eng, g, par, k, o)
        if GT - 1 in tiles:
            mm.then_inc(self.out_done.sem, 1)

    def turn_gates(self, eng, g, par, which):
        pass

    def tensor_walk(self, eng):
        self.turn_z(eng, 0, 0)
        self.hidden(eng, 0, 0, True)
        self.turn_gates(eng, 0, 0, range(5))
        self.turn_z(eng, 1, 1)

        def step(g, par, left):
            if left > 0:
                self.hidden(eng, g + 1, 1 - par)
                self.turn_gates(eng, g + 1, 1 - par, (0, 1))
            if left > 1:
                self.turn_z(eng, g + 2, par)
            self.output(eng, g, par, (0, 1))
            if left > 0:
                self.turn_gates(eng, g + 1, 1 - par, (2, 3))
            self.output(eng, g, par, (2, 3))
            if left > 0:
                self.turn_gates(eng, g + 1, 1 - par, (4,))

        for_groups(eng, step)

    def copy_zt(self, eng, g, par, first=False):
        if not first:
            eng.wait_ge(self.zt_split.sem, self.zt_split.at(g))
        eng.wait_ge(self.zt_turned.sem, self.zt_turned.at(g + 1))
        src = self.core.bank(5)
        if self.affine is not None:
            ins = eng.activation(self.zt[:, :], src, ACT.Identity, scale=self.affine[:, 0:1],
                                 bias=self.affine[:, 1:2])
        else:
            ins = eng.activation(self.zt[:, :], src, ACT.Copy)
        ins.then_inc(self.zt_copied.sem, 1)

    def activate(self, eng, g, par, first=False):
        eng.wait_ge(self.added.sem, self.added.free(g))
        for c in range(self.C):
            w = self.widths[c]
            eng.wait_ge(self.hid_done.sem, self.hid_done.at(self.C * g + c + 1))
            eng.activation(self.hid[0:w, par, c, :], self.hbank(c)[0:w, :], self.func,
                           bias=self.b1[0:w, c:c + 1]).then_inc(self.act_done.sem, 1)

    def scalar_walk(self, eng):
        self.copy_zt(eng, 0, 0, True)
        self.activate(eng, 0, 0, True)
        self.copy_zt(eng, 1, 1)

        def step(g, par, left):
            if left > 0:
                self.activate(eng, g + 1, 1 - par)
            if left > 1:
                self.copy_zt(eng, g + 2, par)
                self.stage_gates(eng, g + 2, par)

        for_groups(eng, step)

    def stage_gates(self, eng, g, par):
        pass

    def split_zt(self, eng, g, par):
        eng.wait_ge(self.zt_copied.sem, self.zt_copied.at(g + 1))
        hi, lo = (p[:, par, :] for p in self.zt_parts)
        eng.tensor_copy(hi, self.zt[:, :]).then_inc(self.zt_hi_done.sem, 1)
        eng.wait_ge(self.zt_hi_done.sem, self.zt_hi_done.at(g + 1))
        eng.tensor_tensor(lo, self.zt[:, :], hi.bitcast(F32), ALU.subtract).then_inc(self.zt_split.sem, 1)

    def apply_gates(self, eng, g, par, which=range(5)):
        pass

    def add_output(self, eng, g, par):
        c = self.core
        eng.wait_ge(self.out_done.sem, self.out_done.at(g + 1))
        if self.ln.bias_added is not None:
            eng.wait_ge(self.ln.bias_added.sem, self.ln.bias_added.at(g + 1))
        xg = c.x[:, ds(GT * g, GT), :]
        eng.tensor_tensor(xg, self.obank(par).rearrange("p (k d) -> p k d", k=GT), xg, ALU.add)\
           .then_inc(self.added.sem, 1)

    def vector_walk(self, eng):
        self.ln.vector_z(eng, 0)
        self.split_zt(eng, 0, 0)
        self.ln.vector_stats(eng, 1)
        self.ln.vector_z(eng, 1)
        self.apply_gates(eng, 0, 0)
        self.split_zt(eng, 1, 1)
        self.ln.vector_stats(eng, 2)

        def step(g, par, left):
            if left > 1:
                self.ln.vector_z(eng, g + 2)
            if left > 2:
                self.ln.vector_stats(eng, g + 3)
            if left > 0:
                self.apply_gates(eng, g + 1, 1 - par, (0, 1))
            if left > 1:
                self.split_zt(eng, g + 2, par)
            if left > 0:
                self.apply_gates(eng, g + 1, 1 - par, (2, 3, 4))
            self.add_output(eng, g, par)

        for_groups(eng, step, 2)
        eng.wait_ge(self.added.sem, self.added.at(GROUPS))
        eng.sem_inc(self.done.sem, 1)

    def gpsimd(self, eng):
        eng.wait_ge(self.before.sem, self.before.at(1))
        self.ln.pool(eng, 0)
        self.wait_bias(eng)
        self.ln.pool_bias(eng, 0)
        with eng.Fori(1, GROUPS) as g:
            self.ln.pool(eng, g)
            self.ln.pool_bias(eng, g)


class SiluFfn(Hidden):

    F = 512

    def __init__(self, core, before):
        self.core = core
        self.i = {k[len("L0_ffn_"):]: v for k, v in core.ins.items() if k.startswith("L0_ffn_")}
        C = self.F // P
        sb, ctx = core.sb, ExitStack()
        self.affine = sb(ctx, "f0_gb", [P, 2], F32)
        self.b1 = sb(ctx, "f0_b1", [P, C], F32)
        self.bias = sb(ctx, "f0_b2", [P, P], F32)
        self.q1 = sb(ctx, "f0_q1", [P, self.F], mybir.dt.int32)
        self.q2 = sb(ctx, "f0_q2", [P, C, P], mybir.dt.int32)
        self.s1 = sb(ctx, "f0_s1", [P, self.F], F32)
        self.w2 = self.s2 = sb(ctx, "f0_w2", [P, C, P], F32)
        self.w1 = [sb(ctx, f"f0_w1{h}", [P, self.F], F32R) for h in ("hi", "lo")]
        self.once = sb(ctx, "f0_once", [P, GT, P], F32)
        self.setup(before, [P] * C, ACT.Silu, LayerNorm(core, True, self.bias, once=self.once))
        self.buffers(ctx, "f0_")
        ctx.close()
        self.loaded = core.claim("w_loaded", 16 * 8)
        self.prep = core.claim("prep_step", 6)

    def sync(self, eng):
        i = self.i
        eng.wait_ge(self.before.sem, self.before.at(1))
        with self.core.nc.allow_non_contiguous_dma("small columns"):
            for dst, src in (
                    (self.q1[:, :], i["fc1_q"]), (self.s1[:, :], i["fc1_scales"][0].partition_broadcast(P)),
                    (self.q2[:, :, :], i["fc2_q"].rearrange("(c p) d -> p c d", p=P)),
                    (self.s2[:, :, :].rearrange("p c d -> p (c d)"),
                     i["fc2_scales"].rearrange("c d -> (c d)").partition_broadcast(P)),
                    (self.affine[:, 0:1], i["ln_gamma"].unsqueeze(1)),
                    (self.affine[:, 1:2], i["ln_beta"].unsqueeze(1)),
                    (self.b1[:, :], i["fc1_bias"].rearrange("(c p) -> p c", p=P)),
                    (self.bias[:, :], i["fc2_bias"].partition_broadcast(P))):
                eng.dma_start(dst, src).then_inc(self.loaded.sem, 16)

    def wait_bias(self, eng):
        eng.wait_ge(self.prep.sem, self.prep.at(4))

    def vector(self, eng):
        eng.wait_ge(self.before.sem, self.before.at(1))
        self.ln.vector_stats(eng, 0)
        eng.wait_ge(self.loaded.sem, self.loaded.at(16 * 8))
        p = self.prep
        for q, s in ((self.q1, self.s1), (self.q2, self.s2)):
            q, s = q[:], s[:]
            eng.scalar_tensor_tensor(out=s, in0=q, scalar=-128.0, in1=s, op0=ALU.add, op1=ALU.mult)\
               .then_inc(p.sem, 1)
        eng.wait_ge(p.sem, p.at(2))
        eng.tensor_scalar(self.s2[:], self.s2[:], 0.5, None, ALU.mult).then_inc(p.sem, 1)
        eng.tensor_scalar(self.bias[:, :], self.bias[:, :], 0.5, None, ALU.mult).then_inc(p.sem, 1)
        eng.wait_ge(p.sem, p.at(4))
        eng.tensor_copy(self.w1[0][:], self.s1[:]).then_inc(p.sem, 1)
        eng.wait_ge(p.sem, p.at(5))
        eng.tensor_tensor(self.w1[1][:], self.s1[:], self.w1[0][:].bitcast(F32), ALU.subtract)\
           .then_inc(p.sem, 1)
        self.vector_walk(eng)

    def tensor(self, eng):
        eng.wait_ge(self.before.sem, self.before.at(1))
        eng.wait_ge(self.prep.sem, self.prep.at(6))
        self.tensor_walk(eng)

    def scalar(self, eng):
        eng.wait_ge(self.before.sem, self.before.at(1))
        eng.wait_ge(self.loaded.sem, self.loaded.at(16 * 8))
        self.scalar_walk(eng)


class QuantFfn(Phase):

    F = 512

    def __init__(self, core, before):
        self.core, self.before = core, before
        i = core.ins
        self.src = {k: i["L1_ffn_" + k] for k in ("W1", "b1", "W2", "b2")}
        self.C = C = self.F // P
        sb, ctx = core.sb, ExitStack()
        n = lambda s: "f1_" + s
        self.w = sb(ctx, n("w"), [P, 2, C, P], F32)
        self.wq = sb(ctx, n("wq"), [P, 2, C, P], BF16)
        self.wt = sb(ctx, n("wt"), [P, 2, C, P], BF16)
        self.b1 = sb(ctx, n("b1"), [P, C], F32)
        self.bias = sb(ctx, n("b2"), [P, P], F32)
        self.zall = sb(ctx, n("z"), [P, BATCH, P], F32)
        self.zq = sb(ctx, n("zq"), [P, 2, GT, P], BF16)
        self.zqt = sb(ctx, n("zqt"), [P, GROUPS * GT * P], BF16)
        self.zu = sb(ctx, n("zu"), [P, 2, GT * P], F32)
        self.h = sb(ctx, n("h"), [P, 2, C, GT * P], F32)
        self.hq = sb(ctx, n("hq"), [P, 2, C, GT * P], BF16)
        self.rng = sb(ctx, n("rng"), [P, 2, 2, GROUPS], F32)
        self.red = sb(ctx, n("red"), [P, 3, 2], F32)
        self.all = sb(ctx, n("all"), [P, 3, 2], F32)
        self.sc = sb(ctx, n("sc"), [P, 2, 8], F32)
        self.ws = sb(ctx, n("ws"), [P, 2, 2], F32)
        ctx.close()
        cl, G = core.claim, GROUPS
        self.loaded = cl("w_loaded", 16 * 4)
        self.ln = LayerNorm(core, False, self.bias,
                            lambda g, k: self.zall[:, ds(GT * g + k, 1), :].rearrange("p a d -> p (a d)"))
        self.chain = Chain(cl("quant_step", 60))
        self.reduce_ready = cl("reduce_ready", 3)
        self.reduced = cl("reduced", 3)
        self.wq_ready = cl("wq_ready", 1)
        self.wt_turned = cl("turned", 2)
        self.wt_ready = cl("wt_ready", 2)
        self.scale_ready = cl("scale_ready", 2)
        self.zq_step = cl("zq_step", 3 * G)
        self.zq_turned = cl("zt_turned", G)
        self.zqt_ready = cl("zt_copied", G)
        self.hid_done = cl("hid_done", 2 * C * G)
        self.act_done = cl("act_done", 2 * C * G)
        self.ranged = cl("ranged", 2 * G)
        self.hq_step = cl("hq_step", 3 * G)
        self.out_done = cl("out_done", G)
        self.added = cl("added", G, credit=2, owner="vector")
        self.done = cl("phase_done", 1)

    def sync(self, eng):
        s, sem = self.src, self.loaded.sem
        eng.wait_ge(self.before.sem, self.before.at(1))
        with self.core.nc.allow_non_contiguous_dma("small columns"):
            eng.dma_start(self.w[:, 0], s["W1"].rearrange("(c p) d -> p c d", p=P)).then_inc(sem, 16)
            eng.dma_start(self.w[:, 1], s["W2"].rearrange("p (c h) -> p c h", c=self.C)).then_inc(sem, 16)
            eng.dma_start(self.b1[:, :], s["b1"].rearrange("(c p) -> p c", p=P)).then_inc(sem, 16)
            eng.dma_start(self.bias[:, :], s["b2"].partition_broadcast(P)).then_inc(sem, 16)

    def gpsimd(self, eng):
        eng.wait_ge(self.before.sem, self.before.at(1))

        def over_partitions(n):
            eng.wait_ge(self.reduce_ready.sem, self.reduce_ready.at(n + 1))
            eng.partition_all_reduce(self.all[:, n, :], self.red[:, n, :], P,
                                     bass.bass_isa.ReduceOp.max).then_inc(self.reduced.sem, 1)

        over_partitions(0)
        eng.wait_ge(self.loaded.sem, self.loaded.at(16 * 4))
        with eng.Fori(0, GROUPS) as g:
            self.ln.pool(eng, g)
            self.ln.pool_bias(eng, g)
        over_partitions(1)
        over_partitions(2)

    def scales(self, eng, n):
        mx, neg_mn = self.all[:, 1 + n, 0:1], self.all[:, 1 + n, 1:2]
        sc = lambda j: self.sc[:, n, j:j + 1]
        do = lambda ins: self.chain.step(eng, ins)
        do(eng.tensor_tensor(sc(5), mx, neg_mn, ALU.add))
        do(eng.tensor_scalar(sc(0), sc(5), 1.0 / 255.0, 1e-8, ALU.mult, ALU.max))
        do(eng.reciprocal(sc(1), sc(0)))
        do(eng.tensor_tensor(sc(5), neg_mn, sc(1), ALU.mult))
        do(eng.tensor_scalar(sc(5), sc(5), MAGIC, MAGIC, ALU.add, ALU.subtract))
        do(eng.tensor_scalar(sc(5), sc(5), -128.0, -128.0, ALU.add, ALU.max))
        do(eng.tensor_scalar(sc(5), sc(5), 127.0, -1.0, ALU.min, ALU.mult))
        do(eng.tensor_scalar(sc(2), sc(5), -128.0, None, ALU.add))
        do(eng.tensor_scalar(sc(3), sc(5), 127.0, None, ALU.add))
        do(eng.tensor_tensor(sc(4), sc(0), self.ws[:, 0, n:n + 1], ALU.mult))
        eng.sem_inc(self.scale_ready.sem, 1)

    def quantise(self, eng, n, src, tmp, dst, claim, g):
        sc = lambda j: self.sc[:, n, j:j + 1]
        eng.tensor_scalar(tmp, src, sc(1), sc(2), ALU.mult, ALU.max).then_inc(claim.sem, 1)
        eng.wait_ge(claim.sem, claim.at(3 * g + 1))
        eng.tensor_scalar(tmp, tmp, sc(3), MAGIC, ALU.min, ALU.add).then_inc(claim.sem, 1)
        eng.wait_ge(claim.sem, claim.at(3 * g + 2))
        eng.tensor_scalar(dst, tmp, MAGIC, None, ALU.subtract).then_inc(claim.sem, 1)

    def ranges(self, eng, n, g, src):
        eng.tensor_reduce(self.rng[:, n, 0, ds(g, 1)], src, AX.X, ALU.max).then_inc(self.ranged.sem, 1)
        eng.tensor_reduce(self.rng[:, n, 1, ds(g, 1)], src, AX.X, ALU.min, negate=True)\
           .then_inc(self.ranged.sem, 1)

    def total_range(self, eng, n):
        self.chain.step(eng, eng.tensor_reduce(self.red[:, 1 + n, :], self.rng[:, n], AX.X, ALU.max))
        eng.sem_inc(self.reduce_ready.sem, 1)

    def vector(self, eng):
        c, C = self.core, self.C
        do = lambda ins: self.chain.step(eng, ins)
        eng.wait_ge(self.before.sem, self.before.at(1))
        eng.wait_ge(self.loaded.sem, self.loaded.at(16 * 4))
        for w in range(2):
            do(eng.tensor_reduce(self.red[:, 0, w:w + 1], self.w[:, w].rearrange("p c d -> p (c d)"), AX.X,
                                 ALU.max, apply_absolute_value=True))
        eng.sem_inc(self.reduce_ready.sem, 1)
        self.ln.vector_stats(eng, 0)
        eng.wait_ge(self.reduced.sem, self.reduced.at(1))
        do(eng.tensor_scalar(self.ws[:, 0, :], self.all[:, 0, :], 1.0 / 127.0, 1e-8, ALU.mult, ALU.max))
        do(eng.reciprocal(self.ws[:, 1, :], self.ws[:, 0, :]))
        for w in range(2):
            do(eng.tensor_scalar(self.w[:, w], self.w[:, w], self.ws[:, 1, w:w + 1], -127.0, ALU.mult, ALU.max))
        do(eng.tensor_scalar(self.w[:], self.w[:], 127.0, MAGIC, ALU.min, ALU.add))
        eng.tensor_scalar(self.wq[:], self.w[:], MAGIC, None, ALU.subtract).then_inc(self.wq_ready.sem, 1)

        with eng.Fori(0, GROUPS - 1) as g:
            self.ln.vector_z(eng, g)
            self.ln.vector_stats(eng, g + 1)
            eng.wait_ge(self.ln.z_ready.sem, self.ln.z_ready.at(GT * g + GT))
            self.ranges(eng, 0, g, self.zall[:, ds(GT * g, GT), :].rearrange("p k d -> p (k d)"))
        self.ln.vector_z(eng, GROUPS - 1)
        eng.wait_ge(self.ln.z_ready.sem, self.ln.z_ready.at(GT * GROUPS))
        self.ranges(eng, 0, GROUPS - 1, self.zall[:, BATCH - GT:BATCH, :].rearrange("p k d -> p (k d)"))
        eng.wait_ge(self.ranged.sem, self.ranged.at(2 * GROUPS))
        self.total_range(eng, 0)
        eng.wait_ge(self.reduced.sem, self.reduced.at(2))
        self.scales(eng, 0)

        def quantise_z(g, par):
            self.quantise(eng, 0, self.zall[:, ds(GT * g, GT), :].rearrange("p k d -> p (k d)"),
                          self.zu[:, par], self.zq[:, par].rearrange("p k d -> p (k d)"), self.zq_step, g)

        def range_h(g, par):
            eng.wait_ge(self.act_done.sem, self.act_done.at(C * g + C))
            self.ranges_h(eng, g, par)

        quantise_z(0, 0)
        quantise_z(1, 1)

        def step(g, par, left):
            if left > 1:
                eng.wait_ge(self.zqt_ready.sem, self.zqt_ready.at(g + 1))
                quantise_z(g + 2, par)
            range_h(g, par)

        for_groups(eng, step)
        eng.wait_ge(self.ranged.sem, self.ranged.at(4 * GROUPS))
        self.total_range(eng, 1)
        eng.wait_ge(self.reduced.sem, self.reduced.at(3))
        self.scales(eng, 1)

        def quantise_h(g, par):
            eng.wait_ge(self.act_done.sem, self.act_done.at(C * (GROUPS + g) + C))
            h = self.h[:, par].rearrange("p c t -> p (c t)")
            self.quantise(eng, 1, h, h, self.hq[:, par].rearrange("p c t -> p (c t)"), self.hq_step, g)

        quantise_h(0, 0)

        def step(g, par, left):
            if left > 0:
                quantise_h(g + 1, 1 - par)
            eng.wait_ge(self.out_done.sem, self.out_done.at(g + 1))
            xg = c.x[:, ds(GT * g, GT), :].rearrange("p k d -> p (k d)")
            eng.scalar_tensor_tensor(out=xg, in0=c.bank(7 - 3 * par), scalar=self.sc[:, 1, 4:5], in1=xg,
                                     op0=ALU.mult, op1=ALU.add).then_inc(self.added.sem, 1)

        for_groups(eng, step)
        eng.wait_ge(self.added.sem, self.added.at(GROUPS))
        eng.sem_inc(self.done.sem, 1)

    def ranges_h(self, eng, g, par):
        h = self.h[:, par].rearrange("p c t -> p (c t)")
        eng.tensor_reduce(self.rng[:, 1, 0, ds(g, 1)], h, AX.X, ALU.max).then_inc(self.ranged.sem, 1)
        eng.tensor_reduce(self.rng[:, 1, 1, ds(g, 1)], h, AX.X, ALU.min, negate=True)\
           .then_inc(self.ranged.sem, 1)

    def tensor(self, eng):
        c, C = self.core, self.C
        eng.wait_ge(self.before.sem, self.before.at(1))
        eng.wait_ge(self.wq_ready.sem, self.wq_ready.at(1))
        turned = lambda b, k: c.bank(b)[:, 0:GT * P // 2].bitcast(BF16)[:, k * P:(k + 1) * P]
        for w in range(2):
            for k in range(C):
                mm = eng.transpose(turned(5 + w, k), self.wq[:, w, k, :], c.ident_bf[:, :])
            mm.then_inc(self.wt_turned.sem, 1)
        eng.wait_ge(self.wt_ready.sem, self.wt_ready.at(2))

        def turn_z(g, par):
            eng.wait_ge(self.zq_step.sem, self.zq_step.at(3 * g + 3))
            for k in range(GT):
                mm = eng.transpose(turned(5 + par, k), self.zq[:, par, k, :], c.ident_bf[:, :])
            mm.then_inc(self.zq_turned.sem, 1)

        def hidden(g, n, first=False):
            for k in range(C):
                if not first:
                    eng.wait_ge(self.act_done.sem, self.act_done.at(C * (n - 1) + k + 1))
                eng.matmul(c.bank(k), self.wt[:, 0, k, :], self.zqt[:, ds(GT * P * g, GT * P)],
                           start=True, stop=True).then_inc(self.hid_done.sem, 1)

        turn_z(0, 0)
        turn_z(1, 1)
        eng.wait_ge(self.zqt_ready.sem, self.zqt_ready.at(1))
        hidden(0, 0, True)

        def step(g, par, left):
            if left > 1:
                turn_z(g + 2, par)
            if left > 0:
                eng.wait_ge(self.zqt_ready.sem, self.zqt_ready.at(g + 2))
                hidden(g + 1, g + 1)

        for_groups(eng, step)
        hidden(0, GROUPS)

        def step(g, par, left):
            if left > 0:
                hidden(g + 1, GROUPS + g + 1)
            eng.wait_ge(self.hq_step.sem, self.hq_step.at(3 * g + 3))
            eng.wait_ge(self.added.sem, self.added.free(g))
            for k in range(GT):
                for j in range(C):
                    mm = eng.matmul(c.bank(7 - 3 * par)[:, k * P:(k + 1) * P],
                                    self.hq[:, par, j, k * P:(k + 1) * P], self.wt[:, 1, j, :],
                                    start=(j == 0), stop=(j == C - 1))
            mm.then_inc(self.out_done.sem, 1)

        for_groups(eng, step)

    def scalar(self, eng):
        c, C = self.core, self.C
        eng.wait_ge(self.before.sem, self.before.at(1))
        for w in range(2):
            eng.wait_ge(self.wt_turned.sem, self.wt_turned.at(w + 1))
            eng.activation(self.wt[:, w].rearrange("p c d -> p (c d)"),
                           c.bank(5 + w)[:, 0:GT * P // 2].bitcast(BF16), ACT.Copy)\
               .then_inc(self.wt_ready.sem, 1)

        def copy_z(g, par):
            eng.wait_ge(self.zq_turned.sem, self.zq_turned.at(g + 1))
            eng.activation(self.zqt[:, ds(GT * P * g, GT * P)],
                           c.bank(5 + par)[:, 0:GT * P // 2].bitcast(BF16), ACT.Copy)\
               .then_inc(self.zqt_ready.sem, 1)

        def gelu(n, par):
            for k in range(C):
                eng.wait_ge(self.hid_done.sem, self.hid_done.at(C * n + k + 1))
                eng.activation(self.h[:, par, k, :], c.bank(k), ACT.Gelu, scale=self.sc[:, 0, 4:5],
                               bias=self.b1[:, k:k + 1]).then_inc(self.act_done.sem, 1)

        copy_z(0, 0)
        copy_z(1, 1)
        eng.wait_ge(self.scale_ready.sem, self.scale_ready.at(1))
        gelu(0, 0)

        def step(g, par, left):
            if left > 1:
                copy_z(g + 2, par)
            if left > 0:
                eng.wait_ge(self.ranged.sem, self.ranged.at(2 * (GROUPS + g)))
                gelu(g + 1, 1 - par)

        for_groups(eng, step)
        eng.wait_ge(self.ranged.sem, self.ranged.at(4 * GROUPS))
        gelu(GROUPS, 0)
        gelu(GROUPS + 1, 1)

        def step(g, par, left):
            if left > 1:
                eng.wait_ge(self.hq_step.sem, self.hq_step.at(3 * g + 3))
                gelu(GROUPS + g + 2, par)

        for_groups(eng, step)


class TopTwo:

    def __init__(self, core, ctx, name, chain, parts=P, tiles=BATCH):
        sb, self.shape = core.sb, [parts, tiles, 8]
        n = lambda s: f"{name}_{s}"
        self.chain = chain
        self.rank = sb(ctx, n("rank"), [parts, 8], F32)
        self.one = [sb(ctx, n(f"one{j}"), self.shape, F32) for j in range(2)]
        self.tmp = sb(ctx, n("tmp"), self.shape, F32)
        self.rest = sb(ctx, n("rest"), self.shape, F32)
        self.best = sb(ctx, n("best"), [parts, 2, tiles], F32)
        self.first = sb(ctx, n("first"), [parts, 2, tiles], F32)

    def gpsimd(self, eng, ready):
        for e in range(8):
            ins = eng.memset(self.rank[:, e:e + 1], float(8 - e))
        ins.then_inc(ready.sem, 1)

    def vector(self, eng, score):
        do = lambda ins: self.chain.step(eng, ins)
        rank = self.rank[:, :].unsqueeze(1).broadcast_to(self.shape)
        tmp = self.tmp[:, :, :]
        for j in range(2):
            src = score if j == 0 else self.rest[:, :, :]
            do(eng.tensor_reduce(self.best[:, j, :], src, AX.X, ALU.max))
            do(eng.tensor_tensor(tmp, src, bc(self.best[:, j, :], 8), ALU.is_ge))
            do(eng.tensor_tensor(tmp, tmp, rank, ALU.mult))
            do(eng.tensor_reduce(self.first[:, j, :], tmp, AX.X, ALU.max))
            do(eng.tensor_tensor(self.one[j][:, :, :], rank, bc(self.first[:, j, :], 8), ALU.is_equal))
            if j == 0:
                do(eng.tensor_scalar(tmp, self.one[0][:, :, :], -1e30, None, ALU.mult))
                do(eng.tensor_tensor(self.rest[:, :, :], tmp, score, ALU.add))


class GatedFfn(Hidden):

    E = 8
    H = 64
    RING = 3

    def __init__(self, core, before):
        self.core = core
        i = {k[len("L2_ffn_"):]: v for k, v in core.ins.items() if k.startswith("L2_ffn_")}
        self.i = i
        sb, ctx = core.sb, ExitStack()
        n = lambda s: "f2_" + s
        self.C = 5
        self.affine = None
        self.b1 = sb(ctx, n("b1"), [P, 5], F32)
        self.bias = sb(ctx, n("bs2"), [P, P], F32)
        self.b2 = sb(ctx, n("b2"), [self.E, P], F32)
        self.gw = sb(ctx, n("gate_w"), [P, self.E], F32)
        self.rs = sb(ctx, n("route_scale"), [P, 1], F32)
        self.w1f = sb(ctx, n("w1"), [P, 4 * P + self.H], F32)
        self.w2 = sb(ctx, n("w2"), [P, 5, P], F32)
        self.w1 = [sb(ctx, n("w1" + h), [P, 4 * P + self.H], F32R) for h in ("hi", "lo")]
        self.chain = Chain(core.claim("gate_step", 60))
        self.top = TopTwo(core, ctx, n("top"), self.chain)
        self.score = sb(ctx, n("score"), [P, BATCH, self.E], F32)
        self.gates = sb(ctx, n("gates"), [P, BATCH, self.E], F32)
        self.gate_t = sb(ctx, n("gate_t"), [self.E, 2, GT * P], F32)
        self.gate_g = sb(ctx, n("gate_g"), [P, 2, GT, self.E, self.H], F32)
        self.zs = sb(ctx, n("zs"), [P, 2, GT * P], F32)
        self.batch = BatchStats(core, ctx, n("x"))
        self.ln0 = SavedLayerNorm(core, self.batch, None, self.staged_z)
        self.setup(before, [P] * 4 + [self.H], ACT.Gelu, gated=True,
                   ln=SavedLayerNorm(core, self.batch, self.bias))
        self.buffers(ctx, n(""))
        ctx.close()
        cl, G = core.claim, GROUPS
        self.loads = 14
        self.loaded = cl("w_loaded", 16 * self.loads)
        self.rank_ready = cl("rank_ready", 1)
        self.zs_turned = cl("t_done", G)
        self.zs_copied = cl("t_copied", G, credit=2, owner="scalar")
        self.logit_done = cl("logit_done", 1)
        self.exp_ready = cl("exp_ready", 1)
        self.w_ready = cl("wt_ready", 1)
        self.gates_ready = cl("gates_ready", 1)
        self.gate_staged = cl("gate_staged", G)
        self.gate_turned = cl("gate_turned", 5 * G)
        self.gate_taken = cl("gate_taken", 5 * G, credit=2, owner="vector")

    def staged_z(self, g, k):
        return self.hid[:, self.par, 0, k * P:(k + 1) * P]

    def sync(self, eng):
        i, sem = self.i, self.loaded.sem
        eng.wait_ge(self.before.sem, self.before.at(1))
        ld = lambda dst, src: eng.dma_start(dst, src).then_inc(sem, 16)
        with self.core.nc.allow_non_contiguous_dma("small columns"):
            ld(self.w1f[:, 0:4 * P].rearrange("d (e h) -> d e h", h=self.H), i["W1"].rearrange("e d h -> d e h"))
            ld(self.w1f[:, 4 * P:], i["Ws1"])
            for c in range(4):
                ld(self.w2[:, c, :], i["W2"][2 * c:2 * c + 2].rearrange("e h d -> (e h) d"))
            ld(self.w2[0:self.H, 4, :], i["Ws2"])
            for s in range(2):
                ld(self.b1[self.H * s:self.H * (s + 1), 0:4],
                   i["b1"].rearrange("(c s) h -> s h c", s=2)[s])
            ld(self.b1[0:self.H, 4:5], i["bs1"].unsqueeze(1))
            ld(self.bias[:, :], i["bs2"].partition_broadcast(P))
            ld(self.b2[:, :], i["b2"])
            ld(self.gw[:, :], i["gate_W"])
            ld(self.rs[:, :], i["route_scale"].partition_broadcast(P))

    def gpsimd(self, eng):
        eng.wait_ge(self.before.sem, self.before.at(1))
        self.top.gpsimd(eng, self.rank_ready)
        eng.wait_ge(self.loaded.sem, self.loaded.at(16 * self.loads))
        with eng.Fori(0, GROUPS) as g:
            self.ln.pool_bias(eng, g)

    def wait_hidden(self, eng, g):
        super().wait_hidden(eng, g)
        eng.wait_ge(self.gate_taken.sem, self.gate_taken.at(5 * g + 5))

    def gated_bias(self, eng, g, par, k, o):
        return eng.matmul(o, self.gate_t[:, par, k * P:(k + 1) * P], self.b2[:, :], start=False, stop=True)

    def tensor(self, eng):
        c = self.core
        eng.wait_ge(self.before.sem, self.before.at(1))
        eng.wait_ge(self.loaded.sem, self.loaded.at(16 * self.loads))

        def turn(g, par):
            eng.wait_ge(self.ln0.z_ready.sem, self.ln0.z_ready.at(GT * g + GT))
            eng.wait_ge(self.zs_copied.sem, self.zs_copied.free(g))
            for k in range(GT):
                mm = eng.transpose(c.ps_t[:, par, k * P:(k + 1) * P],
                                   self.hid[:, par, 0, k * P:(k + 1) * P], c.ident[:, :])
            mm.then_inc(self.zs_turned.sem, 1)

        turn(0, 0)

        def step(g, par, left):
            if left > 0:
                turn(g + 1, 1 - par)
            eng.wait_ge(self.zs_copied.sem, self.zs_copied.at(g + 1))
            for k in range(GT):
                mm = eng.matmul(c.ps_o[:, ds(self.E * GT * g + self.E * k, self.E)],
                                self.zs[:, par, k * P:(k + 1) * P], self.gw[:, :], start=True, stop=True)
            if left == 0:
                mm.then_inc(self.logit_done.sem, 1)

        for_groups(eng, step)
        eng.wait_ge(self.w_ready.sem, self.w_ready.at(1))
        eng.wait_ge(self.gates_ready.sem, self.gates_ready.at(1))
        self.tensor_walk(eng)

    def turn_gates(self, eng, g, par, which):
        c = self.core
        eng.wait_ge(self.gate_staged.sem, self.gate_staged.at(g + 1))
        for j in which:
            eng.wait_ge(self.gate_taken.sem, self.gate_taken.free(5 * g + j))
            o = c.bank(3 + (5 * par + j) % 2)
            for k in range(GT):
                if j < 4:
                    mm = eng.transpose(o[:, k * P:(k + 1) * P],
                                       self.gate_g[:, par, k, 2 * j:2 * j + 2, :].rearrange("p e h -> p (e h)"),
                                       c.ident[:, :])
                else:
                    mm = eng.transpose(o[0:self.E, k * P:(k + 1) * P], self.gate_g[:, par, k, :, 0],
                                       c.ident[:, :])
            mm.then_inc(self.gate_turned.sem, 1)

    def stage_gates(self, eng, g, par):
        eng.activation(self.gate_g[:, par].rearrange("p k e h -> p (k e) h"),
                       bc(self.gates[:, ds(GT * g, GT), :].rearrange("p k e -> p (k e)"), self.H),
                       ACT.Copy).then_inc(self.gate_staged.sem, 1)

    def scalar(self, eng):
        c = self.core
        eng.wait_ge(self.before.sem, self.before.at(1))
        eng.wait_ge(self.loaded.sem, self.loaded.at(16 * self.loads))
        self.batch.scalar(eng)

        def step(g, par, left):
            eng.wait_ge(self.zs_turned.sem, self.zs_turned.at(g + 1))
            eng.activation(self.zs[:, par], c.ps_t[:, par, :], ACT.Copy).then_inc(self.zs_copied.sem, 1)

        for_groups(eng, step)
        eng.wait_ge(self.logit_done.sem, self.logit_done.at(1))
        eng.activation(self.score[:, :, :].rearrange("p b e -> p (b e)"), c.ps_o[:, :], ACT.Exp, scale=-1.0)\
           .then_inc(self.exp_ready.sem, 1)
        eng.wait_ge(self.gates_ready.sem, self.gates_ready.at(1))
        self.stage_gates(eng, 0, 0)
        self.stage_gates(eng, 1, 1)
        self.scalar_walk(eng)

    def apply_gates(self, eng, g, par, which=range(5)):
        c = self.core
        for j in which:
            eng.wait_ge(self.gate_turned.sem, self.gate_turned.at(5 * g + j + 1))
            o = c.bank(3 + (5 * par + j) % 2)
            if j < 4:
                eng.wait_ge(self.act_done.sem, self.act_done.at(5 * g + j + 1))
                h = self.hid[:, par, j, :]
                ins = eng.tensor_tensor(h, o, h, ALU.mult)
            else:
                ins = eng.tensor_copy(self.gate_t[:, par], o[0:self.E, :])
            ins.then_inc(self.gate_taken.sem, 1)

    def vector(self, eng):
        c = self.core
        do = lambda ins: self.chain.step(eng, ins)
        eng.wait_ge(self.before.sem, self.before.at(1))
        self.batch.vector(eng)

        def form(g, par, left):
            self.par = par
            eng.wait_ge(self.zs_turned.sem, self.zs_turned.at(g - 1))
            self.ln0.vector_z(eng, g)

        for_groups(eng, form)
        eng.wait_ge(self.loaded.sem, self.loaded.at(16 * self.loads))
        hi, lo = self.w1
        do(eng.tensor_copy(hi[:], self.w1f[:]))
        do(eng.tensor_tensor(lo[:], self.w1f[:], hi[:].bitcast(F32), ALU.subtract))
        eng.sem_inc(self.w_ready.sem, 1)
        sc = self.score[:, :, :]
        eng.wait_ge(self.exp_ready.sem, self.exp_ready.at(1))
        do(eng.tensor_scalar(sc, sc, 1.0, None, ALU.add))
        do(eng.reciprocal(sc, sc))
        do(eng.tensor_scalar(sc, sc, self.rs[:, 0:1], None, ALU.mult))
        eng.wait_ge(self.rank_ready.sem, self.rank_ready.at(1))
        self.top.vector(eng, sc)
        best, first = self.top.best, self.top.first
        do(eng.tensor_tensor(first[:, 0, :], best[:, 0, :], best[:, 1, :], ALU.add))
        do(eng.reciprocal(first[:, 0, :], first[:, 0, :]))
        for j in range(2):
            do(eng.tensor_tensor(best[:, j, :], best[:, j, :], first[:, 0, :], ALU.mult))
            one = self.top.one[j][:, :, :]
            do(eng.tensor_tensor(one, one, bc(best[:, j, :], 8), ALU.mult))
        do(eng.tensor_tensor(self.gates[:, :, :], self.top.one[0][:, :, :], self.top.one[1][:, :, :], ALU.add))
        eng.sem_inc(self.gates_ready.sem, 1)
        self.ln.vector_stats(eng, 0)
        self.vector_walk(eng)




class WideAttention(Phase):

    def __init__(self, core, before):
        self.core, self.before = core, before
        i = {k[len("L3_xattn_"):]: v for k, v in core.ins.items() if k.startswith("L3_xattn_")}
        self.i = i
        sb, ctx = core.sb, ExitStack()
        n = lambda s: "a3_" + s
        self.wq = sb(ctx, n("wq"), [P, P], F32)
        self.wk = sb(ctx, n("wk"), [CDIM, P], F32)
        self.wv = sb(ctx, n("wv"), [CDIM, P], F32)
        self.wkp = [sb(ctx, n("wk" + h), [CDIM, P], F32R) for h in ("hi", "lo")]
        self.wvp = [sb(ctx, n("wv" + h), [CDIM, P], F32R) for h in ("hi", "lo")]
        self.bq = sb(ctx, n("bq"), [P, 1], F32)
        self.bk = sb(ctx, n("bk"), [P, 1], F32)
        self.bias = sb(ctx, n("bv"), [P, P], F32)
        self.zt = sb(ctx, n("zt"), [P, 2, GT * P], F32)
        self.qt = sb(ctx, n("qt"), [P, 2, GT * P], F32)
        self.kt = sb(ctx, n("kt"), [P, 2, GCOLS], F32)
        self.vt = sb(ctx, n("vt"), [P, 2, GCOLS], F32)
        self.v = sb(ctx, n("v"), [KEYS, 2, GT, P], F32)
        self.e = sb(ctx, n("e"), [P, 2, GCOLS], F32)
        self.pt = sb(ctx, n("pt"), [KEYS, 2, GT, P], F32)
        self.stat = sb(ctx, n("stat"), [P, 3, GT], F32)
        ctx.close()
        cl, G = core.claim, GROUPS
        self.loaded = cl("w_loaded", 16 * 6)
        self.ln = LayerNorm(core, False, self.bias)
        self.chain = Chain(cl("wide_step", 4))
        self.w_ready = cl("wt_ready", 1)
        self.made = cl("t_done", 5 * G)
        self.copied = cl("t_copied", 5 * G)
        self.scores_ready = cl("scores_ready", G)
        self.max_ready = cl("max_ready", G)
        self.shifted = cl("shifted", G)
        self.exp_ready = cl("exp_ready", G)
        self.norm_step = cl("norm_step", 2 * G)
        self.probs_ready = cl("probs_ready", G)
        self.pt_turned = cl("zt_turned", G)
        self.pt_copied = cl("zt_copied", G)
        self.out_done = cl("out_done", G)
        self.added = cl("added", G, credit=2, owner="vector")
        self.done = cl("phase_done", 1)

    def sync(self, eng):
        i, sem = self.i, self.loaded.sem
        eng.wait_ge(self.before.sem, self.before.at(1))
        with self.core.nc.allow_non_contiguous_dma("small columns"):
            for dst, src in ((self.wq, i["Wq"]), (self.wk, i["Wk"]), (self.wv, i["Wv"]),
                             (self.bq, i["bq"].unsqueeze(1)), (self.bk, i["bk"].unsqueeze(1)),
                             (self.bias, i["bv"].partition_broadcast(P))):
                eng.dma_start(dst[:, :], src).then_inc(sem, 16)

    def gpsimd(self, eng):
        eng.wait_ge(self.before.sem, self.before.at(1))
        eng.wait_ge(self.loaded.sem, self.loaded.at(16 * 6))
        with eng.Fori(0, GROUPS) as g:
            self.ln.pool(eng, g)
            self.ln.pool_bias(eng, g)

    def tensor(self, eng):
        c = self.core
        eng.wait_ge(self.before.sem, self.before.at(1))
        eng.wait_ge(self.w_ready.sem, self.w_ready.at(1))

        def prepare(g, par, first=False):
            cols = ds(GCOLS * g, GCOLS)
            eng.wait_ge(self.ln.z_ready.sem, self.ln.z_ready.at(GT * g + GT))
            if not first:
                eng.wait_ge(self.copied.sem, self.copied.at(5 * g))
            for k in range(GT):
                mm = eng.transpose(c.bank(0)[:, k * P:(k + 1) * P], c.z[:, k, :], c.ident[:, :])
            mm.then_inc(self.made.sem, 1)
            ct = [c.ct_hi[:, cols], c.ct_lo[:, cols]]
            for b, w in ((1, self.wkp), (2, self.wvp)):
                three_passes(eng, c.bank(b)[:, 0:GCOLS], [q[:, :] for q in w], ct).then_inc(self.made.sem, 1)
            eng.wait_ge(self.copied.sem, self.copied.at(5 * g + 1))
            eng.matmul(c.bank(3), self.wq[:, :], self.zt[:, par], start=True, stop=True)\
               .then_inc(self.made.sem, 1)
            eng.wait_ge(self.copied.sem, self.copied.at(5 * g + 3))
            for k in range(GT):
                mm = eng.transpose(c.bank(5)[0:KEYS, k * P:(k + 1) * P],
                                   self.vt[:, par, k * KEYS:(k + 1) * KEYS], c.ident[:, :])
            mm.then_inc(self.made.sem, 1)

        def scores(g, par, first=False):
            eng.wait_ge(self.copied.sem, self.copied.at(5 * g + 4))
            if not first:
                eng.wait_ge(self.shifted.sem, self.shifted.at(g))
            for k in range(GT):
                mm = eng.matmul(c.bank(4)[:, k * KEYS:(k + 1) * KEYS], self.qt[:, par, k * P:(k + 1) * P],
                                self.kt[:, par, k * KEYS:(k + 1) * KEYS], start=True, stop=True)
            mm.then_inc(self.scores_ready.sem, 1)

        prepare(0, 0, True)
        scores(0, 0, True)

        def step(g, par, left):
            if left > 0:
                prepare(g + 1, 1 - par)
            eng.wait_ge(self.probs_ready.sem, self.probs_ready.at(g + 1))
            for k in range(GT):
                mm = eng.transpose(c.bank(6)[0:KEYS, k * P:(k + 1) * P],
                                   self.e[:, par, k * KEYS:(k + 1) * KEYS], c.ident[:, :])
            mm.then_inc(self.pt_turned.sem, 1)
            if left > 0:
                scores(g + 1, 1 - par)
            eng.wait_ge(self.pt_copied.sem, self.pt_copied.at(g + 1))
            eng.wait_ge(self.copied.sem, self.copied.at(5 * g + 5))
            eng.wait_ge(self.added.sem, self.added.at(g))
            for k in range(GT):
                mm = eng.matmul(c.bank(7)[:, k * P:(k + 1) * P], self.pt[:, par, k, :], self.v[:, par, k, :],
                                start=True, stop=True)
            mm.then_inc(self.out_done.sem, 1)

        for_groups(eng, step)

    def scalar(self, eng):
        c = self.core
        eng.wait_ge(self.before.sem, self.before.at(1))
        eng.wait_ge(self.loaded.sem, self.loaded.at(16 * 6))

        def prepare(g, par):
            for n in range(5):
                eng.wait_ge(self.made.sem, self.made.at(5 * g + n + 1))
                dst, src, bias = ((self.zt[:, par], c.bank(0), None),
                                  (self.kt[:, par], c.bank(1)[:, 0:GCOLS], self.bk),
                                  (self.vt[:, par], c.bank(2)[:, 0:GCOLS], None),
                                  (self.qt[:, par], c.bank(3), self.bq),
                                  (self.v[:, par].rearrange("p k d -> p (k d)"), c.bank(5)[0:KEYS, :], None))[n]
                if bias is None:
                    ins = eng.activation(dst, src, ACT.Copy)
                else:
                    ins = eng.activation(dst, src, ACT.Identity, bias=bias[:, 0:1])
                ins.then_inc(self.copied.sem, 1)

        def exponentials(g, par):
            eng.wait_ge(self.shifted.sem, self.shifted.at(g + 1))
            eng.activation(self.e[:, par], self.e[:, par], ACT.Exp).then_inc(self.exp_ready.sem, 1)

        prepare(0, 0)
        exponentials(0, 0)

        def step(g, par, left):
            if left > 0:
                prepare(g + 1, 1 - par)
            eng.wait_ge(self.pt_turned.sem, self.pt_turned.at(g + 1))
            eng.activation(self.pt[:, par].rearrange("p k t -> p (k t)"), c.bank(6)[0:KEYS, :], ACT.Copy)\
               .then_inc(self.pt_copied.sem, 1)
            if left > 0:
                exponentials(g + 1, 1 - par)

        for_groups(eng, step)

    def softmax_front(self, eng, g, par):
        c = self.core
        s = c.bank(4)[:, 0:GCOLS].rearrange("p (k s) -> p k s", k=GT)
        eng.wait_ge(self.scores_ready.sem, self.scores_ready.at(g + 1))
        eng.tensor_reduce(self.stat[:, 0, :], s, AX.X, ALU.max).then_inc(self.max_ready.sem, 1)
        eng.wait_ge(self.max_ready.sem, self.max_ready.at(g + 1))
        eng.tensor_tensor(self.e[:, par].rearrange("p (k s) -> p k s", k=GT), s,
                          bc(self.stat[:, 0, :], KEYS), ALU.subtract).then_inc(self.shifted.sem, 1)

    def softmax_back(self, eng, g, par):
        e, st = self.e[:, par].rearrange("p (k s) -> p k s", k=GT), self.norm_step
        eng.wait_ge(self.exp_ready.sem, self.exp_ready.at(g + 1))
        eng.tensor_reduce(self.stat[:, 1, :], e, AX.X, ALU.add).then_inc(st.sem, 1)
        eng.wait_ge(st.sem, st.at(2 * g + 1))
        eng.reciprocal(self.stat[:, 2, :], self.stat[:, 1, :]).then_inc(st.sem, 1)
        eng.wait_ge(st.sem, st.at(2 * g + 2))
        eng.tensor_tensor(e, e, bc(self.stat[:, 2, :], KEYS), ALU.mult).then_inc(self.probs_ready.sem, 1)

    def vector(self, eng):
        c = self.core
        do = lambda ins: self.chain.step(eng, ins)
        eng.wait_ge(self.before.sem, self.before.at(1))
        self.ln.vector_stats(eng, 0)
        eng.wait_ge(self.loaded.sem, self.loaded.at(16 * 6))
        for f, (hi, lo) in ((self.wk, self.wkp), (self.wv, self.wvp)):
            do(eng.tensor_copy(hi[:, :], f[:, :]))
            do(eng.tensor_tensor(lo[:, :], f[:, :], hi[:, :].bitcast(F32), ALU.subtract))
        eng.sem_inc(self.w_ready.sem, 1)
        self.ln.vector_z(eng, 0)
        self.ln.vector_stats(eng, 1)
        self.softmax_front(eng, 0, 0)
        self.ln.vector_z(eng, 1)
        self.softmax_back(eng, 0, 0)

        def step(g, par, left):
            if left > 1:
                self.ln.vector_stats(eng, g + 2)
            if left > 0:
                self.softmax_front(eng, g + 1, 1 - par)
            if left > 1:
                self.ln.vector_z(eng, g + 2)
            eng.wait_ge(self.out_done.sem, self.out_done.at(g + 1))
            eng.wait_ge(self.ln.bias_added.sem, self.ln.bias_added.at(g + 1))
            xg = c.x[:, ds(GT * g, GT), :].rearrange("p k d -> p (k d)")
            eng.tensor_tensor(xg, c.bank(7), xg, ALU.add).then_inc(self.added.sem, 1)
            if left > 0:
                self.softmax_back(eng, g + 1, 1 - par)

        for_groups(eng, step)
        eng.wait_ge(self.added.sem, self.added.at(GROUPS))
        eng.sem_inc(self.done.sem, 1)


class RoutedFfn(Phase):

    E = 8
    F = 512
    U = 2 * GT
    AHEAD = 3
    HIDDEN_BANKS = (0, 1, 4, 5)

    def __init__(self, core, before):
        self.core, self.before = core, before
        self.i = {k[len("L3_ffn_"):]: v for k, v in core.ins.items() if k.startswith("L3_ffn_")}
        core.ct_scope.close()
        sb, ctx, E, F = core.sb, ExitStack(), self.E, self.F
        n = lambda s: "f3_" + s
        self.C = C = F // P
        self.w1 = [sb(ctx, n("w1" + h), [P, E * F], F32R) for h in ("hi", "lo")]
        self.w2 = sb(ctx, n("w2"), [P, E * C * P], F32)
        self.b1 = sb(ctx, n("b1"), [P, E * F], F32)
        self.b2 = sb(ctx, n("b2"), [E, P], F32)
        self.wr = sb(ctx, n("wr"), [P, E], F32)
        self.br = sb(ctx, n("br"), [P, E], F32)
        self.gamma = sb(ctx, n("gamma"), [P, P], F32)
        self.beta = sb(ctx, n("beta"), [P, P], F32)
        self.ones = sb(ctx, n("ones"), [P, P], F32)
        self.batch = BatchStats(core, ctx, n("x"))
        self.mr = sb(ctx, n("mean_rstd"), [P, BATCH], F32)
        self.zmean = sb(ctx, n("zmean"), [P, BATCH], F32)
        self.weight = sb(ctx, n("weight"), [P, BATCH, 2], F32)
        self.offset = sb(ctx, n("offset"), [P, BATCH, 2], mybir.dt.int32)
        self.by_expert = sb(ctx, n("by_expert"), [E, BATCH], F32)
        self.by_expert_g = sb(ctx, n("by_expert_g"), [E, 2, GT], F32)
        self.st = sb(ctx, n("y_stats"), [P, GT, 6], F32)
        self.mv = sb(ctx, n("y_mean_var"), [P, GT, 2], F32)
        self.yr = sb(ctx, n("y_rstd"), [P, 2, GT], F32)
        self.z = sb(ctx, n("z"), [P, 2, GT, P], F32)
        self.y = sb(ctx, n("y"), [P, 2, GT, P], F32)
        self.chain = Chain(core.claim("route_step", 60))
        with ExitStack() as early:
            self.wf = sb(early, n("wf"), [P, E * F], F32)
            self.top = TopTwo(core, early, n("top"), self.chain, BATCH, 1)
            self.score = sb(early, n("score"), [BATCH, 1, E], F32)
            self.choice = sb(early, n("choice"), [BATCH, 4], F32)
        self.zt = sb(ctx, n("zt"), [P, GT * P], F32)
        self.ztp = [sb(ctx, n("zt" + h), [P, 2, GT * P], F32R) for h in ("hi", "lo")]
        self.h = sb(ctx, n("h"), [P, 4, F], F32)
        self.ht = sb(ctx, n("ht"), [P, 2, F], F32)
        ctx.close()
        cl, G, NU = core.claim, GROUPS, 2 * BATCH
        self.loaded = cl("w_loaded", 16 * 6)
        self.late_loaded = cl("late_loaded", 16)
        self.w2_loaded = cl("w2_loaded", 16)
        self.const_done = cl("rank_ready", 1)
        self.w1_high = cl("act_step", 1)
        self.biased = cl("biased", NU)
        self.mr_ready = cl("mr_ready", 1)
        self.means_done = cl("t_done", 1)
        self.choice_ready = cl("choice_ready", 1)
        self.choice_done = cl("choice_done", 1)
        self.zmean_ready = cl("wt_ready", 1)
        self.logit_done = cl("logit_done", 1)
        self.exp_go = cl("shifted", 2)
        self.exp_ready = cl("exp_ready", 2)
        self.routed = cl("gates_ready", 1)
        self.zb_ready = cl("zb_ready", GT * G)
        self.zt_turned = cl("zt_turned", G)
        self.zt_copied = cl("zt_copied", G)
        self.zt_hi_done = cl("zt_hi_done", G)
        self.zt_split = cl("zt_split", G)
        self.hid_done = cl("hid_done", NU)
        self.act_done = cl("act_done", NU)
        self.h_turned = cl("gate_turned", NU)
        self.h_copied = cl("h_copied", NU)
        self.bg_ready = cl("gate_staged", G)
        self.out_done = cl("out_done", G)
        self.y_ready = cl("added", G, credit=2, owner="vector")
        self.y_stats = cl("y_stats", GT * G)
        self.y_seen = cl("stats_seen", G)
        self.y_aggr = cl("y_aggr", GT * G)
        self.y_rstd = cl("y_rstd", 2 * G)
        self.y_normed = cl("y_norm", GT * G)
        self.pool_seen = cl("pool_seen", G)
        self.stored = cl("stored", 16 * 8)
        self.y_pool = cl("y_pool", 3 * G, credit=2, owner="gpsimd")
        self.done = cl("phase_done", 1)

    def sync(self, eng):
        self.load(eng)
        c = self.core
        for q in range(8):
            eng.wait_ge(self.y_pool.sem, self.y_pool.at(3 * (2 * q + 2)))
            b = slice(8 * q, 8 * q + 8)
            eng.dma_start(c.out[b].rearrange("b t d -> t b d"), c.x[:, b, :]).then_inc(self.stored.sem, 16)
        eng.wait_ge(self.stored.sem, self.stored.at(16 * 8))

    def load(self, eng):
        i, sem = self.i, self.loaded.sem
        eng.wait_ge(self.before.sem, self.before.at(1))
        ld = lambda dst, src: eng.dma_start(dst, src).then_inc(sem, 16)
        ld(self.wf[:, :].rearrange("d (e f) -> d e f", e=self.E), i["W1"].rearrange("e d f -> d e f"))
        ld(self.b2[:, :], i["b2"])
        ld(self.wr[:, :], i["Wr"])
        ld(self.br[:, :], i["br"].partition_broadcast(P))
        ld(self.gamma[:, :], i["gamma"].partition_broadcast(P))
        ld(self.beta[:, :], i["beta"].partition_broadcast(P))
        eng.dma_start(self.b1[:, :], i["b1"].rearrange("e f -> (e f)").partition_broadcast(P))\
           .then_inc(self.late_loaded.sem, 16)
        eng.dma_start(self.w2[:, :].rearrange("p (a d) -> p a d", d=P),
                      i["W2"].rearrange("e (c p) d -> p (e c) d", p=P)).then_inc(self.w2_loaded.sem, 16)

    def gpsimd(self, eng):
        c = self.core
        eng.wait_ge(self.before.sem, self.before.at(1))
        self.top.gpsimd(eng, self.const_done)

        def finish(g, par):
            eng.wait_ge(self.y_aggr.sem, self.y_aggr.at(GT * g + GT))
            eng.tensor_tensor(c.ln_var[:, :], self.mv[:, :, 1], c.eps[:, :], ALU.add)\
               .then_inc(self.y_rstd.sem, 1)
            eng.wait_ge(self.y_rstd.sem, self.y_rstd.at(2 * g + 1))
            eng.tensor_tensor(self.yr[:, par], c.ln_var[:, :], c.neg_half[:, :], ALU.pow)\
               .then_inc(self.y_rstd.sem, 1)
            y = self.y[:, par]
            row = lambda a: a[:, :].unsqueeze(1).broadcast_to([P, GT, P])
            eng.wait_ge(self.y_normed.sem, self.y_normed.at(GT * g + GT))
            eng.tensor_tensor(y, y, row(self.gamma), ALU.mult).then_inc(self.y_pool.sem, 1)
            eng.wait_ge(self.y_pool.sem, self.y_pool.at(3 * g + 1))
            eng.tensor_tensor(y, y, row(self.beta), ALU.add).then_inc(self.y_pool.sem, 1)
            eng.wait_ge(self.y_pool.sem, self.y_pool.at(3 * g + 2))
            eng.sem_inc(self.pool_seen.sem, 1)
            xg = c.x[:, ds(GT * g, GT), :]
            eng.tensor_tensor(xg, xg, y, ALU.add).then_inc(self.y_pool.sem, 1)

        for_groups(eng, lambda g, par, left: finish(g, par))
        eng.wait_ge(self.y_pool.sem, self.y_pool.at(3 * GROUPS))
        eng.sem_inc(self.done.sem, 1)

    def tensor(self, eng):
        c, C, F, U, A = self.core, self.C, self.F, self.U, self.AHEAD
        eng.wait_ge(self.before.sem, self.before.at(1))
        def turn_z(g, par):
            eng.wait_ge(self.zb_ready.sem, self.zb_ready.at(GT * g + GT))
            eng.wait_ge(self.y_ready.sem, self.y_ready.free(g))
            for k in range(GT):
                mm = eng.transpose(c.bank(6 + par)[:, k * P:(k + 1) * P], self.z[:, par, k, :], c.ident[:, :])
            mm.then_inc(self.zt_turned.sem, 1)

        for b in range(BATCH):
            if b % self.batch.TILES == 0:
                self.batch.wait(eng, b // self.batch.TILES)
            eng.matmul(c.bank(5)[:, b:b + 1], c.x[:, b, :], self.batch.rstd[:, b:b + 1], start=True, stop=True)
        eng.wait_ge(self.mr_ready.sem, self.mr_ready.at(1))
        eng.matmul(c.bank(3)[:, 0:BATCH], self.ones[:, :], self.mr[:, :], start=True, stop=True)\
           .then_inc(self.means_done.sem, 1)
        turn_z(0, 0)
        eng.wait_ge(self.zmean_ready.sem, self.zmean_ready.at(1))
        eng.matmul(c.bank(4)[0:BATCH, 0:self.E], self.zmean[:, :], self.wr[:, :], start=True, stop=True)\
           .then_inc(self.logit_done.sem, 1)
        eng.wait_ge(self.choice_ready.sem, self.choice_ready.at(1))
        one = c.ident[0:BATCH, 0:BATCH]
        for n in range(4):
            eng.matmul(c.bank(3)[:, n * BATCH:(n + 1) * BATCH],
                       self.choice[:, n:n + 1].broadcast_to([BATCH, P]), one, start=True, stop=True)
        eng.transpose(c.bank(4)[0:self.E, 0:BATCH], self.top.tmp[:, 0, :], one)\
           .then_inc(self.choice_done.sem, 1)

        def hidden(u, j, par):
            off = eng.value_load(self.offset[0:1].rearrange("p b s -> p (b s)")[:, ds(u, 1)],
                                 min_val=0, max_val=F * (self.E - 1))
            k = j // 2
            o = c.bank(self.HIDDEN_BANKS[j % 4])
            three_passes(eng, o, [q[:, par, k * P:(k + 1) * P] for q in self.ztp],
                         [q[:, ds(off, F)] for q in self.w1]).then_inc(self.hid_done.sem, 1)

        def turn(u, j):
            eng.wait_ge(self.act_done.sem, self.act_done.at(u + 1))
            for k in range(C):
                mm = eng.transpose(c.bank(2 + j % 2)[:, k * P:(k + 1) * P],
                                   self.h[:, j % 4, k * P:(k + 1) * P], c.ident[:, :])
            mm.then_inc(self.h_turned.sem, 1)

        def output(u, j, g, par):
            k, s = j // 2, j % 2
            off = eng.value_load(self.offset[0:1].rearrange("p b s -> p (b s)")[:, ds(u, 1)],
                                 min_val=0, max_val=F * (self.E - 1))
            o = c.bank(6 + par)[:, k * P:(k + 1) * P]
            if j == 0:
                eng.wait_ge(self.bg_ready.sem, self.bg_ready.at(g + 1))
            if s == 0:
                eng.matmul(o, self.by_expert_g[:, par, k:k + 1].broadcast_to([self.E, P]), self.b2[:, :],
                           start=True, stop=False)
            eng.wait_ge(self.h_copied.sem, self.h_copied.at(u + 1))
            for q in range(C):
                mm = eng.matmul(o, self.ht[:, s, q * P:(q + 1) * P], self.w2[:, ds(off + q * P, P)],
                                start=False, stop=(s == 1 and q == C - 1))
            if j == U - 1:
                mm.then_inc(self.out_done.sem, 1)

        eng.wait_ge(self.routed.sem, self.routed.at(1))
        eng.wait_ge(self.w2_loaded.sem, self.w2_loaded.at(16))
        eng.wait_ge(self.zt_split.sem, self.zt_split.at(1))
        for u in range(self.AHEAD):
            hidden(u, u, 0)
        turn(0, 0)

        def step(g, par, left):
            for j in range(U):
                u = U * g + j
                if j < U - A:
                    hidden(u + A, j + A, par)
                elif left > 0:
                    if j == U - A:
                        eng.wait_ge(self.zt_split.sem, self.zt_split.at(g + 2))
                    hidden(u + A, j + A - U, 1 - par)
                if j < U - 1 or left > 0:
                    turn(u + 1, (j + 1) % U)
                output(u, j, g, par)
                if j == 2 and left > 0:
                    turn_z(g + 1, 1 - par)

        for_groups(eng, step)

    def scalar(self, eng):
        c, U, A = self.core, self.U, self.AHEAD
        eng.wait_ge(self.before.sem, self.before.at(1))
        self.batch.scalar(eng)
        eng.wait_ge(self.loaded.sem, self.loaded.at(16 * 6))
        eng.activation(self.w1[0][:, :], self.wf[:, :], ACT.Copy).then_inc(self.w1_high.sem, 1)
        def copy_zt(g, par):
            eng.wait_ge(self.zt_turned.sem, self.zt_turned.at(g + 1))
            eng.activation(self.zt[:, :], c.bank(6 + par), ACT.Copy).then_inc(self.zt_copied.sem, 1)

        copy_zt(0, 0)
        sc = self.score[:, 0, :]
        eng.wait_ge(self.exp_go.sem, self.exp_go.at(1))
        eng.activation(sc, sc, ACT.Exp).then_inc(self.exp_ready.sem, 1)
        eng.wait_ge(self.exp_go.sem, self.exp_go.at(2))
        w = self.choice[:, 1:2]
        eng.activation(w, w, ACT.Exp).then_inc(self.exp_ready.sem, 1)

        def gelu(u, j):
            eng.wait_ge(self.biased.sem, self.biased.at(u + 1))
            h = self.h[:, j % 4, :]
            eng.activation(h, h, ACT.Gelu).then_inc(self.act_done.sem, 1)

        def scaled(u, j):
            w = self.weight[:, :, :].rearrange("p b s -> p (b s)")[:, ds(u, 1)]
            eng.wait_ge(self.h_turned.sem, self.h_turned.at(u + 1))
            eng.activation(self.ht[:, j % 2, :], c.bank(2 + j % 2), ACT.Copy, scale=w)\
               .then_inc(self.h_copied.sem, 1)

        eng.wait_ge(self.routed.sem, self.routed.at(1))
        for u in range(A):
            gelu(u, u)
        scaled(0, 0)

        def step(g, par, left):
            for j in range(U):
                u = U * g + j
                if j < U - 1 or left > 0:
                    scaled(u + 1, j + 1)
                if j < U - A or left > 0:
                    gelu(u + A, j + A)
                if j == 2 and left > 0:
                    copy_zt(g + 1, 1 - par)

        for_groups(eng, step)

    def vector(self, eng):
        c, U, E, F, A = self.core, self.U, self.E, self.F, self.AHEAD
        do = lambda ins: self.chain.step(eng, ins)
        eng.wait_ge(self.before.sem, self.before.at(1))
        do(eng.memset(self.ones[:, :], 1.0))
        self.batch.vector(eng)
        eng.tensor_tensor(self.mr[:, :], self.batch.mv[:, :, 0], self.batch.rstd[:, :], ALU.mult)\
           .then_inc(self.mr_ready.sem, 1)
        eng.wait_ge(self.w1_high.sem, self.w1_high.at(1))
        do(eng.tensor_tensor(self.w1[1][:, :], self.wf[:, :], self.w1[0][:, :].bitcast(F32), ALU.subtract))
        def make_z(g, par, tiles=range(GT)):
            for k in tiles:
                col = ds(GT * g + k, 1)
                eng.tensor_scalar(self.z[:, par, k, :], c.x[:, col, :].rearrange("p a d -> p (a d)"),
                                  self.batch.mean_of(GT * g + k), self.batch.rstd_of(GT * g + k), ALU.subtract, ALU.mult)\
                   .then_inc(self.zb_ready.sem, 1)

        def stage_experts(g, par):
            eng.tensor_copy(self.by_expert_g[:, par], self.by_expert[:, ds(GT * g, GT)])\
               .then_inc(self.bg_ready.sem, 1)

        def split_high(g, par):
            eng.wait_ge(self.zt_copied.sem, self.zt_copied.at(g + 1))
            eng.tensor_copy(self.ztp[0][:, par], self.zt[:, :]).then_inc(self.zt_hi_done.sem, 1)

        def split_low(g, par):
            eng.wait_ge(self.zt_hi_done.sem, self.zt_hi_done.at(g + 1))
            eng.tensor_tensor(self.ztp[1][:, par], self.zt[:, :], self.ztp[0][:, par].bitcast(F32),
                              ALU.subtract).then_inc(self.zt_split.sem, 1)

        make_z(0, 0)
        split_high(0, 0)
        split_low(0, 0)
        eng.wait_ge(self.means_done.sem, self.means_done.at(1))
        do(eng.tensor_scalar(self.zmean[:, :], c.bank(5)[:, 0:BATCH], 1.0 / P, None, ALU.mult))
        eng.scalar_tensor_tensor(out=self.zmean[:, :], in0=c.bank(3)[:, 0:BATCH], scalar=-1.0 / P,
                                 in1=self.zmean[:, :], op0=ALU.mult, op1=ALU.add)\
           .then_inc(self.zmean_ready.sem, 1)

        sc, tmp = self.score[:, 0, :], self.top.tmp[:, 0, :]
        red = self.top.first[:, 0, 0:1]
        eng.wait_ge(self.logit_done.sem, self.logit_done.at(1))
        do(eng.tensor_tensor(sc, c.bank(4)[0:BATCH, 0:E], self.br[0:BATCH, :], ALU.add))
        do(eng.tensor_reduce(red, sc, AX.X, ALU.max))
        do(eng.tensor_scalar(sc, sc, red, None, ALU.subtract))
        eng.sem_inc(self.exp_go.sem, 1)
        eng.wait_ge(self.exp_ready.sem, self.exp_ready.at(1))
        do(eng.tensor_reduce(red, sc, AX.X, ALU.add))
        do(eng.reciprocal(red, red))
        do(eng.tensor_scalar(sc, sc, red, None, ALU.mult))
        eng.wait_ge(self.const_done.sem, self.const_done.at(1))
        self.top.vector(eng, self.score[:, :, :])
        best, first = self.top.best[:, :, 0], self.top.first[:, :, 0]
        one = [o[:, 0, :] for o in self.top.one]
        w0, w1 = self.choice[:, 0:1], self.choice[:, 1:2]
        do(eng.tensor_tensor(w1, best[:, 1:2], best[:, 0:1], ALU.subtract))
        eng.sem_inc(self.exp_go.sem, 1)
        do(eng.tensor_scalar(self.choice[:, 2:4], first, -float(F), float(E * F), ALU.mult, ALU.add))
        eng.wait_ge(self.exp_ready.sem, self.exp_ready.at(2))
        do(eng.tensor_scalar(w0, w1, 1.0, None, ALU.add))
        do(eng.reciprocal(w0, w0))
        do(eng.tensor_tensor(w1, w1, w0, ALU.mult))
        for o, w in zip(one, (w0, w1)):
            do(eng.tensor_scalar(o, o, w, None, ALU.mult))
        do(eng.tensor_tensor(tmp, one[0], one[1], ALU.add))
        eng.sem_inc(self.choice_ready.sem, 1)
        eng.wait_ge(self.choice_done.sem, self.choice_done.at(1))
        for n in range(2):
            do(eng.tensor_copy(self.weight[:, :, n], c.bank(3)[:, n * BATCH:(n + 1) * BATCH]))
            do(eng.tensor_copy(self.offset[:, :, n], c.bank(3)[:, (n + 2) * BATCH:(n + 3) * BATCH]))
        do(eng.tensor_copy(self.by_expert[:, :], c.bank(4)[0:E, 0:BATCH]))
        eng.sem_inc(self.routed.sem, 1)

        def add_b1(u, j):
            off = eng.value_load(self.offset[0:1].rearrange("p b s -> p (b s)")[:, ds(u, 1)],
                                 min_val=0, max_val=F * (self.E - 1))
            eng.wait_ge(self.hid_done.sem, self.hid_done.at(u + 1))
            eng.tensor_tensor(self.h[:, j % 4, :], c.bank(self.HIDDEN_BANKS[j % 4]), self.b1[:, ds(off, F)], ALU.add)\
               .then_inc(self.biased.sem, 1)

        def y_sum(g, par, first=False):
            flat = lambda a: a[:, par].rearrange("p k d -> p (k d)")
            eng.wait_ge(self.out_done.sem, self.out_done.at(g + 1))
            if not first:
                eng.wait_ge(self.y_pool.sem, self.y_pool.at(3 * (g - 1)))
            eng.tensor_tensor(flat(self.y), c.bank(6 + par), flat(self.z), ALU.add)\
               .then_inc(self.y_ready.sem, 1)

        def y_statistics(g, par):
            eng.wait_ge(self.y_ready.sem, self.y_ready.at(g + 1))
            for k in range(GT):
                eng.bn_stats(self.st[:, k, :], self.y[:, par, k, :]).then_inc(self.y_stats.sem, 1)

        def y_aggregate(g):
            eng.wait_ge(self.y_stats.sem, self.y_stats.at(GT * g + GT))
            eng.sem_inc(self.y_seen.sem, 1)
            for k in range(GT):
                eng.bn_aggr(self.mv[:, k, :], self.st[:, k, :]).then_inc(self.y_aggr.sem, 1)

        def y_norm(g, par, tiles):
            eng.wait_ge(self.y_rstd.sem, self.y_rstd.at(2 * g + 2))
            for k in tiles:
                y = self.y[:, par, k, :]
                eng.tensor_scalar(y, y, self.mv[:, k, 0:1], self.yr[:, par, k:k + 1], ALU.subtract, ALU.mult)\
                   .then_inc(self.y_normed.sem, 1)

        stage_experts(0, 0)
        eng.wait_ge(self.late_loaded.sem, self.late_loaded.at(16))
        for u in range(A):
            add_b1(u, u)

        def step(g, par, left, first=False, second=False):
            old = 1 - par
            for j in range(U):
                u = U * g + j
                if j == 4 and left > 0:
                    split_low(g + 1, old)
                if j < U - A or left > 0:
                    add_b1(u + A, j + A)
                if j == 0 and not first:
                    y_sum(g - 1, old, second)
                    eng.wait_ge(self.y_ready.sem, self.y_ready.at(g))
                if j == 0 and left > 0:
                    stage_experts(g + 1, old)
                if j in (0, 1) and left > 0:
                    make_z(g + 1, old, range(2 * j, 2 * j + 2))
                if j == 2 and not first:
                    y_statistics(g - 1, old)
                if j == 3 and left > 0:
                    split_high(g + 1, old)
                if j == 4 and not first:
                    y_aggregate(g - 1)
                if j in (6, 7) and not first:
                    y_norm(g - 1, old, range(2 * j - 12, 2 * j - 10))

        step(0, 0, 2, True)
        step(1, 1, 2, second=True)
        with eng.Fori(1, GROUPS // 2 - 1) as i:
            step(2 * i, 0, 2)
            step(2 * i + 1, 1, 2)
        step(GROUPS - 2, 0, 1)
        step(GROUPS - 1, 1, 0)
        y_sum(GROUPS - 1, 1)
        y_statistics(GROUPS - 1, 1)
        y_aggregate(GROUPS - 1)
        y_norm(GROUPS - 1, 1, range(GT))


def cross_attention_ffn_kernel(nc, ins, out):
    with ExitStack() as ctx:
        core = Core(nc, ctx, ins, out)
        phases = build_phases(core)
        block = ctx.enter_context(nc.Block())

        @block.sync
        def _(sp):
            for ph in phases:
                ph.sync(sp)

        @block.gpsimd
        def _(pool):
            core.grant("gpsimd", pool)
            for ph in phases:
                ph.gpsimd(pool)

        @block.scalar
        def _(act):
            core.grant("scalar", act)
            for ph in phases:
                ph.scalar(act)

        @block.vector
        def _(dve):
            core.grant("vector", dve)
            for ph in phases:
                ph.vector(dve)

        @block.tensor
        def _(pe):
            for ph in phases:
                ph.tensor(pe)


def build_phases(core):
    i = core.ins
    setup = Setup(core)
    phases, last = [setup], setup.done

    def add(make, *args, **kw):
        nonlocal last
        phases.append(make(core, *args, before=last, **kw))
        last = phases[-1].done

    wkv = i["L0_xattn_Wkv"]
    add(CrossAttention, "a0", 16, i["L0_xattn_Wq"], wkv[:, 0:1024], wkv[:, 1024:2048],
        i["L0_xattn_Wo"], i["L0_xattn_bo"], twice=True,
        gamma=i["L0_xattn_ln_gamma"], beta=i["L0_xattn_ln_beta"],
        mask=i["mask_1x1xSxS2_bk0"].rearrange("a b q k -> (a b q) k"), setup=setup)
    add(SiluFfn)
    for name, heads in (("L1", 8), ("L2", 16)):
        add(CrossAttention, "a" + name[1], heads, *(i[f"{name}_xattn_{w}"] for w in ("Wq", "Wk", "Wv", "Wo", "bo")))
        add(QuantFfn if name == "L1" else GatedFfn)
    add(WideAttention)
    add(RoutedFfn)
    return phases


_INS = ['x', 'ctx_768', 'mask_1x1xSxS2_bk0', 'L0_xattn_ln_gamma', 'L0_xattn_ln_beta', 'L0_xattn_Wq',
        'L0_xattn_Wkv', 'L0_xattn_Wo', 'L0_xattn_bo', 'L0_ffn_ln_gamma', 'L0_ffn_ln_beta',
        'L0_ffn_fc1_q', 'L0_ffn_fc1_scales', 'L0_ffn_fc1_bias', 'L0_ffn_fc2_q', 'L0_ffn_fc2_scales',
        'L0_ffn_fc2_bias', 'L1_xattn_Wq', 'L1_xattn_Wk', 'L1_xattn_Wv', 'L1_xattn_Wo', 'L1_xattn_bo',
        'L1_ffn_W1', 'L1_ffn_b1', 'L1_ffn_W2', 'L1_ffn_b2', 'L2_xattn_Wq', 'L2_xattn_Wk',
        'L2_xattn_Wv', 'L2_xattn_Wo', 'L2_xattn_bo', 'L2_ffn_gate_W', 'L2_ffn_W1', 'L2_ffn_b1',
        'L2_ffn_W2', 'L2_ffn_b2', 'L2_ffn_Ws1', 'L2_ffn_bs1', 'L2_ffn_Ws2', 'L2_ffn_bs2',
        'L2_ffn_route_scale', 'L3_xattn_Wq', 'L3_xattn_bq', 'L3_xattn_Wk', 'L3_xattn_bk',
        'L3_xattn_Wv', 'L3_xattn_bv', 'L3_ffn_W1', 'L3_ffn_b1', 'L3_ffn_W2', 'L3_ffn_b2',
        'L3_ffn_Wr', 'L3_ffn_br', 'L3_ffn_gamma', 'L3_ffn_beta']


def _arrays(inputs):
    arrays = {}
    for name in _INS:
        a = np.ascontiguousarray(inputs[name])
        arrays[f"in_{name}_dram"] = a.reshape(a.shape or (1,))
    return arrays


def _build(nc, arrays):
    aps = {}
    for name in _INS:
        a = arrays[f"in_{name}_dram"]
        aps[name] = nc.dram_tensor(f"in_{name}_dram", a.shape, mybir.dt.from_np(a.dtype),
                                   kind="ExternalInput").ap()
    out = nc.dram_tensor("out_0_dram", (BATCH, P, P), F32, kind="ExternalOutput").ap()
    cross_attention_ffn_kernel(nc, aps, out)


def kernel(**inputs):
    import concourse.bacc as _bacc
    from concourse.bass_utils import run_bass_kernel_spmd as _run

    nc = _bacc.Bacc("TRN2", target_bir_lowering=False, num_devices=1)
    arrays = _arrays(inputs)
    _build(nc, arrays)
    r = _run(nc, [arrays], core_ids=[0])
    return r.results[0]["out_0_dram"]
```
